# Optimizing a Trainium2 kernel written in Bass

```python
import numpy as np
import jax
import jax.numpy as jnp

def _softmax(x, axis=-1):
    return jax.nn.softmax(x, axis=axis)

def _gelu(x):
    return jax.nn.gelu(x, approximate=True)

def _silu(x):
    return jax.nn.silu(x)

def _sigmoid(x):
    return jax.nn.sigmoid(x)

def _layernorm(x, axis=-1, eps=1e-05):
    m = jnp.mean(x, axis=axis, keepdims=True)
    v = jnp.var(x, axis=axis, keepdims=True)
    return (x - m) / jnp.sqrt(v + eps)

def _scatter_add(tgt, idx, src, axis=0):
    return tgt.at[idx].add(src)

def _segment_sum(src, seg, n):
    return jax.ops.segment_sum(src, seg, n)
kernel_name = 'mk_vit_tower_d1_tok_img768_r4_f1c994'

def setup_inputs(seed: int=0):
    np.random.seed(seed)
    _w = jnp.asarray

    def _rec_inputs():
        import jax
        import jax.numpy as jnp
        _rk = jax.random.key(seed)
        x = -0.00016672 + 0.999947 * jax.random.normal(jax.random.fold_in(_rk, 1), (64, 3, 96, 96), jnp.float32)
        return x
    x = _rec_inputs()

    def _L0_tok_setup():
        import jax, jax.numpy as jnp
        import numpy as np
        IMG = 96
        PATCH = 16
        C = 3
        PROJ = 192
        NUM_PATCHES = (IMG // PATCH) ** 2
        FLAT = C * PATCH * PATCH
        BATCH = 64

        def _patchify(x):
            B, c, H, Wd = x.shape
            hp, wp = (H // PATCH, Wd // PATCH)
            x = x.reshape(B, c, hp, PATCH, wp, PATCH)
            x = x.transpose(0, 2, 4, 1, 3, 5)
            return x.reshape(B, hp * wp, c * PATCH * PATCH)
        key = jax.random.key(seed)
        k1, k2, k3, k4 = jax.random.split(key, 4)
        x = jax.random.normal(k1, (BATCH, C, IMG, IMG), dtype=jnp.float32)
        bound = 1.0 / np.sqrt(FLAT)
        W = jax.random.uniform(k2, (PROJ, FLAT), minval=-bound, maxval=bound, dtype=jnp.float32)
        b = jax.random.uniform(k3, (PROJ,), minval=-bound, maxval=bound, dtype=jnp.float32)
        pos_emb = jax.random.normal(k4, (NUM_PATCHES, PROJ), dtype=jnp.float32)
        return {'x': x, 'W': W, 'b': b, 'pos_emb': pos_emb}
    _L0_tok_all = _L0_tok_setup()
    _L0_tok_in = {k: v for k, v in _L0_tok_all.items() if k in ('W', 'b', 'pos_emb')}
    del _L0_tok_all

    def _L0_attn_setup():
        import jax, jax.numpy as jnp
        import numpy as np
        from jax import lax
        B_SZ, L, D, N, R = (1, 1024, 192, 16, 48)

        def _soft_clamp(x, lo=0.0001, hi=10.0):
            center = (hi + lo) / 2.0
            half_range = (hi - lo) / 2.0
            return center + half_range * jnp.tanh((x - center) / half_range)
        key = jax.random.key(seed)
        ks = jax.random.split(key, 6)
        x = jax.random.normal(ks[0], (B_SZ, L, D), jnp.float32)
        A_log = jnp.log(jnp.broadcast_to(jnp.arange(1, N + 1, dtype=jnp.float32), (D, N)))
        D_param = jnp.ones((D,), jnp.float32)
        W_bc = jax.random.normal(ks[1], (D, 2 * N), jnp.float32) / np.sqrt(D).astype(np.float32)
        W_dt = jax.random.normal(ks[2], (D, R), jnp.float32) / np.sqrt(D).astype(np.float32)
        W_dtp = jax.random.normal(ks[3], (R, D), jnp.float32) / np.sqrt(R).astype(np.float32)
        dt = jax.random.uniform(ks[4], (D,), jnp.float32, 0.001, 0.1)
        dt = jnp.clip(dt, 0.0001)
        b_dt = dt + jnp.log(-jnp.expm1(-dt))
        rms_scale = jnp.ones((D,), jnp.float32)
        return {'x': x, 'A_log': A_log, 'D_param': D_param, 'W_bc': W_bc, 'W_dt': W_dt, 'W_dtp': W_dtp, 'b_dt': b_dt, 'rms_scale': rms_scale}
    _L0_attn_all = _L0_attn_setup()
    _L0_attn_in = {k: v for k, v in _L0_attn_all.items() if k in ('A_log', 'D_param', 'W_bc', 'W_dt', 'W_dtp', 'b_dt', 'rms_scale')}
    del _L0_attn_all

    def _L0_ffn_setup():
        import jax, jax.numpy as jnp
        import numpy as np
        G, E = (4, 8)
        KG, KE = (2, 2)
        D, M = (192, 768)
        SCALE = 0.02

        def _combine_weights(xf, Wg, bg, Wge, bge):
            N = xf.shape[0]
            glog = xf @ Wg + bg
            gtop, gidx = jax.lax.top_k(glog, KG)
            ggate = jax.nn.softmax(gtop, axis=-1)
            elog_all = jnp.einsum('nd,gde->nge', xf, Wge) + bge
            elog = jnp.take_along_axis(elog_all, gidx[:, :, None], axis=1)
            etop, eidx = jax.lax.top_k(elog, KE)
            egate = jax.nn.softmax(etop, axis=-1)
            w = ggate[:, :, None] * egate
            flat = gidx[:, :, None] * E + eidx
            comb = jnp.zeros((N, G * E), xf.dtype).at[jnp.arange(N)[:, None, None], flat].add(w)
            return comb
        key = jax.random.key(seed)
        ks = jax.random.split(key, 8)
        x = jax.random.normal(ks[0], (1, 128, D), jnp.float32)
        Wg = jax.random.normal(ks[1], (D, G), jnp.float32) * SCALE
        bg = jnp.zeros((G,), jnp.float32)
        Wge = jax.random.normal(ks[2], (G, D, E), jnp.float32) * SCALE
        bge = jnp.zeros((G, E), jnp.float32)
        W1 = jax.random.normal(ks[3], (G * E, D, M), jnp.float32) * SCALE
        b1 = jnp.zeros((G * E, M), jnp.float32)
        W2 = jax.random.normal(ks[4], (G * E, M, D), jnp.float32) * SCALE
        b2 = jnp.zeros((G * E, D), jnp.float32)
        return {'x': x, 'Wg': Wg, 'bg': bg, 'Wge': Wge, 'bge': bge, 'W1': W1, 'b1': b1, 'W2': W2, 'b2': b2}
    _L0_ffn_all = _L0_ffn_setup()
    _L0_ffn_in = {k: v for k, v in _L0_ffn_all.items() if k in ('Wg', 'bg', 'Wge', 'bge', 'W1', 'b1', 'W2', 'b2')}
    del _L0_ffn_all
    return {'x': x, 'L0_tok_W': _L0_tok_in['W'], 'L0_tok_b': _L0_tok_in['b'], 'L0_tok_pos_emb': _L0_tok_in['pos_emb'], 'L0_attn_A_log': _L0_attn_in['A_log'], 'L0_attn_D_param': _L0_attn_in['D_param'], 'L0_attn_W_bc': _L0_attn_in['W_bc'], 'L0_attn_W_dt': _L0_attn_in['W_dt'], 'L0_attn_W_dtp': _L0_attn_in['W_dtp'], 'L0_attn_b_dt': _L0_attn_in['b_dt'], 'L0_attn_rms_scale': _L0_attn_in['rms_scale'], 'L0_ffn_Wg': _L0_ffn_in['Wg'], 'L0_ffn_bg': _L0_ffn_in['bg'], 'L0_ffn_Wge': _L0_ffn_in['Wge'], 'L0_ffn_bge': _L0_ffn_in['bge'], 'L0_ffn_W1': _L0_ffn_in['W1'], 'L0_ffn_b1': _L0_ffn_in['b1'], 'L0_ffn_W2': _L0_ffn_in['W2'], 'L0_ffn_b2': _L0_ffn_in['b2']}

def reference(x, L0_tok_W, L0_tok_b, L0_tok_pos_emb, L0_attn_A_log, L0_attn_D_param, L0_attn_W_bc, L0_attn_W_dt, L0_attn_W_dtp, L0_attn_b_dt, L0_attn_rms_scale, L0_ffn_Wg, L0_ffn_bg, L0_ffn_Wge, L0_ffn_bge, L0_ffn_W1, L0_ffn_b1, L0_ffn_W2, L0_ffn_b2):
    import jax
    import jax.numpy as jnp

    def _L0_tok_ref(x, W, b, pos_emb):
        import jax, jax.numpy as jnp
        import numpy as np
        IMG = 96
        PATCH = 16
        C = 3
        PROJ = 192
        NUM_PATCHES = (IMG // PATCH) ** 2
        FLAT = C * PATCH * PATCH
        BATCH = 64

        def _patchify(x):
            B, c, H, Wd = x.shape
            hp, wp = (H // PATCH, Wd // PATCH)
            x = x.reshape(B, c, hp, PATCH, wp, PATCH)
            x = x.transpose(0, 2, 4, 1, 3, 5)
            return x.reshape(B, hp * wp, c * PATCH * PATCH)
        flat = _patchify(x)
        encoded = jnp.einsum('bnf,df->bnd', flat, W) + b + pos_emb[None, :, :]
        return encoded

    def _L0_attn_ref(x, A_log, D_param, W_bc, W_dt, W_dtp, b_dt, rms_scale):
        import jax, jax.numpy as jnp
        import numpy as np
        from jax import lax
        B_SZ, L, D, N, R = (1, 1024, 192, 16, 48)

        def _soft_clamp(x, lo=0.0001, hi=10.0):
            center = (hi + lo) / 2.0
            half_range = (hi - lo) / 2.0
            return center + half_range * jnp.tanh((x - center) / half_range)
        n = A_log.shape[1]
        A = -jnp.exp(A_log)
        bc = x @ W_bc
        B_sel, C_sel = (bc[..., :n], bc[..., n:])
        delta = jax.nn.softplus(x @ W_dt @ W_dtp + b_dt)
        delta = delta * lax.rsqrt(jnp.mean(delta * delta, axis=-1, keepdims=True) + 1e-06) * rms_scale
        delta = _soft_clamp(delta, 0.0001, 10.0)
        dE = delta[..., None]
        half = 0.5 * dE * A
        denom = 1.0 - half
        A_bar = (1.0 + half) / denom
        B_bar = jnp.sqrt(dE) * B_sel[:, :, None, :] / denom
        x_prev = jnp.concatenate([jnp.zeros_like(x[:, :1]), x[:, :-1]], axis=1)
        x_in = 0.5 * (x + x_prev)
        Bx = B_bar * x_in[..., None]

        def op(left, right):
            a_l, b_l = left
            a_r, b_r = right
            return (a_r * a_l, a_r * b_l + b_r)
        _, all_h = lax.associative_scan(op, (A_bar, Bx), axis=1)
        y = jnp.sum(C_sel[:, :, None, :] * all_h, axis=-1)
        return y + D_param * x

    def _L0_ffn_ref(x, Wg, bg, Wge, bge, W1, b1, W2, b2):
        import jax, jax.numpy as jnp
        import numpy as np
        G, E = (4, 8)
        KG, KE = (2, 2)
        D, M = (192, 768)
        SCALE = 0.02

        def _combine_weights(xf, Wg, bg, Wge, bge):
            N = xf.shape[0]
            glog = xf @ Wg + bg
            gtop, gidx = jax.lax.top_k(glog, KG)
            ggate = jax.nn.softmax(gtop, axis=-1)
            elog_all = jnp.einsum('nd,gde->nge', xf, Wge) + bge
            elog = jnp.take_along_axis(elog_all, gidx[:, :, None], axis=1)
            etop, eidx = jax.lax.top_k(elog, KE)
            egate = jax.nn.softmax(etop, axis=-1)
            w = ggate[:, :, None] * egate
            flat = gidx[:, :, None] * E + eidx
            comb = jnp.zeros((N, G * E), xf.dtype).at[jnp.arange(N)[:, None, None], flat].add(w)
            return comb
        shp = x.shape
        xf = x.reshape(-1, D)
        comb = _combine_weights(xf, Wg, bg, Wge, bge)
        h = jax.nn.gelu(jnp.einsum('nd,edm->nem', xf, W1) + b1, approximate=False)
        y = jnp.einsum('nem,emd->ned', h, W2) + b2
        out = jnp.einsum('ne,ned->nd', comb, y)
        return out.reshape(shp)
    h = _L0_tok_ref(x, L0_tok_W, L0_tok_b, L0_tok_pos_emb)
    h = h + _L0_attn_ref(_layernorm(h, axis=-1), L0_attn_A_log, L0_attn_D_param, L0_attn_W_bc, L0_attn_W_dt, L0_attn_W_dtp, L0_attn_b_dt, L0_attn_rms_scale)
    h = h + _L0_ffn_ref(_layernorm(h, axis=-1), L0_ffn_Wg, L0_ffn_bg, L0_ffn_Wge, L0_ffn_bge, L0_ffn_W1, L0_ffn_b1, L0_ffn_W2, L0_ffn_b2)
    return h

_drawn_inputs = setup_inputs


def setup_inputs(seed=0):
    import zlib

    import numpy as np

    out = dict(_drawn_inputs(seed))
    spreads = {'L0_attn_D_param': (1.0, 0.2),
     'L0_attn_rms_scale': (1.0, 0.6),
     'L0_ffn_bg': (0.0, 0.8),
     'L0_ffn_bge': (0.0, 0.478),
     'L0_ffn_b1': (0.0, 0.8),
     'L0_ffn_b2': (0.0, 0.363)}
    factors = {'L0_tok_b': 2.671, 'L0_ffn_Wg': 2.715, 'L0_ffn_W1': 3.19, 'L0_ffn_W2': 2.923}
    for name, (base, spread) in spreads.items():
        noise = np.random.default_rng([zlib.crc32(name.encode()), seed]).standard_normal(out[name].shape)
        drawn = base * np.exp(spread * noise) if base else spread * noise
        out[name] = jnp.asarray(drawn.astype(out[name].dtype))
    for name, factor in factors.items():
        out[name] = (out[name] * factor).astype(out[name].dtype)
    return out
```

```python
from contextlib import ExitStack

import concourse.bass as bass
from concourse import mybir

F32 = mybir.dt.float32
F32R = mybir.dt.float32r
BF16 = mybir.dt.bfloat16
I32 = mybir.dt.int32
ACT = mybir.ActivationFunctionType
ALU = mybir.AluOpType
AX_X = mybir.AxisListType.X
LN2 = 0.6931471805599453

BATCH, CH, IMG, PATCH = 64, 3, 96, 16
HP = IMG // PATCH
WP = IMG // PATCH
SEQ = HP * WP
D = 192
NST = 16
RANK = 48
FLAT = CH * PATCH * PATCH
TOK = BATCH * SEQ
Q = 4
QB = BATCH // Q
QT = QB * SEQ
HT = QT // 2
TP = QB * HP
NCH = FLAT // 128
DB = D // 64
UC = 8
PAD = SEQ + 1
GROUPS, PER = 4, 8
NE = GROUPS * PER
M = 768
MC = M // 128
NR = GROUPS + NE
ROWW = D + NE
TOPK = 4
BLK = 128
NBLK = 104
SETR = 4
LO, HI = 0.0001, 10.0
CEN, HALF = (HI + LO) / 2, (HI - LO) / 2
DUPB = (0, 2, 4, 6, 0, 2)
WRING = 4


def tower(nc, t, out):
    ctx = ExitStack()
    with ctx:
        def sb(name, shape, dt=F32):
            return ctx.enter_context(nc.sbuf_tensor(name, shape, dt))

        def sem(name):
            return ctx.enter_context(nc.semaphore(name))

        rows_dram = nc.dram_tensor("rows_dram", (TOK + BLK, ROWW), F32, kind="Internal").ap()
        acc_dram = nc.dram_tensor("acc_dram", (TOK + BLK, D), F32, kind="Internal").ap()

        ps = ctx.enter_context(nc.psum_tensor("ps", [128, 8, 512], F32))

        ident = sb("ident", [128, 128])
        zero = sb("zero", [128, ROWW])
        iota = sb("iota", [128, 128])
        iota_p = sb("iota_p", [128, 1])
        tok_id = sb("tok_id", [TP, Q * WP])
        pad_id = sb("pad_id", [128, 1])
        carry = sb("carry", [128, NE])
        maskf = sb("maskf", [TP, Q * WP, NE])
        rank = sb("rank", [TP, Q * WP, NE])
        early = ExitStack()

        def sb(name, shape, dt=F32):
            return early.enter_context(nc.sbuf_tensor(name, shape, dt))

        sel = sb("sel", [128, UC, 128], F32R)
        red = sb("red", [128, UC, 64])
        shift = sb("shift", [TP, TP])
        tri = sb("tri", [TP, 128], BF16)
        ones = sb("ones", [TP, 128], BF16)
        rank_i = sb("rank_i", [TP, PER])
        upper = sb("upper", [TP, PER, PER])
        upper4 = sb("upper4", [TP, GROUPS, GROUPS])
        w_t = sb("w_t", [128, NCH, D])
        pos = sb("pos", [TP, WP * D])
        b_in = sb("b_in", [TP, D])
        wbc = sb("wbc", [128, 2, 2 * NST])
        wrep = sb("wrep", [128, 2, 2, 8, NST])
        wdt = sb("wdt", [128, 2, RANK])
        wdtp = sb("wdtp", [65, D])
        wrt = sb("wrt", [128, 2, NR])
        rbias = sb("rbias", [TP, NR])
        rms = sb("rms", [TP, D])
        dpar = sb("dpar", [TP, D])
        b2 = sb("b2", [NE, D])
        alog = sb("alog", [UC * DB, 128])
        abias = sb("abias", [128, UC * DB])
        cols = sb("cols", [128, 4])
        cen = sb("cen", [128, 1])
        x_in = sb("x_in", [TP, CH, PATCH * IMG])
        x_p = sb("x_p", [TP, WP, FLAT])
        w_in = x_p[:, 0:2, :]
        xt = sb("xt", [128, 2, NCH, TP])
        h = sb("h", [TP, WP, D])
        st6 = sb("st6", [TP, WP, 6])
        mv = sb("mv", [TP, WP, 2])
        sd = sb("sd", [TP, WP])
        rs = sb("rs", [TP, WP])
        xn = sb("xn", [TP, WP, D])
        rs2 = sb("rs2", [TP, WP])
        xs = sb("xs", [TP, WP, D])
        xnt = sb("xnt", [128, 2, QT])
        brep = sb("brep", [128, QT])
        crep = sb("crep", [128, QT])
        zt = sb("zt", [65, QT])
        bc = sb("bc", [TP, WP, 2 * NST])
        bcp = sb("bcp", [TP, WP, NST])
        cb = sb("cb", [TP, WP])
        ab = sb("ab", [TP, WP, D])
        ex = sb("ex", [TP, WP, D])
        lg = sb("lg", [TP, WP, D])
        w1m = sb("w1m", [TP, WP, D])
        dl = sb("dl", [TP, WP, D])
        ss = sb("ss", [TP, WP])
        th = sb("th", [TP, WP, D])
        sq = sb("sq", [TP, WP, D])
        two_l = sb("two_l", [TP, WP * DB, 2, 64])
        two_u = sb("two_u", [TP, WP * DB, 2, 64])
        rd = sb("rd", [128, DB, QT], F32R)
        ru = sb("ru", [128, DB, QT], F32R)
        at = sb("at", [128, 2, QB * PAD])
        wt = sb("wt", [128, 2, QB * PAD])
        dt_ = sb("dt_", [128, 2, QB * PAD])
        s_t = sb("s_t", [128, 2, QB * PAD])
        sel_f = s_t[:].rearrange("p a n -> p (a n)")[:, 0:UC * 128].rearrange("p (c m) -> p c m", c=UC)
        cs = sb("cs", [128, 3, QT])
        yt = sb("yt", [64, DB, QT])
        h2 = dl
        row = sb("row", [TP, WP, ROWW])
        gl = sb("gl", [TP, WP, GROUPS])
        el = sb("el", [TP, WP * GROUPS, PER])
        gs = sb("gs", [TP, WP, GROUPS])
        es = sb("es", [TP, WP * GROUPS, PER])
        gp = sb("gp", [TP, WP, GROUPS])
        ep = sb("ep", [TP, WP * GROUPS, PER])
        gmx = sb("gmx", [TP, WP])
        emx = sb("emx", [TP, WP * GROUPS])
        gcmp = sb("gcmp", [TP, WP, GROUPS, GROUPS])
        ecmp = x_p[:, 2:4, :].rearrange("p a n -> p (a n)").rearrange("p (w i j) -> p w i j", i=PER, j=PER)
        grk = sb("grk", [TP, 2, WP, GROUPS])
        erk = sb("erk", [TP, 2, WP * GROUPS, PER])
        gsel = sb("gsel", [TP, WP, GROUPS])
        esel = sb("esel", [TP, WP * GROUPS, PER])
        gz = sb("gz", [TP, WP])
        ez = sb("ez", [TP, WP * GROUPS])
        fac = sb("fac", [TP, WP, GROUPS])
        mask = sb("mask", [TP, WP + 1, NE], BF16)
        combt = sb("combt", [NE, WP, TP])

        names = ("passed", "set_dve", "const_in", "pad_set", "made", "copied", "turned", "x_loaded", "x_split", "patch_t", "patch_c", "emb",
                 "emb_sum", "ln", "ln_act", "xn_done", "shifted", "xs_done", "xn_t", "xn_c", "rep_pe", "rep_act",
                 "z_pe", "z_act", "bc_pe", "bc_dve", "dt_pe", "soft_act", "soft_pool", "dl_done", "rms_act",
                 "rms_dve", "gate_act", "u_done", "two", "dup_pe", "dup_hi", "dup_lo", "unit_rd", "unit_ru", "unit_a",
                 "unit_w", "unit_d", "unit_s", "unit_c", "unit_y", "y_c", "y_t", "skip_pool", "skip", "res",
                 "ln2", "ln2_act", "x2_done", "x2_t", "x2_c", "log_pe", "route", "route_act", "cnt_pe",
                 "comb_t", "comb_c", "b2_pe", "stored", "quarter_done")
        s = {n: sem(n) for n in names}
        block = early.enter_context(nc.Block())
        NCONST = 19
        NMADE = 24
        U = DB * UC
        ROUTE = 26
        HTS = HT // SEQ

        def tokens(ap, b=2):
            return ap.rearrange("p (s c) -> p s c", c=PAD)[:, :, 1:PAD]

        def y_out(act, q, k):
            b = 2 * (k % 2)
            act.wait_ge(s["unit_y"], q * U + (k + 1) * UC)
            act.activation(yt[:, k, :].rearrange("p (b n) -> p b n", b=2), ps[0:64, b:b + 2, 0:HT], ACT.Copy)\
                .then_inc(s["y_c"], 1)
        def turn_tokens(pe, src, done="xn_t"):
            for g in range(WP):
                for kc, p in ((0, 128), (1, 64)):
                    last = pe.transpose(ps[0:p, 2 * kc + g // 3, (g % 3) * TP:(g % 3 + 1) * TP],
                                        src[:, g, 128 * kc:128 * kc + p], ident[0:TP, 0:TP])
            last.then_inc(s[done], 1)

        @block.sync
        def _(sp):
            n = [0]

            def load(dst, src):
                sp.dma_start(dst, src).then_inc(s["const_in"], 16)
                n[0] += 1

            img = t["x"].rearrange("(q b) c (h p) w -> q b h c (p w)", q=Q, h=HP)
            load(w_in, t["L0_tok_W"].rearrange("(a p) f -> p a f", p=96))
            load(b_in[:], t["L0_tok_b"].partition_broadcast(TP))
            load(pos[:], t["L0_tok_pos_emb"].rearrange("(h w) d -> h (w d)", h=HP).partition_broadcast(QB))
            load(wbc[:, 0, :], t["L0_attn_W_bc"][0:128, :])
            load(wbc[0:64, 1, :], t["L0_attn_W_bc"][128:D, :])
            load(wdt[:, 0, :], t["L0_attn_W_dt"][0:128, :])
            load(wdt[0:64, 1, :], t["L0_attn_W_dt"][128:D, :])
            load(rms[:], t["L0_attn_rms_scale"].partition_broadcast(TP))
            load(dpar[:], t["L0_attn_D_param"].partition_broadcast(TP))
            load(alog[:], t["L0_attn_A_log"].rearrange("(u e) n -> u (e n)", e=8))
            load(wrt[:, 0, 0:GROUPS], t["L0_ffn_Wg"][0:128, :])
            load(wrt[0:64, 1, 0:GROUPS], t["L0_ffn_Wg"][128:D, :])
            wge = t["L0_ffn_Wge"].rearrange("g d e -> d g e")
            load(wrt[:, 0, GROUPS:NR].rearrange("p (g e) -> p g e", g=GROUPS), wge[0:128])
            load(wrt[0:64, 1, GROUPS:NR].rearrange("p (g e) -> p g e", g=GROUPS), wge[128:D])
            load(rbias[:, 0:GROUPS], t["L0_ffn_bg"].partition_broadcast(TP))
            load(rbias[:, GROUPS:NR], t["L0_ffn_bge"].rearrange("g e -> (g e)").partition_broadcast(TP))
            load(b2[:], t["L0_ffn_b2"])
            sp.wait_ge(s["made"], 4)
            load(wdtp[0:RANK, :], t["L0_attn_W_dtp"])
            load(wdtp[64:65, :], t["L0_attn_b_dt"].rearrange("(a d) -> a d", a=1))
            assert n[0] == NCONST, n
            sp.dma_start(rows_dram[TOK:TOK + BLK, :], zero[:]).then_inc(s["pad_set"], 16)
            sp.dma_start(acc_dram[TOK:TOK + BLK, :], zero[:, 0:D]).then_inc(s["pad_set"], 16)
            with sp.Fori(0, Q) as q:
                for c in range(CH):
                    sp.dma_start(x_in[:, c, :], img[bass.ds(q, 1)].rearrange("a b h c n -> (a b) h c n")[:, :, c, :])\
                        .then_inc(s["x_loaded"], 16)
                sp.wait_ge(s["route"], (q + 1) * ROUTE)
                sp.dma_start(rows_dram[bass.ds(q * QT, QT), :].rearrange("(p g) c -> p g c", p=TP), row[:])\
                    .then_inc(s["stored"], 16)
                sp.wait_ge(s["res"], (q + 1) * 6)
                sp.dma_start(acc_dram[bass.ds(q * QT, QT), :].rearrange("(p g) c -> p g c", p=TP), h2[:])\
                    .then_inc(s["stored"], 16)
                sp.wait_ge(s["stored"], (q + 1) * 32)
                sp.sem_inc(s["quarter_done"], 1)
                sp.wait_ge(s["quarter_done"], (q + 1) * 5)
                sp.sem_inc(s["passed"], 1)

        @block.gpsimd
        def _(pool):
            n = [0]

            def made(ins):
                n[0] += 1
                ins.then_inc(s["made"], 1)
                pool.wait_ge(s["made"], n[0])

            def cut(ap, pattern, base, mult, op=ALU.is_ge, fill=0.0):
                made(pool.affine_select(out=ap, in_=ap, compare_op=op, fill=fill, base=base,
                                        pattern=pattern, channel_multiplier=mult))

            made(pool.memset(zero[:], 0.0))
            made(pool.memset(zt[32:64, :], 0.0))
            made(pool.memset(zt[64:65, :], 1.0))
            made(pool.memset(wdtp[:], 0.0))
            made(pool.memset(ident[:], 0.0))
            cut(ident[:], [[-1, 128]], 0, 1, ALU.not_equal, 1.0)
            made(pool.memset(sel_f, 1.0))
            for half in (0, 64):
                cut(sel_f[half:half + 64], [[128, UC], [1, 128]], 0, -16)
                cut(sel_f[half:half + 64], [[-128, UC], [-1, 128]], 15, 16)
            made(pool.memset(red[:], 1.0))
            cut(red[:], [[128, UC], [-16, 64]], 0, 1)
            cut(red[:], [[-128, UC], [16, 64]], 15, -1)
            made(pool.memset(shift[:], 0.0))
            cut(shift[:], [[-1, TP]], 1, 1, ALU.not_equal, 1.0)
            made(pool.memset(shift[:].rearrange("k (b h) -> k b h", h=HP)[:, :, 0:1], 0.0))
            pool.memset(ones[:], 1.0)
            pool.memset(mask[:], 0.0)
            made(pool.memset(tri[:], 1.0))
            cut(tri[:], [[1, 128]], -1, -1)
            made(pool.memset(upper[:], 1.0))
            cut(upper[:], [[-1, PER], [1, PER]], -1, 0)
            made(pool.memset(upper4[:], 1.0))
            cut(upper4[:], [[-1, GROUPS], [1, GROUPS]], -1, 0)
            pool.iota(rank_i[:], [[1, PER]], 0, 0, allow_small_or_imprecise_dtypes=True)
            pool.iota(iota[:], [[1, 128]], 0, 0, allow_small_or_imprecise_dtypes=True)
            pool.iota(iota_p[:], [[0, 1]], 0, 1, allow_small_or_imprecise_dtypes=True)
            pool.iota(pad_id[:], [[0, 1]], TOK + 1, 1, allow_small_or_imprecise_dtypes=True)
            pool.iota(tok_id[:], [[QT, Q], [1, WP]], 1, WP, allow_small_or_imprecise_dtypes=True)
            pool.memset(at[:], 0.0)
            pool.memset(wt[:], 0.0)
            pool.memset(dt_[:], 0.0)
            made(pool.memset(carry[:], 0.0))
            assert n[0] == NMADE, n
            with pool.Fori(0, Q) as q:
                pool.wait_ge(s["soft_act"], q * 5 + 4)
                pool.sem_inc(s["passed"], 1)
                pool.tensor_scalar(w1m[:], ex[:], 1.0, -1.0, ALU.add, ALU.add).then_inc(s["soft_pool"], 1)
                pool.wait_ge(s["soft_pool"], q * 2 + 1)
                pool.tensor_tensor(ab[:], w1m[:], ex[:], ALU.subtract).then_inc(s["soft_pool"], 1)

                def add_shifted(i):
                    pool.wait_ge(s["unit_w"], q * U + i + 1)
                    if i >= 2:
                        pool.wait_ge(s["unit_s"], q * U + i - 1)
                    pool.tensor_tensor(dt_[:, i % 2, 1:], wt[:, i % 2, 1:], wt[:, i % 2, :-1], ALU.add)\
                        .then_inc(s["unit_d"], 1)

                for i in range(U):
                    add_shifted(i)
                    if i == 0:
                        pool.wait_ge(s["u_done"], q + 1)
                        pool.tensor_tensor(xs[:], xn[:], dpar[:].unsqueeze(1).to_broadcast([TP, WP, D]), ALU.mult)\
                            .then_inc(s["skip_pool"], 1)
                pool.wait_ge(s["unit_d"], (q + 1) * U)
                pool.sem_inc(s["quarter_done"], 1)
                pool.wait_ge(s["quarter_done"], (q + 1) * 5)

        @block.scalar
        def _(act):
            for j in range(NCH):
                act.wait_ge(s["turned"], j + 1)
                act.activation(w_t[:, j, :], ps[:, j % 4, 0:D], ACT.Copy).then_inc(s["copied"], 1)
            act.wait_ge(s["turned"], NCH + 1)
            act.wait_ge(s["set_dve"], 1)
            act.activation(abias[:], ps[:, 7, 0:UC * DB], ACT.Identity, bias=cols[:, 0:1], scale=-0.5)\
                .then_inc(s["copied"], 1)
            with act.Fori(0, Q) as q:
                for c in range(CH):
                    if c == 0:
                        act.wait_ge(s["x_loaded"], (q + 1) * 16 * CH)
                    act.activation(x_p[:, :, c * PATCH * PATCH:(c + 1) * PATCH * PATCH].rearrange("r g (p v) -> r p g v", p=PATCH),
                                   x_in[:, c, :].rearrange("r (p g v) -> r p g v", p=PATCH, g=WP), ACT.Copy)\
                        .then_inc(s["x_split"], 1)
                for g in range(WP):
                    b = 2 * (g % 2)
                    act.wait_ge(s["patch_t"], q * WP + g + 1)
                    if g >= 2:
                        act.wait_ge(s["emb"], q * WP + g - 1)
                    act.activation(xt[:, g % 2].rearrange("p (b j) n -> p b (j n)", b=2), ps[:, b:b + 2, 0:HT], ACT.Copy)\
                        .then_inc(s["patch_c"], 1)
                act.wait_ge(s["ln"], q * 3 + 2)
                act.activation(sd[:], mv[:, :, 1], ACT.Sqrt, bias=cols[0:TP, 1:2]).then_inc(s["ln_act"], 1)
                act.wait_ge(s["xn_t"], q + 1)
                for kc, p in ((0, 128), (1, 64)):
                    by_row = xnt[0:p, kc, :].rearrange("p (r g) -> p g r", g=WP)
                    for b in range(2):
                        last = act.activation(by_row[:, 3 * b:3 * b + 3, :],
                                              ps[0:p, 2 * kc + b, 0:HT].rearrange("p (g r) -> p g r", g=3), ACT.Copy)
                last.then_inc(s["xn_c"], 1)
                for j, dst in ((0, brep), (1, crep)):
                    act.wait_ge(s["rep_pe"], q * 2 + j + 1)
                    act.activation(dst[:].rearrange("p (b n) -> p b n", b=2), ps[:, 4 + 2 * j:6 + 2 * j, 0:HT], ACT.Copy)\
                        .then_inc(s["rep_act"], 1)
                act.wait_ge(s["z_pe"], q + 1)
                act.activation(zt[0:RANK].rearrange("p (b n) -> p b n", b=2), ps[0:RANK, 0:2, 0:HT], ACT.Copy)\
                    .then_inc(s["z_act"], 1)
                for j in range(3):
                    act.wait_ge(s["dt_pe"], q * 3 + j + 1)
                    act.activation(ab[:, 2 * j:2 * j + 2, :], ps[0:TP, 3 + j, 0:2 * D].rearrange("p (g d) -> p g d", g=2), ACT.Abs)\
                        .then_inc(s["soft_act"], 1)
                act.wait_ge(s["soft_act"], q * 5 + 3)
                act.activation(ex[:], ab[:], ACT.Exp, scale=-1.0).then_inc(s["soft_act"], 1)
                act.wait_ge(s["soft_act"], q * 5 + 4)
                act.activation(lg[:], ex[:], ACT.Ln, bias=1.0).then_inc(s["soft_act"], 1)
                act.wait_ge(s["dl_done"], q * 4 + 4)
                for g in range(WP):
                    last = act.activation(sq[:, g, :], dl[:, g, :], ACT.Square, accum_out=ss[:, g:g + 1])
                last.then_inc(s["rms_act"], 1)
                act.wait_ge(s["rms_act"], q * 2 + 1)
                act.activation(rs2[:], ss[:], ACT.Sqrt, scale=1.0 / D, bias=cols[0:TP, 2:3]).then_inc(s["rms_act"], 1)
                act.wait_ge(s["rms_dve"], q * 2 + 2)
                act.activation(th[:], w1m[:], ACT.Tanh, scale=1.0 / HALF, bias=cols[0:TP, 3:4]).then_inc(s["gate_act"], 1)
                act.wait_ge(s["gate_act"], q * 3 + 1)
                twice = [TP, WP * DB, 2, 64]
                act.activation(two_l[:], th[:].rearrange("p g (k c) -> p (g k) c", k=DB).unsqueeze(2).to_broadcast(twice), ACT.Ln,
                               scale=HALF, bias=cen[0:TP, :]).then_inc(s["gate_act"], 1)
                act.activation(sq[:], th[:], ACT.Sqrt, scale=HALF, bias=cen[0:TP, :]).then_inc(s["gate_act"], 1)
                act.wait_ge(s["u_done"], q + 1)
                act.activation(two_u[:], ex[:].rearrange("p g (k c) -> p (g k) c", k=DB).unsqueeze(2).to_broadcast(twice), ACT.Copy)\
                    .then_inc(s["two"], 1)
                for i in range(2 * DB):
                    dst, k = (rd, ru)[i // DB], i % DB
                    b = DUPB[i]
                    act.wait_ge(s["dup_pe"], q * 6 + i + 1)
                    act.activation(dst[:, k, :].rearrange("p (r b g) -> p b g r", b=2, g=3),
                                   ps[:, b:b + 2, 0:HT].rearrange("p b (g r) -> p b g r", g=3), ACT.Copy)\
                        .then_inc(s["dup_hi"], 1)
                for i in range(U):
                    act.wait_ge(s["unit_rd"], q * U + i + 1)
                    if i >= 2:
                        act.wait_ge(s["unit_s"], q * U + i - 1)
                    act.activation(tokens(at[:, i % 2]).rearrange("p (b s) c -> p b s c", b=2),
                                   ps[:, 4:6, 0:HT].rearrange("p b (s c) -> p b s c", c=SEQ), ACT.Tanh,
                                   scale=-0.5, bias=abias[:, i:i + 1]).then_inc(s["unit_a"], 1)
                    if i % UC == 3 and i > UC:
                        y_out(act, q, i // UC - 1)
                y_out(act, q, DB - 1)
                act.wait_ge(s["ln2"], q * 3 + 2)
                act.activation(sd[:], mv[:, :, 1], ACT.Sqrt, bias=cols[0:TP, 1:2]).then_inc(s["ln2_act"], 1)
                act.wait_ge(s["x2_t"], q + 1)
                for kc, p in ((0, 128), (1, 64)):
                    last = act.activation(xnt[0:p, kc, :].rearrange("p (b n) -> p b n", b=2),
                                          ps[0:p, 2 * kc:2 * kc + 2, 0:HT], ACT.Copy)
                last.then_inc(s["x2_c"], 1)
                act.wait_ge(s["route"], q * ROUTE + 6)
                act.activation(gp[:], gs[:], ACT.Exp)
                act.activation(ep[:], es[:], ACT.Exp).then_inc(s["route_act"], 1)
                act.wait_ge(s["comb_t"], q + 1)
                act.activation(combt[:].rearrange("e (b g) r -> e b (g r)", b=2), ps[0:NE, 0:2, 0:HT], ACT.Copy)\
                    .then_inc(s["comb_c"], 1)
                act.wait_ge(s["comb_c"], q + 1)
                act.sem_inc(s["quarter_done"], 1)
                act.wait_ge(s["quarter_done"], (q + 1) * 5)

        @block.tensor
        def _(pe):
            pe.wait_ge(s["const_in"], 16 * (NCONST))
            pe.wait_ge(s["made"], NMADE)
            for j in range(NCH):
                if j >= 4:
                    pe.wait_ge(s["copied"], j - 3)
                for a in range(2):
                    last = pe.transpose(ps[:, j % 4, a * 96:a * 96 + 96], w_in[:, a, j * 128:(j + 1) * 128], ident[0:96, 0:96])
                last.then_inc(s["turned"], 1)
            pe.transpose(ps[:, 7, 0:UC * DB], alog[:], ident[0:UC * DB, 0:UC * DB]).then_inc(s["turned"], 1)
            pe.wait_ge(s["copied"], NCH + 1)
            pe.wait_ge(s["set_dve"], 5)
            with pe.Fori(0, Q) as q:
                pe.wait_ge(s["x_split"], (q + 1) * CH)

                def patches(g):
                    if g >= 2:
                        pe.wait_ge(s["patch_c"], q * WP + g - 1)
                    for j in range(NCH):
                        src = x_p[:, g, j * 128:(j + 1) * 128]
                        last = pe.transpose(ps[:, 2 * (g % 2) + j // 3, (j % 3) * TP:(j % 3 + 1) * TP], src, ident[0:TP, 0:TP])
                    last.then_inc(s["patch_t"], 1)

                patches(0)
                for g in range(WP):
                    if g + 1 < WP:
                        patches(g + 1)
                    pe.wait_ge(s["patch_c"], q * WP + g + 1)
                    for j in range(NCH):
                        last = pe.matmul(ps[0:TP, 4 + g // 2, (g % 2) * D:(g % 2 + 1) * D], xt[:, g % 2, j, :], w_t[:, j, :],
                                         start=(j == 0), stop=(j == NCH - 1))
                    last.then_inc(s["emb"], 1)
                pe.wait_ge(s["xn_done"], q + 1)
                pe.matmul(ps[0:TP, 7, 0:D], shift[:], xn[:, WP - 1, :], start=True, stop=True).then_inc(s["shifted"], 1)
                turn_tokens(pe, xn)
                pe.wait_ge(s["xn_c"], q + 1)
                for j in range(2):
                    if j == 1:
                        pe.wait_ge(s["xs_done"], q + 1)
                    for b in range(2):
                        for kc, p in ((0, 128), (1, 64)):
                            last = pe.matmul(ps[:, 4 + 2 * j + b, 0:HT], wrep[0:p, kc, j].rearrange("p a n -> p (a n)"),
                                             xnt[0:p, kc, b * HT:(b + 1) * HT], start=(kc == 0), stop=(kc == 1))
                    last.then_inc(s["rep_pe"], 1)
                for b in range(2):
                    for kc, p in ((0, 128), (1, 64)):
                        last = pe.matmul(ps[0:RANK, b, 0:HT], wdt[0:p, kc, :], xnt[0:p, kc, b * HT:(b + 1) * HT],
                                         start=(kc == 0), stop=(kc == 1))
                last.then_inc(s["z_pe"], 1)
                for g in range(WP):
                    for kc, p in ((0, 128), (1, 64)):
                        last = pe.matmul(ps[0:TP, 2, g * 32:g * 32 + 32], xnt[0:p, kc, :].rearrange("p (r g) -> p g r", g=WP)[:, g, :],
                                         wbc[0:p, kc, :], start=(kc == 0), stop=(kc == 1), skip_group_check=True)
                last.then_inc(s["bc_pe"], 1)
                pe.wait_ge(s["z_act"], q + 1)
                pe.wait_ge(s["rep_act"], q * 2 + 1)
                for g in range(WP):
                    last = pe.matmul(ps[0:TP, 3 + g // 2, (g % 2) * D:(g % 2 + 1) * D],
                                     zt[:].rearrange("p (r g) -> p g r", g=WP)[:, g, :], wdtp[:], start=True, stop=True)
                    if g % 2:
                        last.then_inc(s["dt_pe"], 1)
                for i in range(2 * DB):
                    src, k = (two_l, two_u)[i // DB], i % DB
                    if i == 0:
                        pe.wait_ge(s["gate_act"], q * 3 + 2)
                        pe.wait_ge(s["bc_dve"], q * 3 + 1)
                    if i == DB:
                        pe.wait_ge(s["two"], q + 1)
                        pe.wait_ge(s["rep_act"], q * 2 + 2)
                    if i > DB:
                        pe.wait_ge(s["dup_lo"], q * 6 + i - DB)
                    for g in range(WP):
                        last = pe.transpose(ps[:, DUPB[i] + g // 3, (g % 3) * TP:(g % 3 + 1) * TP],
                                            src[:, g * DB + k].rearrange("p a c -> p (a c)"), ident[0:TP, 0:TP])
                    last.then_inc(s["dup_pe"], 1)
                pe.wait_ge(s["dup_lo"], (q + 1) * 6)

                def spread(i):
                    k, c = divmod(i, UC)
                    for src, bank, free, done in ((ru, 6, "unit_w", "unit_ru"), (rd, 4, "unit_a", "unit_rd")):
                        if i >= 1:
                            pe.wait_ge(s[free], q * U + i)
                        for b in range(2):
                            last = pe.matmul(ps[:, bank + b, 0:HT], sel[:, c, :], src[:, k, b * HT:(b + 1) * HT], start=True, stop=True)
                        last.then_inc(s[done], 1)

                def gather_y(i):
                    k, c = divmod(i, UC)
                    pe.wait_ge(s["unit_c"], q * U + i + 1)
                    if c == 0 and k >= 2:
                        pe.wait_ge(s["y_c"], q * DB + k - 1)
                    for b in range(2):
                        last = pe.matmul(ps[0:64, 2 * (k % 2) + b, 0:HT], red[:, c, :], cs[:, i % 3, b * HT:(b + 1) * HT],
                                         start=(c == 0), stop=(c == UC - 1))
                    last.then_inc(s["unit_y"], 1)

                spread(0)
                for i in range(U):
                    if i + 1 < U:
                        spread(i + 1)
                    if i >= 2:
                        gather_y(i - 2)
                gather_y(U - 2)
                gather_y(U - 1)
                pe.wait_ge(s["y_c"], (q + 1) * DB)
                pe.wait_ge(s["unit_w"], (q + 1) * U)
                pe.wait_ge(s["unit_a"], (q + 1) * U)
                pe.sem_inc(s["passed"], 1)
                for g in range(WP):
                    for k in range(DB):
                        last = pe.transpose(ps[0:TP, 4 + g // 2, (g % 2) * D + 64 * k:(g % 2) * D + 64 * k + 64],
                                            yt[:, k, :].rearrange("p (r g) -> p g r", g=WP)[:, g, :], ident[0:64, 0:64])
                last.then_inc(s["y_t"], 1)
                pe.wait_ge(s["x2_done"], q + 1)
                turn_tokens(pe, row, "x2_t")
                pe.wait_ge(s["x2_c"], q + 1)
                for g in range(WP):
                    for kc, p in ((0, 128), (1, 64)):
                        last = pe.matmul(ps[0:TP, 7, g * NR:(g + 1) * NR], xnt[0:p, kc, g * TP:(g + 1) * TP], wrt[0:p, kc, :],
                                         start=(kc == 0), stop=(kc == 1), skip_group_check=True)
                last.then_inc(s["log_pe"], 1)
                pe.wait_ge(s["route"], q * ROUTE + ROUTE - 2)
                pe.matmul(ps[:, 2, 0:(WP + 1) * NE], tri[:], mask[:].rearrange("p g e -> p (g e)"), start=True, stop=False,
                          skip_group_check=True)
                for g in range(WP):
                    last = pe.matmul(ps[:, 2, (g + 1) * NE:(WP + 1) * NE], ones[:],
                                     mask[:, g, :].unsqueeze(1).to_broadcast([TP, WP - g, NE]), start=False, stop=(g == WP - 1),
                                     skip_group_check=True)
                last.then_inc(s["cnt_pe"], 1)
                for g in range(WP):
                    last = pe.transpose(ps[0:NE, g // 3, (g % 3) * TP:(g % 3 + 1) * TP], row[:, g, D:ROWW], ident[0:TP, 0:TP])
                last.then_inc(s["comb_t"], 1)
                pe.wait_ge(s["comb_c"], q + 1)
                for g in range(WP):
                    last = pe.matmul(ps[0:TP, 4 + g // 2, (g % 2) * D:(g % 2 + 1) * D], combt[:, g, :], b2[:], start=True, stop=True)
                last.then_inc(s["b2_pe"], 1)
                pe.wait_ge(s["b2_pe"], q + 1)
                pe.sem_inc(s["quarter_done"], 1)
                pe.wait_ge(s["quarter_done"], (q + 1) * 5)

        @block.vector
        def _(dve):
            n = [0]

            def setup(ins):
                n[0] += 1
                ins.then_inc(s["set_dve"], 1)

            dve.memset(cols[:, 0:1], 0.5 * LN2)
            dve.memset(cols[:, 1:2], 1e-5)
            dve.memset(cols[:, 2:3], 1e-6)
            dve.memset(cen[:], CEN)
            setup(dve.memset(cols[:, 3:4], -CEN / HALF))
            dve.wait_ge(s["made"], NMADE)
            dve.wait_ge(s["const_in"], 16 * (NCONST))
            setup(dve.tensor_copy(sel[:], sel_f))
            for j in range(2):
                for kc, p in ((0, 128), (1, 64)):
                    last = dve.tensor_copy(wrep[0:p, kc, j], wbc[0:p, kc, j * NST:(j + 1) * NST].unsqueeze(1).to_broadcast([p, 8, NST]))
            setup(last)
            setup(dve.tensor_tensor(pos[:].rearrange("p (g d) -> p g d", d=D), pos[:].rearrange("p (g d) -> p g d", d=D),
                                    b_in[:].unsqueeze(1).to_broadcast([TP, WP, D]), ALU.add))
            dve.wait_ge(s["set_dve"], 4)
            setup(dve.memset(cs[:, :, 0:1], 0.0))
            with dve.Fori(0, Q) as q:
                for j in range(3):
                    dve.wait_ge(s["emb"], q * WP + 2 * j + 2)
                    dve.tensor_tensor(h[:, 2 * j:2 * j + 2, :], ps[0:TP, 4 + j, 0:2 * D].rearrange("p (g d) -> p g d", g=2),
                                      pos[:, 2 * j * D:(2 * j + 2) * D].rearrange("p (g d) -> p g d", g=2), ALU.add)\
                        .then_inc(s["emb_sum"], 1)
                dve.wait_ge(s["emb_sum"], q * 3 + 3)

                def norm(src, dst, steps, roots, done):
                    for g in range(WP):
                        last = dve.bn_stats(st6[:, g, :], src[:, g, :])
                    last.then_inc(s[steps], 1)
                    dve.wait_ge(s[steps], q * 3 + 1)
                    dve.sem_inc(s["passed"], 1)
                    for g in range(WP):
                        last = dve.bn_aggr(mv[:, g, :], st6[:, g, :])
                    last.then_inc(s[steps], 1)
                    dve.wait_ge(s[roots], q + 1)
                    dve.reciprocal(rs[:], sd[:]).then_inc(s[steps], 1)
                    dve.wait_ge(s[steps], q * 3 + 3)
                    for g in range(WP):
                        last = dve.tensor_scalar(dst[:, g, 0:D], src[:, g, :], mv[:, g, 0:1], rs[:, g:g + 1], ALU.subtract, ALU.mult)
                    last.then_inc(s[done], 1)

                norm(h, xn, "ln", "ln_act", "xn_done")
                dve.wait_ge(s["xn_done"], q + 1)
                dve.tensor_tensor(xs[:, 1:, :], xn[:, 1:, :], xn[:, :-1, :], ALU.add)
                dve.wait_ge(s["shifted"], q + 1)
                dve.tensor_tensor(xs[:, 0, :], ps[0:TP, 7, 0:D], xn[:, 0, :], ALU.add).then_inc(s["xs_done"], 1)
                dve.wait_ge(s["bc_pe"], q + 1)
                dve.tensor_copy(bc[:], ps[0:TP, 2, 0:WP * 32].rearrange("p (g n) -> p g n", g=WP)).then_inc(s["bc_dve"], 1)
                dve.wait_ge(s["bc_dve"], q * 3 + 1)
                dve.tensor_tensor(bcp[:], bc[:, :, 0:NST], bc[:, :, NST:2 * NST], ALU.mult).then_inc(s["bc_dve"], 1)
                dve.wait_ge(s["bc_dve"], q * 3 + 2)
                dve.tensor_reduce(cb[:], bcp[:], AX_X, ALU.add).then_inc(s["bc_dve"], 1)
                dve.wait_ge(s["soft_act"], q * 5 + 5)
                for j in range(3):
                    dve.scalar_tensor_tensor(out=dl[:, 2 * j:2 * j + 2, :], in0=ps[0:TP, 3 + j, 0:2 * D].rearrange("p (g d) -> p g d", g=2),
                                             scalar=0.0, in1=lg[:, 2 * j:2 * j + 2, :], op0=ALU.max, op1=ALU.add)\
                        .then_inc(s["dl_done"], 1)
                dve.wait_ge(s["soft_pool"], q * 2 + 2)
                dve.wait_ge(s["dl_done"], q * 4 + 3)
                dve.tensor_tensor(dl[:], dl[:], ab[:], ALU.subtract).then_inc(s["dl_done"], 1)
                dve.wait_ge(s["rms_act"], q * 2 + 2)
                dve.reciprocal(rs[:], rs2[:]).then_inc(s["rms_dve"], 1)
                dve.wait_ge(s["rms_dve"], q * 2 + 1)
                for g in range(WP):
                    last = dve.scalar_tensor_tensor(out=w1m[:, g, :], in0=dl[:, g, :], scalar=rs[:, g:g + 1], in1=rms[:],
                                                    op0=ALU.mult, op1=ALU.mult)
                last.then_inc(s["rms_dve"], 1)
                dve.wait_ge(s["gate_act"], q * 3 + 3)
                dve.wait_ge(s["xs_done"], q + 1)
                dve.scalar_tensor_tensor(out=ex[:], in0=sq[:], scalar=0.25, in1=xs[:], op0=ALU.mult, op1=ALU.mult)\
                    .then_inc(s["u_done"], 1)
                for i in range(2 * DB):
                    dst, k = (rd, ru)[i // DB], i % DB
                    b = DUPB[i]
                    dve.wait_ge(s["dup_hi"], q * 6 + i + 1)
                    part = dst[64:128, k, :].rearrange("p (r b g) -> p b g r", b=2, g=3)
                    dve.tensor_tensor(part, ps[64:128, b:b + 2, 0:HT].rearrange("p b (g r) -> p b g r", g=3), part.bitcast(F32),
                                      ALU.subtract).then_inc(s["dup_lo"], 1)

                def inputs(i):
                    dve.wait_ge(s["unit_ru"], q * U + i + 1)
                    if i >= 2:
                        dve.wait_ge(s["unit_d"], q * U + i - 1)
                    dve.tensor_tensor(tokens(wt[:, i % 2]).rearrange("p (b s) c -> p b s c", b=2),
                                      ps[:, 6:8, 0:HT].rearrange("p b (s c) -> p b s c", c=SEQ),
                                      brep[:].rearrange("p (b s c) -> p b s c", b=2, c=SEQ), ALU.mult).then_inc(s["unit_w"], 1)

                def outputs(i):
                    dve.wait_ge(s["unit_s"], q * U + i + 1)
                    if i >= 3:
                        dve.wait_ge(s["unit_y"], q * U + i - 2)
                    dve.tensor_tensor(cs[:, i % 3, :].rearrange("p (s c) -> p s c", c=SEQ), tokens(s_t[:, i % 2]),
                                      crep[:].rearrange("p (s c) -> p s c", c=SEQ), ALU.mult).then_inc(s["unit_c"], 1)

                inputs(0)
                for i in range(U):
                    if i + 1 < U:
                        inputs(i + 1)
                    if i >= 1:
                        outputs(i - 1)
                    dve.wait_ge(s["unit_d"], q * U + i + 1)
                    dve.wait_ge(s["unit_a"], q * U + i + 1)
                    dve.tensor_tensor_scan(s_t[:, i % 2, :], dt_[:, i % 2, :], at[:, i % 2, :], 0.0, ALU.add, ALU.mult)\
                        .then_inc(s["unit_s"], 1)
                outputs(U - 1)
                dve.wait_ge(s["skip_pool"], q + 1)
                for g in range(WP):
                    last = dve.scalar_tensor_tensor(out=th[:, g, :], in0=ex[:, g, :], scalar=cb[:, g:g + 1], in1=xs[:, g, :],
                                                    op0=ALU.mult, op1=ALU.add)
                last.then_inc(s["skip"], 1)
                dve.wait_ge(s["skip"], q * 2 + 1)
                dve.tensor_tensor(h[:], h[:], th[:], ALU.add).then_inc(s["skip"], 1)
                dve.wait_ge(s["skip"], q * 2 + 2)
                dve.wait_ge(s["y_t"], q + 1)
                pair = "p (g d) -> p g d"
                for j in range(3):
                    dve.tensor_tensor(h2[:, 2 * j:2 * j + 2, :], ps[0:TP, 4 + j, 0:2 * D].rearrange(pair, g=2),
                                      h[:, 2 * j:2 * j + 2, :], ALU.add).then_inc(s["res"], 1)
                dve.wait_ge(s["res"], q * 6 + 3)
                norm(h2, row, "ln2", "ln2_act", "x2_done")
                m = [0]

                def link(ins):
                    m[0] += 1
                    ins.then_inc(s["route"], 1)
                    dve.wait_ge(s["route"], q * ROUTE + m[0])

                WG = WP * GROUPS
                dve.wait_ge(s["log_pe"], q + 1)
                logits = ps[0:TP, 7, 0:WP * NR].rearrange("p (g n) -> p g n", g=WP)
                link(dve.tensor_tensor(gl[:], logits[:, :, 0:GROUPS], rbias[:, 0:GROUPS].unsqueeze(1).to_broadcast([TP, WP, GROUPS]), ALU.add))
                link(dve.tensor_tensor(el[:].rearrange("p (w g) e -> p w (g e)", g=GROUPS), logits[:, :, GROUPS:NR],
                                       rbias[:, GROUPS:NR].unsqueeze(1).to_broadcast([TP, WP, NE]), ALU.add))
                link(dve.tensor_reduce(gmx[:], gl[:], AX_X, ALU.max))
                link(dve.tensor_reduce(emx[:], el[:], AX_X, ALU.max))
                link(dve.tensor_tensor(gs[:], gl[:], gmx[:].unsqueeze(2).to_broadcast([TP, WP, GROUPS]), ALU.subtract))
                link(dve.tensor_tensor(es[:], el[:], emx[:].unsqueeze(2).to_broadcast([TP, WG, PER]), ALU.subtract))
                for x, cmp, up, rk, selx, w, n_ in ((gl, gcmp[:], upper4, grk, gsel, WP, GROUPS), (el, ecmp, upper, erk, esel, WG, PER)):
                    big = [TP, w, n_, n_]
                    link(dve.tensor_tensor(cmp, x[:].unsqueeze(2).to_broadcast(big), x[:].unsqueeze(3).to_broadcast(big), ALU.is_gt))
                    link(dve.tensor_tensor(cmp.rearrange("p w i j -> p w (i j)"), cmp.rearrange("p w i j -> p w (i j)"),
                                           up[:].rearrange("p i j -> p (i j)").unsqueeze(1).to_broadcast([TP, w, n_ * n_]), ALU.mult))
                    dve.tensor_reduce(rk[:, 0], cmp, AX_X, ALU.add)
                    link(dve.tensor_reduce(rk[:, 1], cmp.rearrange("p w i j -> p w j i"), AX_X, ALU.add))
                    link(dve.tensor_tensor(rk[:, 0], rk[:, 0], rk[:, 1], ALU.subtract))
                    link(dve.tensor_tensor(rk[:, 0], rk[:, 0], rank_i[:, 0:n_].unsqueeze(1).to_broadcast([TP, w, n_]), ALU.add))
                    link(dve.tensor_scalar(selx[:], rk[:, 0], 2.0, None, ALU.is_lt))
                dve.wait_ge(s["route_act"], q + 1)
                dve.tensor_tensor(gp[:], gp[:], gsel[:], ALU.mult)
                link(dve.tensor_tensor(ep[:], ep[:], esel[:], ALU.mult))
                dve.tensor_reduce(gz[:], gp[:], AX_X, ALU.add)
                link(dve.tensor_reduce(ez[:], ep[:], AX_X, ALU.add))
                dve.reciprocal(gz[:], gz[:])
                link(dve.reciprocal(ez[:], ez[:]))
                link(dve.tensor_tensor(fac[:], gp[:], gz[:].unsqueeze(2).to_broadcast([TP, WP, GROUPS]), ALU.mult))
                fac24 = fac[:].rearrange("p w g -> p (w g)")
                link(dve.tensor_tensor(fac24, fac24, ez[:], ALU.mult))
                chosen = maskf[:, bass.ds(q * WP, WP), :]
                dve.tensor_tensor(row[:, :, D:ROWW].rearrange("p w (g e) -> p w g e", g=GROUPS), ep[:].rearrange("p (w g) e -> p w g e", g=GROUPS),
                                  fac[:].unsqueeze(3).to_broadcast([TP, WP, GROUPS, PER]), ALU.mult)
                dve.tensor_tensor(chosen.rearrange("p w (g e) -> p (w g) e", g=GROUPS), esel[:],
                                  gsel[:].rearrange("p w g -> p (w g)").unsqueeze(2).to_broadcast([TP, WG, PER]), ALU.mult)
                link(dve.tensor_tensor(mask[:, 0:WP, :].rearrange("p w (g e) -> p (w g) e", g=GROUPS), esel[:],
                                       gsel[:].rearrange("p w g -> p (w g)").unsqueeze(2).to_broadcast([TP, WG, PER]), ALU.mult))
                assert m[0] == ROUTE - 2, m
                dve.wait_ge(s["cnt_pe"], q + 1)
                link(dve.tensor_tensor(rank[:, bass.ds(q * WP, WP), :], ps[0:TP, 2, 0:WP * NE].rearrange("p (w e) -> p w e", w=WP),
                                       carry[0:TP].unsqueeze(1).to_broadcast([TP, WP, NE]), ALU.add))
                link(dve.tensor_tensor(carry[:], carry[:], ps[:, 2, WP * NE:(WP + 1) * NE], ALU.add))
                dve.wait_ge(s["b2_pe"], q + 1)
                for j in range(3):
                    dve.tensor_tensor(h2[:, 2 * j:2 * j + 2, :], h2[:, 2 * j:2 * j + 2, :],
                                      ps[0:TP, 4 + j, 0:2 * D].rearrange(pair, g=2), ALU.add).then_inc(s["res"], 1)
                dve.wait_ge(s["res"], (q + 1) * 6)
                dve.sem_inc(s["quarter_done"], 1)
                dve.wait_ge(s["quarter_done"], (q + 1) * 5)

        early.close()
        def lb(name, shape, dt=F32):
            return ctx.enter_context(nc.sbuf_tensor(name, shape, dt))

        NG = Q * WP
        cnt_i = lb("cnt_i", [128, NE], I32)
        nblk_i = lb("nblk_i", [128, NE], I32)
        nblk = lb("nblk", [128, NE])
        endb = lb("endb", [128, NE])
        first = lb("first", [128, NE])
        key = lb("key", [TP, NG, NE])
        top = lb("top", [TP, NG, 8])
        slot_i = lb("slot_i", [TP, NG, TOPK], I32)
        at_i = lb("at_i", [TP, 2, NG * TOPK], I32)
        at_f = lb("at_f", [TP, 2, NG * TOPK])
        is_row = lb("is_row", [TP, 8, BLK], F32R)
        is_blk = lb("is_blk", [TP, 8, NBLK], F32R)
        passed_e = lb("passed_e", [128, NE])
        e_col = lb("e_col", [128, 1])
        e_tab = lb("e_tab", [1, 128], I32)
        ring_tab = lb("ring_tab", [1, 128], I32)
        end_tab = lb("end_tab", [1, NE], I32)
        empty = lb("empty", [128, NBLK])
        ix = lb("ix", [128, NBLK + SETR], I32)
        ixg = lb("ixg", [128, SETR], I32)
        ixs = lb("ixs", [128, SETR], I32)
        xg = lb("xg", [128, SETR, ROWW])
        xa = lb("xa", [128, 2, BLK])
        xb = lb("xb", [65, 2, BLK])
        w1a = lb("w1a", [128, WRING, M])
        w1b = lb("w1b", [65, WRING, M])
        w2 = lb("w2", [128, WRING, MC, D])
        ht = lb("ht", [128, 2, M])
        ys = lb("ys", [128, 2, D])
        for n_ in ("tab", "oh", "oh_used", "e_t", "ready", "gathered0", "gathered1", "gathered2", "gathered3", "col",
                   "added", "x_t", "x_e", "h_pe", "h_act", "y_pe", "y_dve",
                   "w_in0", "w_in1", "w_in2", "w_in3", "w_ready", "out_done", "b1_one"):
            s[n_] = sem("p2_" + n_)
        gathered = [s[f"gathered{j}"] for j in range(SETR)]
        w_in_ = [s[f"w_in{j}"] for j in range(WRING)]
        MH = M // 2
        block2 = ctx.enter_context(nc.Block())

        @block2.sync
        def _(sp):
            def load_expert(e, j):
                one = (lambda ap: ap[e]) if isinstance(e, int) else (lambda ap: ap[bass.ds(e, 1)][0])
                w1, w2_, b1 = one(t["L0_ffn_W1"]), one(t["L0_ffn_W2"]), one(t["L0_ffn_b1"])
                sp.dma_start(w1a[:, j, :], w1[0:128, :]).then_inc(w_in_[j], 16)
                sp.dma_start(w1b[0:64, j, :], w1[128:D, :]).then_inc(w_in_[j], 16)
                sp.dma_start(w1b[64:65, j, :], b1.rearrange("(a m) -> a m", a=1)).then_inc(w_in_[j], 16)
                sp.dma_start(w2[:, j, :, :], w2_.rearrange("(c p) d -> p c d", p=128)).then_inc(w_in_[j], 16)

            for e in range(WRING):
                load_expert(e, e)
                if e >= 1:
                    sp.wait_ge(w_in_[e - 1], 64)
                    sp.sem_inc(s["w_ready"], 1)
            sp.wait_ge(s["ready"], 1)
            with sp.Fori(1, NE // WRING) as r:
                for j in range(WRING):
                    end = sp.value_load(end_tab[0:1, bass.ds((r - 1) * WRING + j, 1)], min_val=1, max_val=NBLK)
                    sp.wait_ge(s["y_pe"], end)
                    load_expert(r * WRING + j, j)
                    sp.wait_ge(w_in_[(j - 1) % WRING], 64 * r if j == 0 else 64 * (r + 1))
                    sp.sem_inc(s["w_ready"], 1)
            sp.wait_ge(w_in_[WRING - 1], 64 * (NE // WRING))
            sp.sem_inc(s["w_ready"], 1)
            sp.wait_ge(s["added"], 16 * NBLK)
            sp.dma_start(out.rearrange("b s d -> (b s) d"), acc_dram[0:TOK, :]).then_inc(s["out_done"], 16)
            sp.wait_ge(s["out_done"], 16)

        @block2.gpsimd
        def _(pool):
            def column(ring, t_, j):
                pool.tensor_copy(ring[:, j:j + 1], ix[:, bass.ds(t_, 1)]).then_inc(s["col"], 1)

            def gather(t_, j, cols):
                column(ixg, t_, j)
                pool.wait_ge(s["col"], cols)
                pool.sem_inc(s["passed"], 1)
                pool.indirect_dma_start(xg[:, j, :], None, rows_dram, bass.IndirectOffsetOnAxis(ixg[:, j:j + 1], 0))\
                    .then_inc(gathered[j], 16)

            pool.wait_ge(s["ready"], 1)
            for j in range(SETR):
                gather(j, j, j + 1)
            with pool.Fori(0, NBLK // SETR) as r:
                for j in range(SETR):
                    if j > 0:
                        pool.wait_ge(s["added"], (r * SETR + j) * 16)
                    column(ixs, r * SETR + j, j)
                    pool.wait_ge(s["col"], (r * SETR + j) * 2 + SETR + 1)
                    pool.wait_ge(s["y_dve"], r * SETR + j + 1)
                    pool.sem_inc(s["passed"], 1)
                    pool.indirect_dma_start(acc_dram, bass.IndirectOffsetOnAxis(ixs[:, j:j + 1], 0), ys[:, j % 2, :], None,
                                            compute_op=ALU.add).then_inc(s["added"], 16)
                    gather(r * SETR + j + SETR, j, (r * SETR + j + 1) * 2 + SETR)
                pool.wait_ge(s["added"], (r + 1) * SETR * 16)
                pool.sem_inc(s["passed"], 1)
            for j in range(SETR):
                pool.wait_ge(gathered[j], 16 * (NBLK // SETR + 1))

        def in_steps(eng, step):
            for i in range(SETR):
                step(i, i)
            with eng.Fori(0, NBLK // SETR - 1) as r:
                for j in range(SETR):
                    step(r * SETR + j + SETR, j)
            step(NBLK, 0)

        @block2.scalar
        def _(act):
            act.wait_ge(s["b1_one"], 1)

            def x_out(t_, j):
                act.wait_ge(s["x_t"], t_ + 1)
                if not (isinstance(t_, int) and t_ < 2):
                    act.wait_ge(s["h_pe"], t_ - 1)
                act.activation(xa[:, j, :], ps[:, 5 * j, 0:BLK], ACT.Copy)
                act.activation(xb[0:64, j, :], ps[0:64, 5 * j, BLK:2 * BLK], ACT.Copy).then_inc(s["x_e"], 1)

            def step(t_, j):
                fixed = isinstance(t_, int)
                if fixed and t_ == 0:
                    x_out(0, 0)
                if not fixed or t_ < NBLK:
                    act.wait_ge(s["h_pe"], t_ + 1)
                    if not fixed or t_ >= 2:
                        act.wait_ge(s["y_pe"], t_ - 1)
                    b = 1 + 2 * (j % 2)
                    act.activation(ht[:, j % 2, :].rearrange("p (b m) -> p b m", b=2), ps[:, b:b + 2, 0:MH], ACT.Gelu)\
                        .then_inc(s["h_act"], 1)
                if not fixed or t_ + 1 < NBLK:
                    x_out(t_ + 1, (j + 1) % 2)

            in_steps(act, step)

        @block2.tensor
        def _(pe):
            pe.wait_ge(s["e_t"], 1)
            pe.transpose(ps[0:1, 1, 0:128], e_col[:], ident[:]).then_inc(s["e_t"], 1)
            for g in range(NG):
                for k in range(TOPK):
                    i = g * TOPK + k
                    pe.wait_ge(s["oh"], i + 1)
                    pe.matmul(ps[:, 0, 0:NBLK], is_row[:, i % 8, :], is_blk[:, i % 8, :], start=(i == 0), stop=(i == NG * TOPK - 1))\
                        .then_inc(s["oh_used"], 1)
            pe.wait_ge(s["ready"], 1)

            def turn_x(t_, j):
                if isinstance(t_, int):
                    pe.wait_ge(gathered[j], (t_ // SETR + 1) * 16)
                else:
                    pe.wait_ge(gathered[j], (t_ - j) * (16 // SETR) + 16)
                if not isinstance(t_, int) or t_ >= 2:
                    pe.wait_ge(s["x_e"], t_ - 1)
                pe.sem_inc(s["passed"], 1)
                pe.transpose(ps[:, 5 * (j % 2), 0:BLK], xg[:, j, 0:128], ident[:])
                pe.transpose(ps[0:64, 5 * (j % 2), BLK:2 * BLK], xg[:, j, 128:D], ident[:]).then_inc(s["x_t"], 1)

            def hidden(b, x, k):
                for c in range(MC):
                    dst = ps[:, b + c // 3, (c % 3) * BLK:(c % 3 + 1) * BLK]
                    pe.matmul(dst, w1a[:, k, c * 128:(c + 1) * 128], xa[:, x, :], start=True, stop=False)
                    last = pe.matmul(dst, w1b[:, k, c * 128:(c + 1) * 128], xb[:, x, :], start=False, stop=True)
                last.then_inc(s["h_pe"], 1)

            def output(b, x, k):
                for c in range(MC):
                    last = pe.matmul(ps[:, b, 0:D], ht[:, x, c * BLK:(c + 1) * BLK], w2[:, k, c, :],
                                     start=(c == 0), stop=(c == MC - 1))
                last.then_inc(s["y_pe"], 1)

            def at_place(place, layer, b, x):
                with pe.If(place < 2):
                    with pe.If(place < 1):
                        layer(b, x, 0)
                    with pe.Else():
                        layer(b, x, 1)
                with pe.Else():
                    with pe.If(place < 3):
                        layer(b, x, 2)
                    with pe.Else():
                        layer(b, x, 3)

            held = [None]

            def step(t_, j):
                fixed = isinstance(t_, int)
                if fixed and t_ == 0:
                    turn_x(0, 0)
                if not fixed or t_ < NBLK:
                    e = pe.value_load(e_tab[0:1, bass.ds(t_, 1)], min_val=0, max_val=NE - 1)
                    place = e & (WRING - 1)
                    before, held[0] = held[0], (place, j)
                    pe.wait_ge(s["w_ready"], e + 1)
                    pe.wait_ge(s["x_e"], t_ + 1)
                    if not fixed or t_ >= 2:
                        pe.wait_ge(s["h_act"], t_ - 1)
                    pe.sem_inc(s["passed"], 1)
                    at_place(place, hidden, 1 + 2 * (j % 2), j % 2)
                if not fixed or t_ + 1 < NBLK:
                    turn_x(t_ + 1, (j + 1) % SETR)
                if not fixed or t_ >= 1:
                    if fixed or j == 0:
                        place = pe.value_load(ring_tab[0:1, bass.ds(t_ - 1, 1)], min_val=0, max_val=WRING - 1)
                    else:
                        place = before[0]
                    pe.wait_ge(s["h_act"], t_)
                    if not fixed or t_ >= 3:
                        pe.wait_ge(s["y_dve"], t_ - 2)
                    pe.sem_inc(s["passed"], 1)
                    at_place(place, output, 6 + (j - 1) % 2, (j - 1) % 2)

            in_steps(pe, step)

        @block2.vector
        def _(dve):
            n = [0]

            def link(ins):
                n[0] += 1
                ins.then_inc(s["tab"], 1)
                dve.wait_ge(s["tab"], n[0])

            dve.memset(xb[64:65, :, :], 1.0).then_inc(s["b1_one"], 1)
            link(dve.tensor_scalar(cnt_i[:], carry[:], float(BLK - 1), None, ALU.add))
            link(dve.tensor_scalar(nblk_i[:], cnt_i[:], 7, None, ALU.arith_shift_right))
            link(dve.tensor_copy(nblk[:], nblk_i[:]))
            link(dve.tensor_scalar(nblk[:], nblk[:], 1.0, None, ALU.max))
            link(dve.tensor_tensor_scan(endb[:], nblk[:], zero[:, 0:NE], 0.0, ALU.add, ALU.add))
            link(dve.tensor_tensor(first[:], endb[:], nblk[:], ALU.subtract))
            link(dve.tensor_scalar(first[:], first[:], float(BLK), 1.0, ALU.mult, ALU.add))
            link(dve.tensor_scalar(passed_e[:], endb[:], iota_p[:, 0:1], None, ALU.is_le))
            link(dve.tensor_reduce(e_col[:], passed_e[:], AX_X, ALU.add))
            dve.tensor_scalar(e_col[:], e_col[:], float(NE - 1), None, ALU.min).then_inc(s["e_t"], 1)
            dve.tensor_copy(end_tab[:], endb[0:1, :])
            link(dve.tensor_tensor(key[:], rank[:], first[0:TP].unsqueeze(1).to_broadcast([TP, NG, NE]), ALU.add))
            link(dve.tensor_tensor(key[:], key[:], maskf[:], ALU.mult))
            for g in range(NG):
                last = dve.max(top[:, g, :], key[:, g, :])
            link(last)
            link(dve.tensor_scalar(slot_i[:], top[:, :, 0:TOPK], -1.0, None, ALU.add))
            flat = slot_i[:].rearrange("p g k -> p (g k)")
            dve.tensor_scalar(at_i[:, 0, :], flat, BLK - 1, None, ALU.bitwise_and)
            link(dve.tensor_scalar(at_i[:, 1, :], flat, 7, None, ALU.arith_shift_right))
            link(dve.tensor_copy(at_f[:], at_i[:]))
            dve.wait_ge(s["e_t"], 2)
            link(dve.tensor_copy(e_tab[:], ps[0:1, 1, 0:128]))
            dve.tensor_scalar(ring_tab[:], e_tab[:], WRING - 1, None, ALU.bitwise_and)
            for g in range(NG):
                for k in range(TOPK):
                    i = g * TOPK + k
                    if i >= 8:
                        dve.wait_ge(s["oh_used"], i - 7)
                    dve.tensor_scalar(is_row[:, i % 8, :], iota[0:TP, :], at_f[:, 0, i:i + 1], None, ALU.is_equal)
                    dve.tensor_scalar(is_blk[:, i % 8, :], iota[0:TP, 0:NBLK], at_f[:, 1, i:i + 1], tok_id[:, g:g + 1],
                                      ALU.is_equal, ALU.mult).then_inc(s["oh"], 1)
            dve.wait_ge(s["oh_used"], NG * TOPK)
            link(dve.tensor_scalar(empty[:], ps[:, 0, 0:NBLK], 0.0, pad_id[:, 0:1], ALU.is_equal, ALU.mult))
            dve.tensor_scalar(ix[:, NBLK:], zero[:, 0:SETR], 0.0, pad_id[:, 0:1], ALU.mult, ALU.add)
            link(dve.scalar_tensor_tensor(out=empty[:], in0=ps[:, 0, 0:NBLK], scalar=-1.0, in1=empty[:], op0=ALU.add, op1=ALU.add))
            link(dve.tensor_scalar(ix[:, NBLK:], zero[:, 0:SETR], pad_id[:, 0:1], -1.0, ALU.add, ALU.add))
            dve.tensor_copy(ix[:, 0:NBLK], empty[:]).then_inc(s["ready"], 1)

            def step(t_, j):
                fixed = isinstance(t_, int)
                if not fixed or t_ >= 1:
                    e = dve.value_load(e_tab[0:1, bass.ds(t_ - 1, 1)], min_val=0, max_val=NE - 1)
                    dve.wait_ge(s["y_pe"], t_)
                    if not fixed or t_ >= 3:
                        dve.wait_ge(s["added"], 16 * (t_ - 2))
                    dve.tensor_scalar(ys[:, (j - 1) % 2, :], ps[:, 6 + (j - 1) % 2, 0:D], xg[:, (j - 1) % SETR, bass.ds(e + D, 1)], None, ALU.mult)\
                        .then_inc(s["y_dve"], 1)

            in_steps(dve, step)


_INS = ["x", "L0_tok_W", "L0_tok_b", "L0_tok_pos_emb", "L0_attn_A_log", "L0_attn_D_param", "L0_attn_W_bc",
        "L0_attn_W_dt", "L0_attn_W_dtp", "L0_attn_b_dt", "L0_attn_rms_scale", "L0_ffn_Wg", "L0_ffn_bg",
        "L0_ffn_Wge", "L0_ffn_bge", "L0_ffn_W1", "L0_ffn_b1", "L0_ffn_W2", "L0_ffn_b2"]


def kernel(**inputs):
    import numpy as _np
    import concourse.bacc as _bacc
    from concourse import mybir as _mybir
    from concourse.bass_utils import run_bass_kernel_spmd as _run

    nc = _bacc.Bacc("TRN2", target_bir_lowering=False, num_devices=1)
    arrays, t = {}, {}
    for name in _INS:
        a = _np.ascontiguousarray(inputs[name])
        arrays[f"in_{name}"] = a
        t[name] = nc.dram_tensor(f"in_{name}", a.shape, _mybir.dt.from_np(a.dtype), kind="ExternalInput").ap()
    out = nc.dram_tensor("out_0", (BATCH, SEQ, D), F32, kind="ExternalOutput").ap()
    tower(nc, t, out)
    r = _run(nc, [arrays], core_ids=[0])
    return r.results[0]["out_0"]
```

```python
from contextlib import ExitStack

import concourse.bass as bass
from concourse import mybir

F32 = mybir.dt.float32
F32R = mybir.dt.float32r
BF16 = mybir.dt.bfloat16
I32 = mybir.dt.int32
ACT = mybir.ActivationFunctionType
ALU = mybir.AluOpType
AX_X = mybir.AxisListType.X
LN2 = 0.6931471805599453

BATCH, CH, IMG, PATCH = 64, 3, 96, 16
HP = IMG // PATCH
WP = IMG // PATCH
SEQ = HP * WP
D = 192
NST = 16
RANK = 48
FLAT = CH * PATCH * PATCH
TOK = BATCH * SEQ
Q = 4
QB = BATCH // Q
QT = QB * SEQ
HT = QT // 2
TP = QB * HP
NCH = FLAT // 128
DB = D // 64
UC = 8
PAD = SEQ + 1
GROUPS, PER = 4, 8
NE = GROUPS * PER
M = 768
MC = M // 128
NR = GROUPS + NE
ROWW = D + NE
TOPK = 4
BLK = 128
NBLK = 104
SETR = 4
LO, HI = 0.0001, 10.0
CEN, HALF = (HI + LO) / 2, (HI - LO) / 2
MID = 2
DUPS = (("l", 0), ("l", 1), ("u", 0), ("u", 1), ("l", 2), ("u", 2))
WRING = 4


def tower(nc, t, out):
    ctx = ExitStack()
    with ctx:
        def sb(name, shape, dt=F32):
            return ctx.enter_context(nc.sbuf_tensor(name, shape, dt))

        def sem(name):
            return ctx.enter_context(nc.semaphore(name))

        rows_dram = nc.dram_tensor("rows_dram", (TOK + BLK, ROWW), F32, kind="Internal").ap()
        acc_dram = nc.dram_tensor("acc_dram", (TOK + BLK, D), F32, kind="Internal").ap()

        ps = ctx.enter_context(nc.psum_tensor("ps", [128, 8, 512], F32))

        ident = sb("ident", [128, 128])
        zero = sb("zero", [128, ROWW])
        iota = sb("iota", [128, 128])
        iota_p = sb("iota_p", [128, 1])
        tok_id = sb("tok_id", [TP, Q * WP])
        pad_id = sb("pad_id", [128, 1])
        carry = sb("carry", [128, NE])
        maskf = sb("maskf", [TP, Q * WP, NE])
        rank = sb("rank", [TP, Q * WP, NE])
        early = ExitStack()

        def sb(name, shape, dt=F32):
            return early.enter_context(nc.sbuf_tensor(name, shape, dt))

        sel = sb("sel", [128, UC, 128], F32R)
        red = sb("red", [128, UC, 64])
        shift = sb("shift", [TP, TP])
        tri = sb("tri", [TP, 128], BF16)
        ones = sb("ones", [TP, 128], BF16)
        rank_i = sb("rank_i", [TP, PER])
        upper = sb("upper", [TP, PER, PER])
        upper4 = sb("upper4", [TP, GROUPS, GROUPS])
        w_t = sb("w_t", [128, NCH, D])
        pos = sb("pos", [TP, WP * D])
        b_in = sb("b_in", [TP, D])
        wbc = sb("wbc", [128, 2, 2 * NST])
        wrep = sb("wrep", [128, 2, 2, 8, NST])
        wdt = sb("wdt", [128, 2, RANK])
        wdtp = sb("wdtp", [65, D])
        wrt = sb("wrt", [128, 2, NR])
        rbias = sb("rbias", [TP, NR])
        rms = sb("rms", [TP, D])
        dpar = sb("dpar", [TP, D])
        b2 = sb("b2", [NE, D])
        alog = sb("alog", [UC * DB, 128])
        abias = sb("abias", [128, UC * DB])
        cols = sb("cols", [128, 4])
        cen = sb("cen", [128, 1])
        x_in = sb("x_in", [TP, CH, PATCH * IMG])
        x_p = sb("x_p", [TP, WP, FLAT])
        w_in = x_in[:, 0, :].rearrange("p (a n) -> p a n", a=2)
        xt = sb("xt", [128, 2, NCH, TP])
        h = sb("h", [TP, WP, D])
        st6 = sb("st6", [TP, WP, 6])
        mv = sb("mv", [TP, WP, 2])
        sd = sb("sd", [TP, WP])
        rs = sb("rs", [TP, WP])
        xn = sb("xn", [TP, WP, D])
        rs2 = sb("rs2", [TP, WP])
        xs = sb("xs", [TP, WP, D])
        fs = sb("fs", [TP, WP, D])
        hs = sb("hs", [TP, WP, D])
        xnt = sb("xnt", [128, 2, QT])
        brep = sb("brep", [128, QT])
        crep = sb("crep", [128, QT])
        next_b = sb("next_b", [128, QT])
        next_c = sb("next_c", [128, QT])
        zt = sb("zt", [65, QT])
        bc = sb("bc", [TP, WP, 2 * NST])
        bcp = sb("bcp", [TP, WP, NST])
        cb = sb("cb", [TP, WP])
        ab = sb("ab", [TP, WP, D])
        ex = sb("ex", [TP, WP, D])
        lg = sb("lg", [TP, WP, D])
        w1m = sb("w1m", [TP, WP, D])
        dl = sb("dl", [TP, WP, D])
        ss = sb("ss", [TP, WP])
        th = lg
        sq = ab
        two_l = sb("two_l", [TP, WP * DB, 2, 64])
        two_u = sb("two_u", [TP, WP * DB, 2, 64])
        rd = sb("rd", [128, DB, QT], F32R)
        ru = sb("ru", [128, DB, QT], F32R)
        at = sb("at", [128, 2, QB * PAD])
        wt = sb("wt", [128, 2, QB * PAD])
        dt_ = sb("dt_", [128, 2, QB * PAD])
        s_t = sb("s_t", [128, 2, QB * PAD])
        sel_f = s_t[:].rearrange("p a n -> p (a n)")[:, 0:UC * 128].rearrange("p (c m) -> p c m", c=UC)
        cs = sb("cs", [128, 3, QT])
        yt = sb("yt", [64, DB, QT])
        h2 = hs
        row = sb("row", [TP, WP, ROWW])
        gl = sb("gl", [TP, WP, GROUPS])
        el = sb("el", [TP, WP * GROUPS, PER])
        gs = sb("gs", [TP, WP, GROUPS])
        es = sb("es", [TP, WP * GROUPS, PER])
        gp = sb("gp", [TP, WP, GROUPS])
        ep = sb("ep", [TP, WP * GROUPS, PER])
        gmx = sb("gmx", [TP, WP])
        emx = sb("emx", [TP, WP * GROUPS])
        def spare(at, n):
            return two_l[:].rearrange("p a b c -> p (a b c)")[:, at:at + n]

        gcmp = sb("gcmp", [TP, WP, GROUPS, GROUPS])
        ecmp = spare(0, 1536).rearrange("p (w i j) -> p w i j", i=PER, j=PER)
        grk = sb("grk", [TP, 2, WP, GROUPS])
        erk = spare(1536, 384).rearrange("p (a w e) -> p a w e", a=2, e=PER)
        gsel = sb("gsel", [TP, WP, GROUPS])
        esel = spare(1920, 192).rearrange("p (w e) -> p w e", e=PER)
        gz = sb("gz", [TP, WP])
        ez = sb("ez", [TP, WP * GROUPS])
        fac = sb("fac", [TP, WP, GROUPS])
        mask = sb("mask", [TP, WP + 1, NE], BF16)
        combt = xt[0:NE, 0]

        names = ("passed", "set_dve", "const_in", "pad_set", "made", "copied", "turned", "x_loaded", "x_split", "patch_t", "patch_c", "emb",
                 "emb_sum", "ln", "ln_act", "xn_done", "shifted", "xs_done", "xn_t", "xn_c", "rep_pe", "rep_act", "set_rep",
                 "z_pe", "z_act", "bc_pe", "bc_dve", "dt_pe", "soft_act", "soft", "dl_done", "rms_act",
                 "rms_dve", "gate_act", "u_done", "two", "dup_pe", "dup_hi", "dup_lo", "unit_rd", "unit_ru", "unit_a",
                 "unit_w", "unit_d", "unit_s", "unit_c", "unit_y", "y_c", "y_t", "skip_pool", "skip", "set_next", "res", "bias_a", "b2_a", "b2_b",
                 "ln2", "ln2_act", "x2_done", "x2_t", "x2_c", "log_pe", "route", "route_act", "cnt_pe",
                 "comb_t", "comb_c", "b2_pe", "stored", "quarter_done")
        s = {n: sem(n) for n in names}
        block = early.enter_context(nc.Block())
        NCONST = 19
        last_q = Q - 1
        NMADE = 24
        U = DB * UC
        ROUTE = 26
        HTS = HT // SEQ

        def tokens(ap, b=2):
            return ap.rearrange("p (s c) -> p s c", c=PAD)[:, :, 1:PAD]

        def by_block(x):
            return x[:].rearrange("p g (k c) -> p (g k) c", k=DB)

        def y_out(act, q, k):
            act.wait_ge(s["unit_y"], q * U + (k + 1) * UC)
            act.activation(yt[:, k, :].rearrange("p (b n) -> p b n", b=2), ps[0:64, 0:2, 0:HT], ACT.Copy)\
                .then_inc(s["y_c"], 1)

        def turn_tokens(pe, src, done="xn_t"):
            for g in range(WP):
                for kc, p in ((0, 128), (1, 64)):
                    last = pe.transpose(ps[0:p, 2 * kc + g // 3, (g % 3) * TP:(g % 3 + 1) * TP],
                                        src[:, g, 128 * kc:128 * kc + p], ident[0:TP, 0:TP])
            last.then_inc(s[done], 1)

        @block.sync
        def _(sp):
            n = [0]

            def load(dst, src):
                sp.dma_start(dst, src).then_inc(s["const_in"], 16)
                n[0] += 1

            img = t["x"].rearrange("(q b) c (h p) w -> q b h c (p w)", q=Q, h=HP)
            load(w_in, t["L0_tok_W"].rearrange("(a p) f -> p a f", p=96))
            load(b_in[:], t["L0_tok_b"].partition_broadcast(TP))
            load(pos[:], t["L0_tok_pos_emb"].rearrange("(h w) d -> h (w d)", h=HP).partition_broadcast(QB))
            load(wbc[:, 0, :], t["L0_attn_W_bc"][0:128, :])
            load(wbc[0:64, 1, :], t["L0_attn_W_bc"][128:D, :])
            load(wdt[:, 0, :], t["L0_attn_W_dt"][0:128, :])
            load(wdt[0:64, 1, :], t["L0_attn_W_dt"][128:D, :])
            load(rms[:], t["L0_attn_rms_scale"].partition_broadcast(TP))
            load(dpar[:], t["L0_attn_D_param"].partition_broadcast(TP))
            load(alog[:], t["L0_attn_A_log"].rearrange("(u e) n -> u (e n)", e=8))
            load(wrt[:, 0, 0:GROUPS], t["L0_ffn_Wg"][0:128, :])
            load(wrt[0:64, 1, 0:GROUPS], t["L0_ffn_Wg"][128:D, :])
            wge = t["L0_ffn_Wge"].rearrange("g d e -> d g e")
            load(wrt[:, 0, GROUPS:NR].rearrange("p (g e) -> p g e", g=GROUPS), wge[0:128])
            load(wrt[0:64, 1, GROUPS:NR].rearrange("p (g e) -> p g e", g=GROUPS), wge[128:D])
            load(rbias[:, 0:GROUPS], t["L0_ffn_bg"].partition_broadcast(TP))
            load(rbias[:, GROUPS:NR], t["L0_ffn_bge"].rearrange("g e -> (g e)").partition_broadcast(TP))
            load(b2[:], t["L0_ffn_b2"])
            sp.wait_ge(s["made"], 4)
            load(wdtp[0:RANK, :], t["L0_attn_W_dtp"])
            load(wdtp[64:65, :], t["L0_attn_b_dt"].rearrange("(a d) -> a d", a=1))
            assert n[0] == NCONST, n
            sp.dma_start(rows_dram[TOK:TOK + BLK, :], zero[:]).then_inc(s["pad_set"], 16)
            sp.dma_start(acc_dram[TOK:TOK + BLK, :], zero[:, 0:D]).then_inc(s["pad_set"], 16)

            def images(q):
                for c in range(CH):
                    src = img[q] if isinstance(q, int) else img[bass.ds(q, 1)].rearrange("a b h c n -> (a b) h c n")
                    sp.dma_start(x_in[:, c, :], src[:, :, c, :]).then_inc(s["x_loaded"], 16)

            def results(q):
                sp.wait_ge(s["route"], (q + 1) * ROUTE)
                sp.dma_start(rows_dram[bass.ds(q * QT, QT), :].rearrange("(p g) c -> p g c", p=TP), row[:])\
                    .then_inc(s["stored"], 16)
                sp.wait_ge(s["res"], (q + 1) * 4)
                sp.dma_start(acc_dram[bass.ds(q * QT, QT), :].rearrange("(p g) c -> p g c", p=TP), h2[:])\
                    .then_inc(s["stored"], 16)

            sp.wait_ge(s["turned"], NCH)
            images(0)
            sp.wait_ge(s["x_split"], CH)
            images(1)
            with sp.Fori(0, last_q) as q:
                with sp.If(q < Q - 2):
                    sp.wait_ge(s["x_split"], (q + 2) * CH)
                    sp.sem_inc(s["passed"], 1)
                    images((q + 2) & (Q - 1))
                results(q)
            results(last_q)
            sp.wait_ge(s["stored"], 32 * Q)
            sp.sem_inc(s["passed"], 1)

        @block.gpsimd
        def _(pool):
            n = [0]

            def made(ins):
                n[0] += 1
                ins.then_inc(s["made"], 1)
                pool.wait_ge(s["made"], n[0])

            def cut(ap, pattern, base, mult, op=ALU.is_ge, fill=0.0):
                made(pool.affine_select(out=ap, in_=ap, compare_op=op, fill=fill, base=base,
                                        pattern=pattern, channel_multiplier=mult))

            made(pool.memset(zero[:], 0.0))
            made(pool.memset(zt[32:64, :], 0.0))
            made(pool.memset(zt[64:65, :], 1.0))
            made(pool.memset(wdtp[:], 0.0))
            made(pool.memset(ident[:], 0.0))
            cut(ident[:], [[-1, 128]], 0, 1, ALU.not_equal, 1.0)
            made(pool.memset(sel_f, 1.0))
            for half in (0, 64):
                cut(sel_f[half:half + 64], [[128, UC], [1, 128]], 0, -16)
                cut(sel_f[half:half + 64], [[-128, UC], [-1, 128]], 15, 16)
            made(pool.memset(red[:], 1.0))
            cut(red[:], [[128, UC], [-16, 64]], 0, 1)
            cut(red[:], [[-128, UC], [16, 64]], 15, -1)
            made(pool.memset(shift[:], 0.0))
            cut(shift[:], [[-1, TP]], 1, 1, ALU.not_equal, 1.0)
            made(pool.memset(shift[:].rearrange("k (b h) -> k b h", h=HP)[:, :, 0:1], 0.0))
            pool.memset(ones[:], 1.0)
            pool.memset(mask[:], 0.0)
            made(pool.memset(tri[:], 1.0))
            cut(tri[:], [[1, 128]], -1, -1)
            made(pool.memset(upper[:], 1.0))
            cut(upper[:], [[-1, PER], [1, PER]], -1, 0)
            made(pool.memset(upper4[:], 1.0))
            cut(upper4[:], [[-1, GROUPS], [1, GROUPS]], -1, 0)
            pool.iota(rank_i[:], [[1, PER]], 0, 0, allow_small_or_imprecise_dtypes=True)
            pool.iota(iota[:], [[1, 128]], 0, 0, allow_small_or_imprecise_dtypes=True)
            pool.iota(iota_p[:], [[0, 1]], 0, 1, allow_small_or_imprecise_dtypes=True)
            pool.iota(pad_id[:], [[0, 1]], TOK + 1, 1, allow_small_or_imprecise_dtypes=True)
            pool.iota(tok_id[:], [[QT, Q], [1, WP]], 1, WP, allow_small_or_imprecise_dtypes=True)
            pool.memset(at[:], 0.0)
            pool.memset(wt[:], 0.0)
            pool.memset(dt_[:], 0.0)
            made(pool.memset(carry[:], 0.0))
            assert n[0] == NMADE, n

            def front(q, i):
                if i == 14:
                    pool.wait_ge(s["xn_done"], q + 1)
                    if not isinstance(q, int):
                        pool.wait_ge(s["set_next"], q)
                    pool.tensor_tensor(fs[:], xn[:], dpar[:].unsqueeze(1).to_broadcast([TP, WP, D]), ALU.mult)\
                        .then_inc(s["skip_pool"], 1)
                if i == 15:
                    pool.wait_ge(s["skip_pool"], q * 2 + 1)
                    pool.tensor_tensor(fs[:], fs[:], h[:], ALU.add).then_inc(s["skip_pool"], 1)

            def units(q, with_front):
                def add_shifted(i):
                    pool.wait_ge(s["unit_w"], q * U + i + 1)
                    if i >= 2:
                        pool.wait_ge(s["unit_s"], q * U + i - 1)
                    pool.tensor_tensor(dt_[:, i % 2, 1:], wt[:, i % 2, 1:], wt[:, i % 2, :-1], ALU.add)\
                        .then_inc(s["unit_d"], 1)

                for i in range(U):
                    add_shifted(i)
                    if with_front:
                        front(q + 1, i)
                pool.wait_ge(s["unit_d"], (q + 1) * U)
                pool.sem_inc(s["quarter_done"], 1)
                pool.wait_ge(s["quarter_done"], (q + 1) * 4)

            for i in range(U):
                front(0, i)
            with pool.Fori(0, last_q) as q:
                units(q, True)
            units(last_q, False)

        @block.scalar
        def _(act):
            for j in range(NCH):
                act.wait_ge(s["turned"], j + 1)
                act.activation(w_t[:, j, :], ps[:, j % 4, 0:D], ACT.Copy).then_inc(s["copied"], 1)
            act.wait_ge(s["turned"], NCH + 1)
            act.wait_ge(s["set_dve"], 1)
            act.activation(abias[:], ps[:, 7, 0:UC * DB], ACT.Identity, bias=cols[:, 0:1], scale=-0.5)\
                .then_inc(s["copied"], 1)

            def split(q):
                act.wait_ge(s["x_loaded"], (q + 1) * 16 * CH)
                if not isinstance(q, int) or q >= 1:
                    act.wait_ge(s["emb"], q * WP)
                act.sem_inc(s["passed"], 1)
                for c in range(CH):
                    act.activation(x_p[:, :, c * PATCH * PATCH:(c + 1) * PATCH * PATCH].rearrange("r g (p v) -> r p g v", p=PATCH),
                                   x_in[:, c, :].rearrange("r (p g v) -> r p g v", p=PATCH, g=WP), ACT.Copy)\
                        .then_inc(s["x_split"], 1)

            def dup_hi(q, i):
                which, k = DUPS[i]
                act.wait_ge(s["dup_pe"], q * 6 + i + 1)
                act.activation({"l": rd, "u": ru}[which][:, k, :].rearrange("p (r b g) -> p b g r", b=2, g=3),
                               ps[:, MID:MID + 2, 0:HT].rearrange("p b (g r) -> p b g r", g=3), ACT.Copy)\
                    .then_inc(s["dup_hi"], 1)

            def front(q, i):
                if i < WP:
                    act.wait_ge(s["patch_t"], q * WP + i + 1)
                    act.activation(xt[:, i % 2].rearrange("p (b j) n -> p b (j n)", b=2), ps[:, MID:MID + 2, 0:HT], ACT.Copy)\
                        .then_inc(s["patch_c"], 1)
                if i == 6:
                    act.wait_ge(s["ln"], q * 3 + 2)
                    act.activation(sd[:], mv[:, :, 1], ACT.Sqrt, bias=cols[0:TP, 1:2]).then_inc(s["ln_act"], 1)
                if i in (9, 10):
                    kc, p = ((0, 128), (1, 64))[i - 9]
                    act.wait_ge(s["xn_t"], q * 2 + kc + 1)
                    act.activation(xnt[0:p, kc, :].rearrange("p (r b g) -> p b g r", b=2, g=3),
                                   ps[0:p, MID:MID + 2, 0:HT].rearrange("p b (g r) -> p b g r", g=3), ACT.Copy)\
                        .then_inc(s["xn_c"], 1)
                if i in (11, 12):
                    j = i - 11
                    act.wait_ge(s["rep_pe"], q * 2 + j + 1)
                    act.activation((next_b, next_c)[j][:].rearrange("p (b n) -> p b n", b=2), ps[:, MID:MID + 2, 0:HT], ACT.Copy)\
                        .then_inc(s["rep_act"], 1)
                if i == 13:
                    act.wait_ge(s["z_pe"], q + 1)
                    act.activation(zt[0:RANK].rearrange("p (b n) -> p b n", b=2), ps[0:RANK, MID:MID + 2, 0:HT], ACT.Copy)\
                        .then_inc(s["z_act"], 1)
                if i in (14, 15):
                    part = dl[:, 0:4, :] if i == 14 else dl[:, 4:6, :]
                    act.wait_ge(s["dt_pe"], q * 2 + i - 13)
                    act.activation(part.rearrange("p (b g) d -> p b (g d)", g=2),
                                   ps[0:TP, MID:MID + (2 if i == 14 else 1), 0:2 * D], ACT.Copy).then_inc(s["soft_act"], 1)
                if i == 15:
                    act.wait_ge(s["soft_act"], q * 5 + 2)
                    act.activation(ab[:], dl[:], ACT.Abs).then_inc(s["soft_act"], 1)
                    act.wait_ge(s["soft_act"], q * 5 + 3)
                    act.activation(ex[:], ab[:], ACT.Exp, scale=-1.0).then_inc(s["soft_act"], 1)
                if i == 16:
                    act.wait_ge(s["soft_act"], q * 5 + 4)
                    act.activation(lg[:], ex[:], ACT.Ln, bias=1.0).then_inc(s["soft_act"], 1)
                if i == 17:
                    act.wait_ge(s["dl_done"], q * 2 + 2)
                    for g in range(WP):
                        last = act.activation(sq[:, g, :], dl[:, g, :], ACT.Square, accum_out=ss[:, g:g + 1])
                    last.then_inc(s["rms_act"], 1)
                    act.wait_ge(s["rms_act"], q * 2 + 1)
                    act.activation(rs2[:], ss[:], ACT.Sqrt, scale=1.0 / D, bias=cols[0:TP, 2:3]).then_inc(s["rms_act"], 1)
                if i == 18:
                    act.wait_ge(s["rms_dve"], q * 2 + 2)
                    act.activation(th[:], w1m[:], ACT.Tanh, scale=1.0 / HALF, bias=cols[0:TP, 3:4]).then_inc(s["gate_act"], 1)
                if i == 19:
                    act.wait_ge(s["gate_act"], q * 3 + 1)
                    act.activation(two_l[:], by_block(th).unsqueeze(2).to_broadcast(twice), ACT.Ln,
                                   scale=HALF, bias=cen[0:TP, :]).then_inc(s["gate_act"], 1)
                    act.activation(sq[:], th[:], ACT.Sqrt, scale=HALF, bias=cen[0:TP, :]).then_inc(s["gate_act"], 1)
                if i == 20:
                    dup_hi(q, 0)
                if i == 21:
                    dup_hi(q, 1)
                    act.wait_ge(s["u_done"], q + 1)
                    act.activation(two_u[:], by_block(ex).unsqueeze(2).to_broadcast(twice), ACT.Copy).then_inc(s["two"], 1)
                if i == 22:
                    dup_hi(q, 2)
                if i == 23:
                    dup_hi(q, 3)

            def behind(q):
                dup_hi(q, 4)
                act.wait_ge(s["rep_act"], q * 2 + 2)
                if not isinstance(q, int):
                    act.wait_ge(s["unit_c"], q * U)
                act.activation(brep[:], next_b[:], ACT.Copy).then_inc(s["set_rep"], 1)
                act.activation(crep[:], next_c[:], ACT.Copy).then_inc(s["set_rep"], 1)
                dup_hi(q, 5)

            def units(q, with_front):
                decay(q, 0)
                for i in range(U):
                    if i + 1 < U:
                        decay(q, i + 1)
                    if i % UC == 1 and i > UC:
                        y_out(act, q, i // UC - 1)
                    if with_front:
                        front(q + 1, i)
                    if i == 6:
                        with act.If(q > 0):
                            weights_out(q - 1)
                    if i == 12:
                        with act.If(q > 0):
                            act.wait_ge(s["stored"], q * 32)
                            act.sem_inc(s["passed"], 1)
                        act.wait_ge(s["skip"], q + 1)
                        act.activation(hs[:], fs[:], ACT.Copy).then_inc(s["set_next"], 1)
                y_out(act, q, DB - 1)
                if with_front:
                    behind(q + 1)

            def weights_out(q):
                act.wait_ge(s["comb_t"], q + 1)
                act.activation(combt[:].rearrange("e (b g) r -> e b (g r)", b=2), ps[0:NE, MID:MID + 2, 0:HT], ACT.Copy)\
                    .then_inc(s["comb_c"], 1)

            def decay(q, i):
                act.wait_ge(s["unit_rd"], q * U + i + 1)
                if i >= 2:
                    act.wait_ge(s["unit_s"], q * U + i - 1)
                act.activation(tokens(at[:, i % 2]).rearrange("p (b s) c -> p b s c", b=2),
                               ps[:, 4:6, 0:HT].rearrange("p b (s c) -> p b s c", c=SEQ), ACT.Tanh,
                               scale=-0.5, bias=abias[:, i:i + 1]).then_inc(s["unit_a"], 1)

            def back(q):
                act.wait_ge(s["ln2"], q * 3 + 2)
                act.activation(sd[:], mv[:, :, 1], ACT.Sqrt, bias=cols[0:TP, 1:2]).then_inc(s["ln2_act"], 1)
                act.wait_ge(s["x2_t"], q + 1)
                for kc, p in ((0, 128), (1, 64)):
                    last = act.activation(xnt[0:p, kc, :].rearrange("p (b n) -> p b n", b=2),
                                          ps[0:p, 2 * kc:2 * kc + 2, 0:HT], ACT.Copy)
                last.then_inc(s["x2_c"], 1)
                act.wait_ge(s["route"], q * ROUTE + 6)
                act.activation(gp[:], gs[:], ACT.Exp)
                act.activation(ep[:], es[:], ACT.Exp).then_inc(s["route_act"], 1)
                act.wait_ge(s["route_act"], q + 1)
                act.sem_inc(s["quarter_done"], 1)

            twice = [TP, WP * DB, 2, 64]
            split(0)
            for i in range(U):
                front(0, i)
                if i == 16:
                    split(1)
            behind(0)
            with act.Fori(0, last_q) as q:
                units(q, True)
                with act.If(q < Q - 2):
                    split(q + 2)
                back(q)
                act.wait_ge(s["quarter_done"], (q + 1) * 4)
            units(last_q, False)
            back(last_q)
            act.wait_ge(s["quarter_done"], Q * 4)
            weights_out(last_q)

        @block.tensor
        def _(pe):
            pe.wait_ge(s["const_in"], 16 * (NCONST))
            pe.wait_ge(s["made"], NMADE)
            for j in range(NCH):
                if j >= 4:
                    pe.wait_ge(s["copied"], j - 3)
                for a in range(2):
                    last = pe.transpose(ps[:, j % 4, a * 96:a * 96 + 96], w_in[:, a, j * 128:(j + 1) * 128], ident[0:96, 0:96])
                last.then_inc(s["turned"], 1)
            pe.transpose(ps[:, 7, 0:UC * DB], alog[:], ident[0:UC * DB, 0:UC * DB]).then_inc(s["turned"], 1)
            pe.wait_ge(s["copied"], NCH + 1)
            pe.wait_ge(s["set_dve"], 5)

            def dup(q, i):
                which, k = DUPS[i]
                if i == 0:
                    pe.wait_ge(s["gate_act"], q * 3 + 2)
                    pe.wait_ge(s["bc_dve"], q * 3 + 1)
                    pe.wait_ge(s["soft_act"], q * 5 + 2)
                    pe.sem_inc(s["passed"], 1)
                if i == 2:
                    pe.wait_ge(s["two"], q + 1)
                if i > 0:
                    pe.wait_ge(s["dup_lo"], q * 6 + i)
                for g in range(WP):
                    last = pe.transpose(ps[:, MID + g // 3, (g % 3) * TP:(g % 3 + 1) * TP],
                                        {"l": two_l, "u": two_u}[which][:, g * DB + k].rearrange("p a c -> p (a c)"), ident[0:TP, 0:TP])
                last.then_inc(s["dup_pe"], 1)

            def embed(q, g):
                pe.wait_ge(s["patch_c"], q * WP + g + 1)
                for j in range(NCH):
                    last = pe.matmul(ps[0:TP, MID, 0:D], xt[:, g % 2, j, :], w_t[:, j, :], start=(j == 0), stop=(j == NCH - 1))
                last.then_inc(s["emb"], 1)

            def front(q, i):
                if i == 0:
                    pe.wait_ge(s["x_split"], (q + 1) * CH)
                if 1 <= i <= WP:
                    pe.wait_ge(s["emb_sum"], q * WP + i)
                if i < WP:
                    for j in range(NCH):
                        last = pe.transpose(ps[:, MID + j // 3, (j % 3) * TP:(j % 3 + 1) * TP],
                                            x_p[:, i, j * 128:(j + 1) * 128], ident[0:TP, 0:TP])
                    last.then_inc(s["patch_t"], 1)
                if i == 8:
                    pe.wait_ge(s["xn_done"], q + 1)
                    pe.matmul(ps[0:TP, MID, 0:D], shift[:], xn[:, WP - 1, :], start=True, stop=True, skip_group_check=True)\
                        .then_inc(s["shifted"], 1)
                if i in (9, 10):
                    kc, p = ((0, 128), (1, 64))[i - 9]
                    if kc == 0:
                        pe.wait_ge(s["xs_done"], q + 1)
                    else:
                        pe.wait_ge(s["xn_c"], q * 2 + 1)
                    pe.sem_inc(s["passed"], 1)
                    for g in range(WP):
                        last = pe.transpose(ps[0:p, MID + g // 3, (g % 3) * TP:(g % 3 + 1) * TP],
                                            xn[:, g, 128 * kc:128 * kc + p], ident[0:TP, 0:TP])
                    last.then_inc(s["xn_t"], 1)
                if i in (11, 12):
                    j = i - 11
                    if j == 0:
                        pe.wait_ge(s["xn_c"], q * 2 + 2)
                    else:
                        pe.wait_ge(s["rep_act"], q * 2 + 1)
                    for b in range(2):
                        for kc, p in ((0, 128), (1, 64)):
                            last = pe.matmul(ps[:, MID + b, 0:HT], wrep[0:p, kc, j].rearrange("p a n -> p (a n)"),
                                             xnt[0:p, kc, b * HT:(b + 1) * HT], start=(kc == 0), stop=(kc == 1))
                    last.then_inc(s["rep_pe"], 1)
                if i == 13:
                    pe.wait_ge(s["rep_act"], q * 2 + 2)
                    for b in range(2):
                        for kc, p in ((0, 128), (1, 64)):
                            last = pe.matmul(ps[0:RANK, MID + b, 0:HT], wdt[0:p, kc, :], xnt[0:p, kc, b * HT:(b + 1) * HT],
                                             start=(kc == 0), stop=(kc == 1))
                    last.then_inc(s["z_pe"], 1)
                if i in (14, 15):
                    if i == 14:
                        pe.wait_ge(s["z_act"], q + 1)
                    else:
                        pe.wait_ge(s["soft_act"], q * 5 + 1)
                    for g in (range(0, 4) if i == 14 else range(4, WP)):
                        last = pe.matmul(ps[0:TP, MID + g % 4 // 2, (g % 2) * D:(g % 2 + 1) * D],
                                         zt[:].rearrange("p (r g) -> p g r", g=WP)[:, g, :], wdtp[:], start=True, stop=True)
                    last.then_inc(s["dt_pe"], 1)
                if i == 15:
                    for g in range(WP):
                        for kc, p in ((0, 128), (1, 64)):
                            last = pe.matmul(ps[0:TP, MID + 1, g * 32:g * 32 + 32],
                                             xnt[0:p, kc, :].rearrange("p (r g) -> p g r", g=WP)[:, g, :],
                                             wbc[0:p, kc, :], start=(kc == 0), stop=(kc == 1), skip_group_check=True)
                    last.then_inc(s["bc_pe"], 1)
                if i >= 20:
                    dup(q, i - 20)

            def behind(q):
                dup(q, 4)
                dup(q, 5)

            def units(q, with_front):
                def spread(i):
                    k, c = divmod(i, UC)
                    for src, bank, free, done in ((ru, 6, "unit_w", "unit_ru"), (rd, 4, "unit_a", "unit_rd")):
                        if i >= 1:
                            pe.wait_ge(s[free], q * U + i)
                        for b in range(2):
                            last = pe.matmul(ps[:, bank + b, 0:HT], sel[:, c, :], src[:, k, b * HT:(b + 1) * HT], start=True, stop=True)
                        last.then_inc(s[done], 1)

                def gather_y(i):
                    k, c = divmod(i, UC)
                    pe.wait_ge(s["unit_c"], q * U + i + 1)
                    if c == 0 and k >= 1:
                        pe.wait_ge(s["y_c"], q * DB + k)
                    for b in range(2):
                        last = pe.matmul(ps[0:64, b, 0:HT], red[:, c, :], cs[:, i % 3, b * HT:(b + 1) * HT],
                                         start=(c == 0), stop=(c == UC - 1), skip_group_check=True)
                    last.then_inc(s["unit_y"], 1)

                pe.wait_ge(s["dup_lo"], (q + 1) * 6)
                spread(0)
                for i in range(U):
                    if i + 1 < U:
                        spread(i + 1)
                    if 8 <= i <= 9:
                        with pe.If(q > 0):
                            if i == 8:
                                bias(q - 1, 2)
                            else:
                                pe.wait_ge(s["res"], q * 4)
                                pe.sem_inc(s["passed"], 1)
                    if with_front:
                        front(q + 1, i)
                    if i >= 2:
                        gather_y(i - 2)
                    if with_front and i < WP:
                        embed(q + 1, i)
                    if 6 <= i <= 7:
                        with pe.If(q > 0):
                            bias(q - 1, i - 6)
                gather_y(U - 2)
                gather_y(U - 1)

            def bias(q, part):
                if part == 0:
                    for g in range(WP):
                        last = pe.transpose(ps[0:NE, MID + g // 3, (g % 3) * TP:(g % 3 + 1) * TP], row[:, g, D:ROWW], ident[0:TP, 0:TP])
                    last.then_inc(s["comb_t"], 1)
                else:
                    if part == 1:
                        pe.wait_ge(s["comb_c"], q + 1)
                    else:
                        pe.wait_ge(s["bias_a"], q + 1)
                    for g in (range(0, 4) if part == 1 else range(4, WP)):
                        bank = MID + g // 2 if part == 1 else MID + 1
                        last = pe.matmul(ps[0:TP, bank, (g % 2) * D:(g % 2 + 1) * D], combt[:, g, :], b2[:], start=True, stop=True)
                    last.then_inc(s[("b2_a", "b2_b")[part - 1]], 1)

            def back(q, with_front):
                pe.wait_ge(s["y_c"], (q + 1) * DB)
                pe.wait_ge(s["unit_w"], (q + 1) * U)
                pe.wait_ge(s["unit_a"], (q + 1) * U)
                pe.sem_inc(s["passed"], 1)
                for g in range(WP):
                    for k in range(DB):
                        last = pe.transpose(ps[0:TP, 4 + g // 2, (g % 2) * D + 64 * k:(g % 2) * D + 64 * k + 64],
                                            yt[:, k, :].rearrange("p (r g) -> p g r", g=WP)[:, g, :], ident[0:64, 0:64])
                last.then_inc(s["y_t"], 1)
                if with_front:
                    behind(q + 1)
                pe.wait_ge(s["x2_done"], q + 1)
                if with_front:
                    pe.wait_ge(s["dup_lo"], (q + 2) * 6)
                turn_tokens(pe, row, "x2_t")
                pe.wait_ge(s["x2_c"], q + 1)
                for g in range(WP):
                    for kc, p in ((0, 128), (1, 64)):
                        last = pe.matmul(ps[0:TP, 7, g * NR:(g + 1) * NR], xnt[0:p, kc, g * TP:(g + 1) * TP], wrt[0:p, kc, :],
                                         start=(kc == 0), stop=(kc == 1), skip_group_check=True)
                last.then_inc(s["log_pe"], 1)
                pe.wait_ge(s["route"], q * ROUTE + ROUTE - 2)
                pe.matmul(ps[:, 2, 0:(WP + 1) * NE], tri[:], mask[:].rearrange("p g e -> p (g e)"), start=True, stop=False,
                          skip_group_check=True)
                for g in range(WP):
                    last = pe.matmul(ps[:, 2, (g + 1) * NE:(WP + 1) * NE], ones[:],
                                     mask[:, g, :].unsqueeze(1).to_broadcast([TP, WP - g, NE]), start=False, stop=(g == WP - 1),
                                     skip_group_check=True)
                last.then_inc(s["cnt_pe"], 1)
                pe.wait_ge(s["cnt_pe"], q + 1)
                pe.sem_inc(s["quarter_done"], 1)
                pe.wait_ge(s["quarter_done"], (q + 1) * 4)

            for i in range(U):
                front(0, i)
                if i < WP:
                    embed(0, i)
            behind(0)
            with pe.Fori(0, last_q) as q:
                units(q, True)
                back(q, True)
            units(last_q, False)
            back(last_q, False)
            for part in range(3):
                bias(last_q, part)

        @block.vector
        def _(dve):
            n = [0]

            def setup(ins):
                n[0] += 1
                ins.then_inc(s["set_dve"], 1)

            dve.memset(cols[:, 0:1], 0.5 * LN2)
            dve.memset(cols[:, 1:2], 1e-5)
            dve.memset(cols[:, 2:3], 1e-6)
            dve.memset(cen[:], CEN)
            setup(dve.memset(cols[:, 3:4], -CEN / HALF))
            dve.wait_ge(s["made"], NMADE)
            dve.wait_ge(s["const_in"], 16 * (NCONST))
            setup(dve.tensor_copy(sel[:], sel_f))
            for j in range(2):
                for kc, p in ((0, 128), (1, 64)):
                    last = dve.tensor_copy(wrep[0:p, kc, j], wbc[0:p, kc, j * NST:(j + 1) * NST].unsqueeze(1).to_broadcast([p, 8, NST]))
            setup(last)
            setup(dve.tensor_tensor(pos[:].rearrange("p (g d) -> p g d", d=D), pos[:].rearrange("p (g d) -> p g d", d=D),
                                    b_in[:].unsqueeze(1).to_broadcast([TP, WP, D]), ALU.add))
            dve.wait_ge(s["set_dve"], 4)
            setup(dve.memset(cs[:, :, 0:1], 0.0))

            def moments(q, src, steps):
                for g in range(WP):
                    last = dve.bn_stats(st6[:, g, :], src[:, g, :])
                last.then_inc(s[steps], 1)
                dve.wait_ge(s[steps], q * 3 + 1)
                dve.sem_inc(s["passed"], 1)
                for g in range(WP):
                    last = dve.bn_aggr(mv[:, g, :], st6[:, g, :])
                last.then_inc(s[steps], 1)

            def norm(q, src, dst, steps, roots, done):
                dve.wait_ge(s[roots], q + 1)
                dve.reciprocal(rs[:], sd[:]).then_inc(s[steps], 1)
                dve.wait_ge(s[steps], q * 3 + 3)
                for g in range(WP):
                    last = dve.tensor_scalar(dst[:, g, 0:D], src[:, g, :], mv[:, g, 0:1], rs[:, g:g + 1], ALU.subtract, ALU.mult)
                last.then_inc(s[done], 1)

            def dup_lo(q, i):
                which, k = DUPS[i]
                dve.wait_ge(s["dup_hi"], q * 6 + i + 1)
                part = {"l": rd, "u": ru}[which][64:128, k, :].rearrange("p (r b g) -> p b g r", b=2, g=3)
                dve.tensor_tensor(part, ps[64:128, MID:MID + 2, 0:HT].rearrange("p b (g r) -> p b g r", g=3), part.bitcast(F32),
                                  ALU.subtract).then_inc(s["dup_lo"], 1)

            def front(q, i):
                if i < WP:
                    dve.wait_ge(s["emb"], q * WP + i + 1)
                    dve.tensor_tensor(h[:, i, :], ps[0:TP, MID, 0:D], pos[:, i * D:(i + 1) * D], ALU.add).then_inc(s["emb_sum"], 1)
                if i == 6:
                    dve.wait_ge(s["emb_sum"], (q + 1) * WP)
                    moments(q, h, "ln")
                if i == 7:
                    norm(q, h, xn, "ln", "ln_act", "xn_done")
                if i == 8:
                    dve.wait_ge(s["xn_done"], q + 1)
                    dve.tensor_tensor(xs[:, 1:, :], xn[:, 1:, :], xn[:, :-1, :], ALU.add)
                    dve.wait_ge(s["shifted"], q + 1)
                    dve.tensor_tensor(xs[:, 0, :], ps[0:TP, MID, 0:D], xn[:, 0, :], ALU.add).then_inc(s["xs_done"], 1)
                if i == 16:
                    dve.wait_ge(s["soft_act"], q * 5 + 4)
                    dve.tensor_scalar(w1m[:], ex[:], 1.0, -1.0, ALU.add, ALU.add).then_inc(s["soft"], 1)
                    dve.wait_ge(s["soft"], q * 2 + 1)
                    dve.tensor_tensor(ab[:], w1m[:], ex[:], ALU.subtract).then_inc(s["soft"], 1)
                if i == 15:
                    dve.wait_ge(s["bc_pe"], q + 1)
                    dve.tensor_copy(bc[:], ps[0:TP, MID + 1, 0:WP * 32].rearrange("p (g n) -> p g n", g=WP)).then_inc(s["bc_dve"], 1)
                    dve.wait_ge(s["bc_dve"], q * 3 + 1)
                    dve.tensor_tensor(bcp[:], bc[:, :, 0:NST], bc[:, :, NST:2 * NST], ALU.mult).then_inc(s["bc_dve"], 1)
                    dve.wait_ge(s["bc_dve"], q * 3 + 2)
                    dve.tensor_reduce(cb[:], bcp[:], AX_X, ALU.add).then_inc(s["bc_dve"], 1)
                if i == 17:
                    dve.wait_ge(s["soft_act"], q * 5 + 5)
                    dve.scalar_tensor_tensor(out=dl[:], in0=dl[:], scalar=0.0, in1=lg[:], op0=ALU.max, op1=ALU.add)\
                        .then_inc(s["dl_done"], 1)
                    dve.wait_ge(s["soft"], q * 2 + 2)
                    dve.wait_ge(s["dl_done"], q * 2 + 1)
                    dve.tensor_tensor(dl[:], dl[:], ab[:], ALU.subtract).then_inc(s["dl_done"], 1)
                if i == 18:
                    dve.wait_ge(s["rms_act"], q * 2 + 2)
                    dve.reciprocal(rs[:], rs2[:]).then_inc(s["rms_dve"], 1)
                    dve.wait_ge(s["rms_dve"], q * 2 + 1)
                    for g in range(WP):
                        last = dve.scalar_tensor_tensor(out=w1m[:, g, :], in0=dl[:, g, :], scalar=rs[:, g:g + 1], in1=rms[:],
                                                        op0=ALU.mult, op1=ALU.mult)
                    last.then_inc(s["rms_dve"], 1)
                if i == 20:
                    dup_lo(q, 0)
                    dve.wait_ge(s["gate_act"], q * 3 + 3)
                    dve.wait_ge(s["xs_done"], q + 1)
                    dve.scalar_tensor_tensor(out=ex[:], in0=sq[:], scalar=0.25, in1=xs[:], op0=ALU.mult, op1=ALU.mult)\
                        .then_inc(s["u_done"], 1)
                if i == 21:
                    dup_lo(q, 1)
                if i == 22:
                    dup_lo(q, 2)
                    dve.wait_ge(s["u_done"], q + 1)
                    dve.wait_ge(s["skip_pool"], q * 2 + 2)
                    dve.sem_inc(s["passed"], 1)
                    for g in range(WP):
                        last = dve.scalar_tensor_tensor(out=fs[:, g, :], in0=ex[:, g, :], scalar=cb[:, g:g + 1], in1=fs[:, g, :],
                                                        op0=ALU.mult, op1=ALU.add)
                    last.then_inc(s["skip"], 1)
                if i == 23:
                    dup_lo(q, 3)

            def behind(q):
                dup_lo(q, 4)
                dup_lo(q, 5)

            def units(q, with_front):
                def inputs(i):
                    dve.wait_ge(s["unit_ru"], q * U + i + 1)
                    if i >= 2:
                        dve.wait_ge(s["unit_d"], q * U + i - 1)
                    dve.tensor_tensor(tokens(wt[:, i % 2]).rearrange("p (b s) c -> p b s c", b=2),
                                      ps[:, 6:8, 0:HT].rearrange("p b (s c) -> p b s c", c=SEQ),
                                      brep[:].rearrange("p (b s c) -> p b s c", b=2, c=SEQ), ALU.mult).then_inc(s["unit_w"], 1)

                def outputs(i):
                    dve.wait_ge(s["unit_s"], q * U + i + 1)
                    if i >= 3:
                        dve.wait_ge(s["unit_y"], q * U + i - 2)
                    dve.tensor_tensor(cs[:, i % 3, :].rearrange("p (s c) -> p s c", c=SEQ), tokens(s_t[:, i % 2]),
                                      crep[:].rearrange("p (s c) -> p s c", c=SEQ), ALU.mult).then_inc(s["unit_c"], 1)

                dve.wait_ge(s["set_rep"], (q + 1) * 2)
                inputs(0)
                for i in range(U):
                    if i + 1 < U:
                        inputs(i + 1)
                    if i >= 1:
                        outputs(i - 1)
                    dve.wait_ge(s["unit_d"], q * U + i + 1)
                    dve.wait_ge(s["unit_a"], q * U + i + 1)
                    dve.tensor_tensor_scan(s_t[:, i % 2, :], dt_[:, i % 2, :], at[:, i % 2, :], 0.0, ALU.add, ALU.mult)\
                        .then_inc(s["unit_s"], 1)
                    if with_front:
                        front(q + 1, i)
                    if i in (7, 8):
                        with dve.If(q > 0):
                            bias(q - 1, i - 7)
                outputs(U - 1)

            def bias(q, part):
                dve.wait_ge(s[("b2_a", "b2_b")[part]], q + 1)
                g, b, n_ = ((0, MID, 2), (4, MID + 1, 1))[part]
                mine = h2[:, g:g + 2 * n_, :].rearrange("p (b g) d -> p b (g d)", g=2)
                dve.tensor_tensor(mine, ps[0:TP, b:b + n_, 0:2 * D], mine, ALU.add).then_inc(s[("bias_a", "res")[part]], 1)

            def back(q, with_front):
                dve.wait_ge(s["set_next"], q + 1)
                dve.wait_ge(s["y_t"], q + 1)
                dve.sem_inc(s["passed"], 1)
                pair = "p (g d) -> p g d"
                for j in range(3):
                    dve.tensor_tensor(h2[:, 2 * j:2 * j + 2, :], ps[0:TP, 4 + j, 0:2 * D].rearrange(pair, g=2),
                                      h2[:, 2 * j:2 * j + 2, :], ALU.add).then_inc(s["res"], 1)
                if with_front:
                    dup_lo(q + 1, 4)
                dve.wait_ge(s["res"], q * 4 + 3)
                moments(q, h2, "ln2")
                if with_front:
                    dup_lo(q + 1, 5)
                norm(q, h2, row, "ln2", "ln2_act", "x2_done")
                m = [0]

                def link(ins):
                    m[0] += 1
                    ins.then_inc(s["route"], 1)
                    dve.wait_ge(s["route"], q * ROUTE + m[0])

                WG = WP * GROUPS
                dve.wait_ge(s["log_pe"], q + 1)
                logits = ps[0:TP, 7, 0:WP * NR].rearrange("p (g n) -> p g n", g=WP)
                link(dve.tensor_tensor(gl[:], logits[:, :, 0:GROUPS], rbias[:, 0:GROUPS].unsqueeze(1).to_broadcast([TP, WP, GROUPS]), ALU.add))
                link(dve.tensor_tensor(el[:].rearrange("p (w g) e -> p w (g e)", g=GROUPS), logits[:, :, GROUPS:NR],
                                       rbias[:, GROUPS:NR].unsqueeze(1).to_broadcast([TP, WP, NE]), ALU.add))
                link(dve.tensor_reduce(gmx[:], gl[:], AX_X, ALU.max))
                link(dve.tensor_reduce(emx[:], el[:], AX_X, ALU.max))
                link(dve.tensor_tensor(gs[:], gl[:], gmx[:].unsqueeze(2).to_broadcast([TP, WP, GROUPS]), ALU.subtract))
                link(dve.tensor_tensor(es[:], el[:], emx[:].unsqueeze(2).to_broadcast([TP, WG, PER]), ALU.subtract))
                for x, cmp, up, rk, selx, w, n_ in ((gl, gcmp[:], upper4, grk, gsel, WP, GROUPS), (el, ecmp, upper, erk, esel, WG, PER)):
                    big = [TP, w, n_, n_]
                    link(dve.tensor_tensor(cmp, x[:].unsqueeze(2).to_broadcast(big), x[:].unsqueeze(3).to_broadcast(big), ALU.is_gt))
                    link(dve.tensor_tensor(cmp.rearrange("p w i j -> p w (i j)"), cmp.rearrange("p w i j -> p w (i j)"),
                                           up[:].rearrange("p i j -> p (i j)").unsqueeze(1).to_broadcast([TP, w, n_ * n_]), ALU.mult))
                    dve.tensor_reduce(rk[:, 0], cmp, AX_X, ALU.add)
                    link(dve.tensor_reduce(rk[:, 1], cmp.rearrange("p w i j -> p w j i"), AX_X, ALU.add))
                    link(dve.tensor_tensor(rk[:, 0], rk[:, 0], rk[:, 1], ALU.subtract))
                    link(dve.tensor_tensor(rk[:, 0], rk[:, 0], rank_i[:, 0:n_].unsqueeze(1).to_broadcast([TP, w, n_]), ALU.add))
                    link(dve.tensor_scalar(selx[:], rk[:, 0], 2.0, None, ALU.is_lt))
                dve.wait_ge(s["route_act"], q + 1)
                dve.tensor_tensor(gp[:], gp[:], gsel[:], ALU.mult)
                link(dve.tensor_tensor(ep[:], ep[:], esel[:], ALU.mult))
                dve.tensor_reduce(gz[:], gp[:], AX_X, ALU.add)
                link(dve.tensor_reduce(ez[:], ep[:], AX_X, ALU.add))
                dve.reciprocal(gz[:], gz[:])
                link(dve.reciprocal(ez[:], ez[:]))
                link(dve.tensor_tensor(fac[:], gp[:], gz[:].unsqueeze(2).to_broadcast([TP, WP, GROUPS]), ALU.mult))
                fac24 = fac[:].rearrange("p w g -> p (w g)")
                link(dve.tensor_tensor(fac24, fac24, ez[:], ALU.mult))
                chosen = maskf[:, bass.ds(q * WP, WP), :]
                dve.tensor_tensor(row[:, :, D:ROWW].rearrange("p w (g e) -> p w g e", g=GROUPS), ep[:].rearrange("p (w g) e -> p w g e", g=GROUPS),
                                  fac[:].unsqueeze(3).to_broadcast([TP, WP, GROUPS, PER]), ALU.mult)
                dve.tensor_tensor(chosen.rearrange("p w (g e) -> p (w g) e", g=GROUPS), esel[:],
                                  gsel[:].rearrange("p w g -> p (w g)").unsqueeze(2).to_broadcast([TP, WG, PER]), ALU.mult)
                link(dve.tensor_tensor(mask[:, 0:WP, :].rearrange("p w (g e) -> p (w g) e", g=GROUPS), esel[:],
                                       gsel[:].rearrange("p w g -> p (w g)").unsqueeze(2).to_broadcast([TP, WG, PER]), ALU.mult))
                assert m[0] == ROUTE - 2, m
                dve.wait_ge(s["cnt_pe"], q + 1)
                link(dve.tensor_tensor(rank[:, bass.ds(q * WP, WP), :], ps[0:TP, 2, 0:WP * NE].rearrange("p (w e) -> p w e", w=WP),
                                       carry[0:TP].unsqueeze(1).to_broadcast([TP, WP, NE]), ALU.add))
                link(dve.tensor_tensor(carry[:], carry[:], ps[:, 2, WP * NE:(WP + 1) * NE], ALU.add))
                dve.sem_inc(s["quarter_done"], 1)
                dve.wait_ge(s["quarter_done"], (q + 1) * 4)

            for i in range(U):
                front(0, i)
            behind(0)
            with dve.Fori(0, last_q) as q:
                units(q, True)
                back(q, True)
            units(last_q, False)
            back(last_q, False)
            for part in range(2):
                bias(last_q, part)

        early.close()
        def lb(name, shape, dt=F32):
            return ctx.enter_context(nc.sbuf_tensor(name, shape, dt))

        NG = Q * WP
        cnt_i = lb("cnt_i", [128, NE], I32)
        nblk_i = lb("nblk_i", [128, NE], I32)
        nblk = lb("nblk", [128, NE])
        endb = lb("endb", [128, NE])
        first = lb("first", [128, NE])
        key = lb("key", [TP, NG, NE])
        top = lb("top", [TP, NG, 8])
        slot_i = lb("slot_i", [TP, NG, TOPK], I32)
        at_i = lb("at_i", [TP, 2, NG * TOPK], I32)
        at_f = lb("at_f", [TP, 2, NG * TOPK])
        is_row = lb("is_row", [TP, 8, BLK], F32R)
        is_blk = lb("is_blk", [TP, 8, NBLK], F32R)
        passed_e = lb("passed_e", [128, NE])
        e_col = lb("e_col", [128, 1])
        e_tab = lb("e_tab", [1, 128], I32)
        ring_tab = lb("ring_tab", [1, 128], I32)
        end_tab = lb("end_tab", [1, NE], I32)
        groups_tab = lb("groups_tab", [1, 1], I32)
        empty = lb("empty", [128, NBLK])
        ix = lb("ix", [128, NBLK + SETR], I32)
        ixg = lb("ixg", [128, SETR], I32)
        ixs = lb("ixs", [128, SETR], I32)
        xg = lb("xg", [128, SETR, ROWW])
        xa = lb("xa", [128, 2, BLK])
        xb = lb("xb", [65, 2, BLK])
        w1a = lb("w1a", [128, WRING, M])
        w1b = lb("w1b", [65, WRING, M])
        w2 = lb("w2", [128, WRING, MC, D])
        ht = lb("ht", [128, 2, M])
        ys = lb("ys", [128, 2, D])
        for n_ in ("tab", "oh", "oh_used", "e_t", "ready", "gathered0", "gathered1", "gathered2", "gathered3", "col",
                   "added", "x_t", "x_e", "h_pe", "h_act", "y_pe", "y_dve",
                   "w_in0", "w_in1", "w_in2", "w_in3", "w_ready", "out_done", "b1_one"):
            s[n_] = sem("p2_" + n_)
        gathered = [s[f"gathered{j}"] for j in range(SETR)]
        w_in_ = [s[f"w_in{j}"] for j in range(WRING)]
        MH = M // 2
        block2 = ctx.enter_context(nc.Block())

        def used(eng):
            return eng.value_load(groups_tab[0:1, 0:1], min_val=NE // SETR - 1, max_val=NBLK // SETR - 1)

        @block2.sync
        def _(sp):
            def load_expert(e, j):
                one = (lambda ap: ap[e]) if isinstance(e, int) else (lambda ap: ap[bass.ds(e, 1)][0])
                w1, w2_, b1 = one(t["L0_ffn_W1"]), one(t["L0_ffn_W2"]), one(t["L0_ffn_b1"])
                sp.dma_start(w1a[:, j, :], w1[0:128, :]).then_inc(w_in_[j], 16)
                sp.dma_start(w1b[0:64, j, :], w1[128:D, :]).then_inc(w_in_[j], 16)
                sp.dma_start(w1b[64:65, j, :], b1.rearrange("(a m) -> a m", a=1)).then_inc(w_in_[j], 16)
                sp.dma_start(w2[:, j, :, :], w2_.rearrange("(c p) d -> p c d", p=128)).then_inc(w_in_[j], 16)

            for e in range(WRING):
                load_expert(e, e)
                if e >= 1:
                    sp.wait_ge(w_in_[e - 1], 64)
                    sp.sem_inc(s["w_ready"], 1)
            sp.wait_ge(s["ready"], 1)
            with sp.Fori(1, NE // WRING) as r:
                for j in range(WRING):
                    end = sp.value_load(end_tab[0:1, bass.ds((r - 1) * WRING + j, 1)], min_val=1, max_val=NBLK)
                    sp.wait_ge(s["y_pe"], end)
                    load_expert(r * WRING + j, j)
                    sp.wait_ge(w_in_[(j - 1) % WRING], 64 * r if j == 0 else 64 * (r + 1))
                    sp.sem_inc(s["w_ready"], 1)
            sp.wait_ge(w_in_[WRING - 1], 64 * (NE // WRING))
            sp.sem_inc(s["w_ready"], 1)
            sp.wait_ge(s["added"], used(sp) * (SETR * 16) + SETR * 16)
            sp.sem_inc(s["passed"], 1)
            sp.dma_start(out.rearrange("b s d -> (b s) d"), acc_dram[0:TOK, :]).then_inc(s["out_done"], 16)
            sp.wait_ge(s["out_done"], 16)

        @block2.gpsimd
        def _(pool):
            def column(ring, t_, j):
                pool.tensor_copy(ring[:, j:j + 1], ix[:, bass.ds(t_, 1)]).then_inc(s["col"], 1)

            def gather(t_, j, cols):
                column(ixg, t_, j)
                pool.wait_ge(s["col"], cols)
                pool.sem_inc(s["passed"], 1)
                pool.indirect_dma_start(xg[:, j, :], None, rows_dram, bass.IndirectOffsetOnAxis(ixg[:, j:j + 1], 0))\
                    .then_inc(gathered[j], 16)

            pool.wait_ge(s["ready"], 1)
            for j in range(SETR):
                gather(j, j, j + 1)
            groups = used(pool)
            with pool.Fori(0, NBLK // SETR) as r, pool.If(r <= groups):
                for j in range(SETR):
                    if j > 0:
                        pool.wait_ge(s["added"], (r * SETR + j) * 16)
                    column(ixs, r * SETR + j, j)
                    pool.wait_ge(s["col"], (r * SETR + j) * 2 + SETR + 1)
                    pool.wait_ge(s["y_dve"], r * SETR + j + 1)
                    pool.sem_inc(s["passed"], 1)
                    pool.indirect_dma_start(acc_dram, bass.IndirectOffsetOnAxis(ixs[:, j:j + 1], 0), ys[:, j % 2, :], None,
                                            compute_op=ALU.add).then_inc(s["added"], 16)
                    gather(r * SETR + j + SETR, j, (r * SETR + j + 1) * 2 + SETR)
                pool.wait_ge(s["added"], (r + 1) * SETR * 16)
                pool.sem_inc(s["passed"], 1)
            for j in range(SETR):
                pool.wait_ge(gathered[j], groups * 16 + 32)

        def in_steps(eng, step):
            groups = used(eng)
            for i in range(SETR):
                step(i, i)
            with eng.Fori(0, NBLK // SETR - 1) as r:
                with eng.If(r < groups):
                    for j in range(SETR):
                        step(r * SETR + j + SETR, j)
            step(groups * SETR + SETR, 0, True)

        @block2.scalar
        def _(act):
            act.wait_ge(s["b1_one"], 1)
            act.wait_ge(s["ready"], 1)

            def x_out(t_, j):
                act.wait_ge(s["x_t"], t_ + 1)
                if not (isinstance(t_, int) and t_ < 2):
                    act.wait_ge(s["h_pe"], t_ - 1)
                act.activation(xa[:, j, :], ps[:, 5 * j, 0:BLK], ACT.Copy)
                act.activation(xb[0:64, j, :], ps[0:64, 5 * j, BLK:2 * BLK], ACT.Copy).then_inc(s["x_e"], 1)

            def step(t_, j, last=False):
                fixed = isinstance(t_, int)
                if fixed and t_ == 0:
                    x_out(0, 0)
                if not last:
                    act.wait_ge(s["h_pe"], t_ + 1)
                    if not fixed or t_ >= 2:
                        act.wait_ge(s["y_pe"], t_ - 1)
                    b = 1 + 2 * (j % 2)
                    act.activation(ht[:, j % 2, :].rearrange("p (b m) -> p b m", b=2), ps[:, b:b + 2, 0:MH], ACT.Gelu)\
                        .then_inc(s["h_act"], 1)
                    x_out(t_ + 1, (j + 1) % 2)

            in_steps(act, step)

        @block2.tensor
        def _(pe):
            pe.wait_ge(s["e_t"], 1)
            pe.transpose(ps[0:1, 1, 0:128], e_col[:], ident[:]).then_inc(s["e_t"], 1)
            for g in range(NG):
                for k in range(TOPK):
                    i = g * TOPK + k
                    pe.wait_ge(s["oh"], i + 1)
                    pe.matmul(ps[:, 0, 0:NBLK], is_row[:, i % 8, :], is_blk[:, i % 8, :], start=(i == 0), stop=(i == NG * TOPK - 1))\
                        .then_inc(s["oh_used"], 1)
            pe.wait_ge(s["ready"], 1)

            def turn_x(t_, j):
                if isinstance(t_, int):
                    pe.wait_ge(gathered[j], (t_ // SETR + 1) * 16)
                else:
                    pe.wait_ge(gathered[j], (t_ - j) * (16 // SETR) + 16)
                if not isinstance(t_, int) or t_ >= 2:
                    pe.wait_ge(s["x_e"], t_ - 1)
                pe.sem_inc(s["passed"], 1)
                pe.transpose(ps[:, 5 * (j % 2), 0:BLK], xg[:, j, 0:128], ident[:])
                pe.transpose(ps[0:64, 5 * (j % 2), BLK:2 * BLK], xg[:, j, 128:D], ident[:]).then_inc(s["x_t"], 1)

            def hidden(b, x, k):
                for c in range(MC):
                    dst = ps[:, b + c // 3, (c % 3) * BLK:(c % 3 + 1) * BLK]
                    pe.matmul(dst, w1a[:, k, c * 128:(c + 1) * 128], xa[:, x, :], start=True, stop=False)
                    last = pe.matmul(dst, w1b[:, k, c * 128:(c + 1) * 128], xb[:, x, :], start=False, stop=True)
                last.then_inc(s["h_pe"], 1)

            def output(b, x, k):
                for c in range(MC):
                    last = pe.matmul(ps[:, b, 0:D], ht[:, x, c * BLK:(c + 1) * BLK], w2[:, k, c, :],
                                     start=(c == 0), stop=(c == MC - 1))
                last.then_inc(s["y_pe"], 1)

            def at_place(place, layer, b, x):
                with pe.If(place < 2):
                    with pe.If(place < 1):
                        layer(b, x, 0)
                    with pe.Else():
                        layer(b, x, 1)
                with pe.Else():
                    with pe.If(place < 3):
                        layer(b, x, 2)
                    with pe.Else():
                        layer(b, x, 3)

            held = [None]

            def step(t_, j, last=False):
                fixed = isinstance(t_, int)
                if fixed and t_ == 0:
                    turn_x(0, 0)
                if not last:
                    e = pe.value_load(e_tab[0:1, bass.ds(t_, 1)], min_val=0, max_val=NE - 1)
                    place = e & (WRING - 1)
                    before, held[0] = held[0], (place, j)
                    pe.wait_ge(s["w_ready"], e + 1)
                    pe.wait_ge(s["x_e"], t_ + 1)
                    if not fixed or t_ >= 2:
                        pe.wait_ge(s["h_act"], t_ - 1)
                    pe.sem_inc(s["passed"], 1)
                    at_place(place, hidden, 1 + 2 * (j % 2), j % 2)
                    turn_x(t_ + 1, (j + 1) % SETR)
                if not fixed or t_ >= 1:
                    if fixed or last or j == 0:
                        place = pe.value_load(ring_tab[0:1, bass.ds(t_ - 1, 1)], min_val=0, max_val=WRING - 1)
                    else:
                        place = before[0]
                    pe.wait_ge(s["h_act"], t_)
                    if not fixed or t_ >= 3:
                        pe.wait_ge(s["y_dve"], t_ - 2)
                    pe.sem_inc(s["passed"], 1)
                    at_place(place, output, 6 + (j - 1) % 2, (j - 1) % 2)

            in_steps(pe, step)

        @block2.vector
        def _(dve):
            n = [0]

            def link(ins):
                n[0] += 1
                ins.then_inc(s["tab"], 1)
                dve.wait_ge(s["tab"], n[0])

            dve.memset(xb[64:65, :, :], 1.0).then_inc(s["b1_one"], 1)
            link(dve.tensor_scalar(cnt_i[:], carry[:], float(BLK - 1), None, ALU.add))
            link(dve.tensor_scalar(nblk_i[:], cnt_i[:], 7, None, ALU.arith_shift_right))
            link(dve.tensor_copy(nblk[:], nblk_i[:]))
            link(dve.tensor_scalar(nblk[:], nblk[:], 1.0, None, ALU.max))
            link(dve.tensor_tensor_scan(endb[:], nblk[:], zero[:, 0:NE], 0.0, ALU.add, ALU.add))
            link(dve.tensor_tensor(first[:], endb[:], nblk[:], ALU.subtract))
            link(dve.tensor_scalar(first[:], first[:], float(BLK), 1.0, ALU.mult, ALU.add))
            link(dve.tensor_scalar(passed_e[:], endb[:], iota_p[:, 0:1], None, ALU.is_le))
            link(dve.tensor_reduce(e_col[:], passed_e[:], AX_X, ALU.add))
            dve.tensor_scalar(e_col[:], e_col[:], float(NE - 1), None, ALU.min).then_inc(s["e_t"], 1)
            dve.tensor_copy(end_tab[:], endb[0:1, :])
            link(dve.tensor_scalar(groups_tab[:], endb[0:1, NE - 1:NE], -1.0, None, ALU.add))
            link(dve.tensor_scalar(groups_tab[:], groups_tab[:], 2, None, ALU.arith_shift_right))
            link(dve.tensor_tensor(key[:], rank[:], first[0:TP].unsqueeze(1).to_broadcast([TP, NG, NE]), ALU.add))
            link(dve.tensor_tensor(key[:], key[:], maskf[:], ALU.mult))
            for g in range(NG):
                last = dve.max(top[:, g, :], key[:, g, :])
            link(last)
            link(dve.tensor_scalar(slot_i[:], top[:, :, 0:TOPK], -1.0, None, ALU.add))
            flat = slot_i[:].rearrange("p g k -> p (g k)")
            dve.tensor_scalar(at_i[:, 0, :], flat, BLK - 1, None, ALU.bitwise_and)
            link(dve.tensor_scalar(at_i[:, 1, :], flat, 7, None, ALU.arith_shift_right))
            link(dve.tensor_copy(at_f[:], at_i[:]))
            dve.wait_ge(s["e_t"], 2)
            link(dve.tensor_copy(e_tab[:], ps[0:1, 1, 0:128]))
            dve.tensor_scalar(ring_tab[:], e_tab[:], WRING - 1, None, ALU.bitwise_and)
            for g in range(NG):
                for k in range(TOPK):
                    i = g * TOPK + k
                    if i >= 8:
                        dve.wait_ge(s["oh_used"], i - 7)
                    dve.tensor_scalar(is_row[:, i % 8, :], iota[0:TP, :], at_f[:, 0, i:i + 1], None, ALU.is_equal)
                    dve.tensor_scalar(is_blk[:, i % 8, :], iota[0:TP, 0:NBLK], at_f[:, 1, i:i + 1], tok_id[:, g:g + 1],
                                      ALU.is_equal, ALU.mult).then_inc(s["oh"], 1)
            dve.wait_ge(s["oh_used"], NG * TOPK)
            link(dve.tensor_scalar(empty[:], ps[:, 0, 0:NBLK], 0.0, pad_id[:, 0:1], ALU.is_equal, ALU.mult))
            dve.tensor_scalar(ix[:, NBLK:], zero[:, 0:SETR], 0.0, pad_id[:, 0:1], ALU.mult, ALU.add)
            link(dve.scalar_tensor_tensor(out=empty[:], in0=ps[:, 0, 0:NBLK], scalar=-1.0, in1=empty[:], op0=ALU.add, op1=ALU.add))
            link(dve.tensor_scalar(ix[:, NBLK:], zero[:, 0:SETR], pad_id[:, 0:1], -1.0, ALU.add, ALU.add))
            dve.tensor_copy(ix[:, 0:NBLK], empty[:]).then_inc(s["ready"], 1)

            def step(t_, j, last=False):
                fixed = isinstance(t_, int)
                if not fixed or t_ >= 1:
                    e = dve.value_load(e_tab[0:1, bass.ds(t_ - 1, 1)], min_val=0, max_val=NE - 1)
                    dve.wait_ge(s["y_pe"], t_)
                    if not fixed or t_ >= 3:
                        dve.wait_ge(s["added"], 16 * (t_ - 2))
                    dve.tensor_scalar(ys[:, (j - 1) % 2, :], ps[:, 6 + (j - 1) % 2, 0:D], xg[:, (j - 1) % SETR, bass.ds(e + D, 1)], None, ALU.mult)\
                        .then_inc(s["y_dve"], 1)

            dve.wait_ge(s["ready"], 1)
            in_steps(dve, step)


_INS = ["x", "L0_tok_W", "L0_tok_b", "L0_tok_pos_emb", "L0_attn_A_log", "L0_attn_D_param", "L0_attn_W_bc",
        "L0_attn_W_dt", "L0_attn_W_dtp", "L0_attn_b_dt", "L0_attn_rms_scale", "L0_ffn_Wg", "L0_ffn_bg",
        "L0_ffn_Wge", "L0_ffn_bge", "L0_ffn_W1", "L0_ffn_b1", "L0_ffn_W2", "L0_ffn_b2"]


def kernel(**inputs):
    import numpy as _np
    import concourse.bacc as _bacc
    from concourse import mybir as _mybir
    from concourse.bass_utils import run_bass_kernel_spmd as _run

    nc = _bacc.Bacc("TRN2", target_bir_lowering=False, num_devices=1)
    arrays, t = {}, {}
    for name in _INS:
        a = _np.ascontiguousarray(inputs[name])
        arrays[f"in_{name}"] = a
        t[name] = nc.dram_tensor(f"in_{name}", a.shape, _mybir.dt.from_np(a.dtype), kind="ExternalInput").ap()
    out = nc.dram_tensor("out_0", (BATCH, SEQ, D), F32, kind="ExternalOutput").ap()
    tower(nc, t, out)
    r = _run(nc, [arrays], core_ids=[0])
    return r.results[0]["out_0"]
```

```python
from contextlib import ExitStack

import concourse.bass as bass
from concourse import mybir

F32 = mybir.dt.float32
F32R = mybir.dt.float32r
BF16 = mybir.dt.bfloat16
I32 = mybir.dt.int32
ACT = mybir.ActivationFunctionType
ALU = mybir.AluOpType
AX_X = mybir.AxisListType.X
LN2 = 0.6931471805599453

BATCH, CH, IMG, PATCH = 64, 3, 96, 16
HP = IMG // PATCH
WP = IMG // PATCH
SEQ = HP * WP
D = 192
NST = 16
RANK = 48
FLAT = CH * PATCH * PATCH
TOK = BATCH * SEQ
Q = 4
QB = BATCH // Q
QT = QB * SEQ
HT = QT // 2
TP = QB * HP
NCH = FLAT // 128
DB = D // 64
UC = 8
PAD = SEQ + 1
GROUPS, PER = 4, 8
NE = GROUPS * PER
M = 768
MC = M // 128
NR = GROUPS + NE
ROWW = D + NE
TOPK = 4
BLK = 128
NBLK = 104
SETR = 4
LO, HI = 0.0001, 10.0
CEN, HALF = (HI + LO) / 2, (HI - LO) / 2
MID = 2
DUPS = (("l", 0), ("l", 1), ("u", 0), ("u", 1), ("l", 2), ("u", 2))
WRING = 4


def tower(nc, t, out):
    ctx = ExitStack()
    with ctx:
        def sb(name, shape, dt=F32):
            return ctx.enter_context(nc.sbuf_tensor(name, shape, dt))

        def sem(name):
            return ctx.enter_context(nc.semaphore(name))

        rows_dram = nc.dram_tensor("rows_dram", (TOK + BLK, ROWW), F32, kind="Internal").ap()
        acc_dram = nc.dram_tensor("acc_dram", (TOK + BLK, D), F32, kind="Internal").ap()

        ps = ctx.enter_context(nc.psum_tensor("ps", [128, 8, 512], F32))

        ident = sb("ident", [128, 128])
        zero = sb("zero", [128, ROWW])
        iota = sb("iota", [128, 128])
        iota_p = sb("iota_p", [128, 1])
        tok_id = sb("tok_id", [TP, Q * WP])
        pad_id = sb("pad_id", [128, 1])
        carry = sb("carry", [128, NE])
        maskf = sb("maskf", [TP, Q * WP, NE])
        rank = sb("rank", [TP, Q * WP, NE])
        early = ExitStack()

        def sb(name, shape, dt=F32):
            return early.enter_context(nc.sbuf_tensor(name, shape, dt))

        sel = sb("sel", [128, UC, 128], F32R)
        red = sb("red", [128, UC, 64])
        shift = sb("shift", [TP, TP])
        tri = sb("tri", [TP, 128], BF16)
        ones = sb("ones", [TP, 128], BF16)
        rank_i = sb("rank_i", [TP, PER])
        upper = sb("upper", [TP, PER, PER])
        upper4 = sb("upper4", [TP, GROUPS, GROUPS])
        w_t = sb("w_t", [128, NCH, D])
        pos = sb("pos", [TP, WP * D])
        b_in = sb("b_in", [TP, D])
        wbc = sb("wbc", [128, 2, 2 * NST])
        wrep = sb("wrep", [128, 2, 2, 8, NST])
        wdt = sb("wdt", [128, 2, RANK])
        wdtp = sb("wdtp", [65, D])
        wrt = sb("wrt", [128, 2, NR])
        rbias = sb("rbias", [TP, NR])
        rms = sb("rms", [TP, D])
        dpar = sb("dpar", [TP, D])
        b2 = sb("b2", [NE, D])
        alog = sb("alog", [UC * DB, 128])
        abias = sb("abias", [128, UC * DB])
        cols = sb("cols", [128, 4])
        cen = sb("cen", [128, 1])
        x_in = sb("x_in", [TP, CH, PATCH * IMG])
        x_p = sb("x_p", [TP, WP, FLAT])
        w_in = x_p[:, 0:2, :]
        xt = sb("xt", [128, 2, NCH, TP])
        h = sb("h", [TP, WP, D])
        st6 = sb("st6", [TP, WP, 6])
        mv = sb("mv", [TP, WP, 2])
        sd = sb("sd", [TP, WP])
        rs = sb("rs", [TP, WP])
        xn = sb("xn", [TP, WP, D])
        rs2 = sb("rs2", [TP, WP])
        xs = sb("xs", [TP, WP, D])
        fs = sb("fs", [TP, WP, D])
        xnt = sb("xnt", [128, 2, QT])
        brep = sb("brep", [128, QT])
        crep = sb("crep", [128, QT])
        next_b = sb("next_b", [128, QT])
        next_c = sb("next_c", [128, QT])
        zt = sb("zt", [65, QT])
        bc = sb("bc", [TP, WP, 2 * NST])
        bcp = sb("bcp", [TP, WP, NST])
        cb = sb("cb", [TP, WP])
        ab = sb("ab", [TP, WP, D])
        ex = sb("ex", [TP, WP, D])
        lg = sb("lg", [TP, WP, D])
        w1m = sb("w1m", [TP, WP, D])
        dl = sb("dl", [TP, WP, D])
        ss = sb("ss", [TP, WP])
        th = lg
        sq = ab
        two_l = sb("two_l", [TP, WP * DB, 2, 64])
        two_u = sb("two_u", [TP, WP * DB, 2, 64])
        rd = sb("rd", [128, DB, QT], F32R)
        ru = sb("ru", [128, DB, QT], F32R)
        at = sb("at", [128, 2, QB * PAD])
        wt = sb("wt", [128, 2, QB * PAD])
        dt_ = sb("dt_", [128, 2, QB * PAD])
        s_t = sb("s_t", [128, 2, QB * PAD])
        sel_f = s_t[:].rearrange("p a n -> p (a n)")[:, 0:UC * 128].rearrange("p (c m) -> p c m", c=UC)
        cs = sb("cs", [128, 3, QT])
        yt = sb("yt", [64, DB, QT])
        h2 = sb("h2", [TP, WP, D])
        row = sb("row", [TP, WP, ROWW])
        gl = sb("gl", [TP, WP, GROUPS])
        el = sb("el", [TP, WP * GROUPS, PER])
        gs = sb("gs", [TP, WP, GROUPS])
        es = sb("es", [TP, WP * GROUPS, PER])
        gp = sb("gp", [TP, WP, GROUPS])
        ep = sb("ep", [TP, WP * GROUPS, PER])
        gmx = sb("gmx", [TP, WP])
        emx = sb("emx", [TP, WP * GROUPS])

        def spare(at, n):
            return two_l[:].rearrange("p a b c -> p (a b c)")[:, at:at + n]

        gcmp = sb("gcmp", [TP, WP, GROUPS, GROUPS])
        ecmp = spare(0, 1536).rearrange("p (w i j) -> p w i j", i=PER, j=PER)
        grk = sb("grk", [TP, 2, WP, GROUPS])
        erk = spare(1536, 384).rearrange("p (a w e) -> p a w e", a=2, e=PER)
        gsel = sb("gsel", [TP, WP, GROUPS])
        esel = spare(1920, 192).rearrange("p (w e) -> p w e", e=PER)
        gz = sb("gz", [TP, WP])
        ez = sb("ez", [TP, WP * GROUPS])
        fac = sb("fac", [TP, WP, GROUPS])
        mask = sb("mask", [TP, WP + 1, NE], BF16)
        combt = xt[0:NE, 0]

        names = (
            "passed",
            "const_in", "w_loaded", "pad_set", "made", "set_dve", "turned", "copied",
            "x_loaded", "x_split", "patch_t", "patch_c", "emb", "emb_sum",
            "ln", "ln_act", "xn_done", "shifted", "xs_done",
            "xn_t", "xn_c", "rep_pe", "rep_act", "set_rep", "z_pe", "z_act", "bc_pe", "bc_dve",
            "dt_pe", "soft_act", "soft", "dl_done", "rms_act", "rms_dve", "gate_act", "u_done",
            "dup_pe", "dup_hi", "dup_lo",
            "unit_rd", "unit_ru", "unit_a", "unit_w", "unit_d", "unit_s", "unit_c", "unit_y",
            "y_c", "y_t", "skip_pool", "skip", "res", "bias_a", "b2_a", "b2_b",
            "ln2", "ln2_act", "x2_done", "x2_t", "x2_c", "log_pe", "route", "route_act", "cnt_pe",
            "comb_t", "comb_c", "stored", "quarter_done")
        s = {n: sem(n) for n in names}
        block = early.enter_context(nc.Block())
        NCONST = 18
        NMADE = 24
        last_q = Q - 1
        U = DB * UC
        ROUTE = 26
        ROUTED = (0, 1, 2, 3, 4, 5, 9, 10, 14)

        def tokens(ap):
            return ap.rearrange("p (s c) -> p s c", c=PAD)[:, :, 1:PAD]

        def turn_bank(q, g):
            return 4 if isinstance(q, int) and g % 2 else MID

        def emb_bank(q, g):
            return 6 + g % 2 if isinstance(q, int) else MID

        def before(q):
            return q - 1 if isinstance(q, int) else (q - 1) & (Q - 1)

        def by_block(x):
            return x[:].rearrange("p g (k c) -> p (g k) c", k=DB)

        def y_out(act, q, k):
            act.wait_ge(s["unit_y"], q * U + (k + 1) * UC)
            act.activation(yt[:, k, :].rearrange("p (b n) -> p b n", b=2), ps[0:64, 0:2, 0:HT], ACT.Copy)\
                .then_inc(s["y_c"], 1)

        def turn_tokens(pe, src, done="xn_t"):
            for g in range(WP):
                for kc, p in ((0, 128), (1, 64)):
                    last = pe.transpose(ps[0:p, 2 * kc + g // 3, (g % 3) * TP:(g % 3 + 1) * TP],
                                        src[:, g, 128 * kc:128 * kc + p], ident[0:TP, 0:TP])
            last.then_inc(s[done], 1)

        @block.sync
        def _(sp):
            n = [0]

            def load(dst, src):
                sp.dma_start(dst, src).then_inc(s["const_in"], 16)
                n[0] += 1

            img = t["x"].rearrange("(q b) c (h p) w -> q b h c (p w)", q=Q, h=HP)

            def images(q):
                for c in range(CH):
                    src = img[q] if isinstance(q, int) else img[bass.ds(q, 1)].rearrange("a b h c n -> (a b) h c n")
                    sp.dma_start(x_in[:, c, :], src[:, :, c, :]).then_inc(s["x_loaded"], 16)

            sp.dma_start(w_in, t["L0_tok_W"].rearrange("(a p) f -> p a f", p=96)).then_inc(s["w_loaded"], 16)
            images(0)
            load(b_in[:], t["L0_tok_b"].partition_broadcast(TP))
            load(pos[:], t["L0_tok_pos_emb"].rearrange("(h w) d -> h (w d)", h=HP).partition_broadcast(QB))
            load(wbc[:, 0, :], t["L0_attn_W_bc"][0:128, :])
            load(wbc[0:64, 1, :], t["L0_attn_W_bc"][128:D, :])
            load(wdt[:, 0, :], t["L0_attn_W_dt"][0:128, :])
            load(wdt[0:64, 1, :], t["L0_attn_W_dt"][128:D, :])
            load(rms[:], t["L0_attn_rms_scale"].partition_broadcast(TP))
            load(dpar[:], t["L0_attn_D_param"].partition_broadcast(TP))
            load(alog[:], t["L0_attn_A_log"].rearrange("(u e) n -> u (e n)", e=8))
            load(wrt[:, 0, 0:GROUPS], t["L0_ffn_Wg"][0:128, :])
            load(wrt[0:64, 1, 0:GROUPS], t["L0_ffn_Wg"][128:D, :])
            wge = t["L0_ffn_Wge"].rearrange("g d e -> d g e")
            load(wrt[:, 0, GROUPS:NR].rearrange("p (g e) -> p g e", g=GROUPS), wge[0:128])
            load(wrt[0:64, 1, GROUPS:NR].rearrange("p (g e) -> p g e", g=GROUPS), wge[128:D])
            load(rbias[:, 0:GROUPS], t["L0_ffn_bg"].partition_broadcast(TP))
            load(rbias[:, GROUPS:NR], t["L0_ffn_bge"].rearrange("g e -> (g e)").partition_broadcast(TP))
            load(b2[:], t["L0_ffn_b2"])
            sp.wait_ge(s["made"], 6)
            load(wdtp[0:RANK, :], t["L0_attn_W_dtp"])
            load(wdtp[64:65, :], t["L0_attn_b_dt"].rearrange("(a d) -> a d", a=1))
            assert n[0] == NCONST, n
            sp.dma_start(rows_dram[TOK:TOK + BLK, :], zero[:]).then_inc(s["pad_set"], 16)
            sp.dma_start(acc_dram[TOK:TOK + BLK, :], zero[:, 0:D]).then_inc(s["pad_set"], 16)

            def results(q):
                sp.wait_ge(s["route"], (q + 1) * ROUTE)
                sp.dma_start(rows_dram[bass.ds(q * QT, QT), :].rearrange("(p g) c -> p g c", p=TP), row[:])\
                    .then_inc(s["stored"], 16)
                sp.wait_ge(s["res"], (q + 1) * 4)
                sp.dma_start(acc_dram[bass.ds(q * QT, QT), :].rearrange("(p g) c -> p g c", p=TP), h2[:])\
                    .then_inc(s["stored"], 16)

            sp.wait_ge(s["x_split"], CH)
            images(1)
            with sp.Fori(0, last_q) as q:
                with sp.If(q < Q - 2):
                    sp.wait_ge(s["x_split"], (q + 2) * CH)
                    sp.sem_inc(s["passed"], 1)
                    images((q + 2) & (Q - 1))
                results(q)
            results(last_q)
            sp.wait_ge(s["pad_set"], 32)
            sp.wait_ge(s["stored"], 32 * Q)
            sp.sem_inc(s["passed"], 1)

        @block.gpsimd
        def _(pool):
            n = [0]

            def made(ins):
                n[0] += 1
                ins.then_inc(s["made"], 1)
                pool.wait_ge(s["made"], n[0])

            def cut(ap, pattern, base, mult, op=ALU.is_ge, fill=0.0):
                made(pool.affine_select(out=ap, in_=ap, compare_op=op, fill=fill, base=base,
                                        pattern=pattern, channel_multiplier=mult))

            made(pool.memset(ident[:], 0.0))
            cut(ident[:], [[-1, 128]], 0, 1, ALU.not_equal, 1.0)
            made(pool.memset(zero[:], 0.0))
            made(pool.memset(zt[32:64, :], 0.0))
            made(pool.memset(zt[64:65, :], 1.0))
            made(pool.memset(wdtp[:], 0.0))
            made(pool.memset(sel_f, 1.0))
            for half in (0, 64):
                cut(sel_f[half:half + 64], [[128, UC], [1, 128]], 0, -16)
                cut(sel_f[half:half + 64], [[-128, UC], [-1, 128]], 15, 16)
            made(pool.memset(red[:], 1.0))
            cut(red[:], [[128, UC], [-16, 64]], 0, 1)
            cut(red[:], [[-128, UC], [16, 64]], 15, -1)
            made(pool.memset(shift[:], 0.0))
            cut(shift[:], [[-1, TP]], 1, 1, ALU.not_equal, 1.0)
            made(pool.memset(shift[:].rearrange("k (b h) -> k b h", h=HP)[:, :, 0:1], 0.0))
            pool.memset(ones[:], 1.0)
            pool.memset(mask[:], 0.0)
            made(pool.memset(tri[:], 1.0))
            cut(tri[:], [[1, 128]], -1, -1)
            made(pool.memset(upper[:], 1.0))
            cut(upper[:], [[-1, PER], [1, PER]], -1, 0)
            made(pool.memset(upper4[:], 1.0))
            cut(upper4[:], [[-1, GROUPS], [1, GROUPS]], -1, 0)
            pool.iota(rank_i[:], [[1, PER]], 0, 0, allow_small_or_imprecise_dtypes=True)
            pool.iota(iota[:], [[1, 128]], 0, 0, allow_small_or_imprecise_dtypes=True)
            pool.iota(iota_p[:], [[0, 1]], 0, 1, allow_small_or_imprecise_dtypes=True)
            pool.iota(pad_id[:], [[0, 1]], TOK + 1, 1, allow_small_or_imprecise_dtypes=True)
            pool.iota(tok_id[:], [[QT, Q], [1, WP]], 1, WP, allow_small_or_imprecise_dtypes=True)
            pool.memset(at[:], 0.0)
            pool.memset(wt[:], 0.0)
            pool.memset(dt_[:], 0.0)
            made(pool.memset(carry[:], 0.0))
            assert n[0] == NMADE, n

            def skip(q):
                pool.wait_ge(s["xn_done"], q + 1)
                if not isinstance(q, int):
                    pool.wait_ge(s["res"], before(q) * 4 + 3)
                pool.tensor_tensor(fs[:], xn[:], dpar[:].unsqueeze(1).to_broadcast([TP, WP, D]), ALU.mult)\
                    .then_inc(s["skip_pool"], 1)
                pool.wait_ge(s["skip_pool"], q * 2 + 1)
                pool.tensor_tensor(fs[:], fs[:], h[:], ALU.add).then_inc(s["skip_pool"], 1)

            def units(q, with_front):
                def add_shifted(i):
                    pool.wait_ge(s["unit_w"], q * U + i + 1)
                    if i >= 2:
                        pool.wait_ge(s["unit_s"], q * U + i - 1)
                    pool.tensor_tensor(dt_[:, i % 2, 1:], wt[:, i % 2, 1:], wt[:, i % 2, :-1], ALU.add)\
                        .then_inc(s["unit_d"], 1)

                for i in range(U):
                    add_shifted(i)
                if with_front:
                    skip(q + 1)
                pool.wait_ge(s["unit_d"], (q + 1) * U)
                pool.sem_inc(s["quarter_done"], 1)
                pool.wait_ge(s["quarter_done"], (q + 1) * 4)

            skip(0)
            with pool.Fori(0, last_q) as q:
                units(q, True)
            units(last_q, False)

        @block.scalar
        def _(act):
            for j in range(NCH):
                act.wait_ge(s["turned"], j + 1)
                act.activation(w_t[:, j, :], ps[:, j % 4, 0:D], ACT.Copy).then_inc(s["copied"], 1)
            act.wait_ge(s["turned"], NCH + 1)
            act.wait_ge(s["set_dve"], 1)
            act.activation(abias[:], ps[:, 7, 0:UC * DB], ACT.Identity, bias=cols[:, 0:1], scale=-0.5)\
                .then_inc(s["copied"], 1)

            def split(q):
                act.wait_ge(s["x_loaded"], (q + 1) * 16 * CH)
                if not isinstance(q, int) or q >= 1:
                    act.wait_ge(s["emb"], q * WP)
                act.sem_inc(s["passed"], 1)
                for c in range(CH):
                    act.activation(x_p[:, :, c * PATCH * PATCH:(c + 1) * PATCH * PATCH].rearrange("r g (p v) -> r p g v", p=PATCH),
                                   x_in[:, c, :].rearrange("r (p g v) -> r p g v", p=PATCH, g=WP), ACT.Copy)\
                        .then_inc(s["x_split"], 1)

            def dup_hi(q, i):
                which, k = DUPS[i]
                act.wait_ge(s["dup_pe"], q * 6 + i + 1)
                b = turn_bank(q, i)
                act.activation({"l": rd, "u": ru}[which][:, k, :].rearrange("p (r b g) -> p b g r", b=2, g=3),
                               ps[:, b:b + 2, 0:HT].rearrange("p b (g r) -> p b g r", g=3), ACT.Copy)\
                    .then_inc(s["dup_hi"], 1)

            def front(q, i):
                if i < WP:
                    act.wait_ge(s["patch_t"], q * WP + i + 1)
                    b = turn_bank(q, i)
                    act.activation(xt[:, i % 2].rearrange("p (b j) n -> p b (j n)", b=2), ps[:, b:b + 2, 0:HT], ACT.Copy)\
                        .then_inc(s["patch_c"], 1)
                if i == 6:
                    act.wait_ge(s["ln"], q * 3 + 2)
                    act.activation(sd[:], mv[:, :, 1], ACT.Sqrt, bias=cols[0:TP, 1:2]).then_inc(s["ln_act"], 1)
                if i in (9, 10):
                    kc, p = ((0, 128), (1, 64))[i - 9]
                    act.wait_ge(s["xn_t"], q * 2 + kc + 1)
                    act.activation(xnt[0:p, kc, :].rearrange("p (r b g) -> p b g r", b=2, g=3),
                                   ps[0:p, MID:MID + 2, 0:HT].rearrange("p b (g r) -> p b g r", g=3), ACT.Copy)\
                        .then_inc(s["xn_c"], 1)
                if i in (15, 16):
                    j = i - 15
                    act.wait_ge(s["rep_pe"], q * 2 + j + 1)
                    act.activation((next_b, next_c)[j][:].rearrange("p (b n) -> p b n", b=2), ps[:, MID:MID + 2, 0:HT], ACT.Copy)\
                        .then_inc(s["rep_act"], 1)
                if i == 11:
                    act.wait_ge(s["z_pe"], q + 1)
                    act.activation(zt[0:RANK].rearrange("p (b n) -> p b n", b=2), ps[0:RANK, MID:MID + 2, 0:HT], ACT.Copy)\
                        .then_inc(s["z_act"], 1)
                if i in (12, 13):
                    part = dl[:, 0:4, :] if i == 12 else dl[:, 4:6, :]
                    act.wait_ge(s["dt_pe"], q * 2 + i - 11)
                    act.activation(part.rearrange("p (b g) d -> p b (g d)", g=2),
                                   ps[0:TP, MID:MID + (2 if i == 12 else 1), 0:2 * D], ACT.Copy).then_inc(s["soft_act"], 1)
                if i == 13:
                    act.wait_ge(s["soft_act"], q * 5 + 2)
                    act.activation(ab[:], dl[:], ACT.Abs).then_inc(s["soft_act"], 1)
                    act.wait_ge(s["soft_act"], q * 5 + 3)
                    act.activation(ex[:], ab[:], ACT.Exp, scale=-1.0).then_inc(s["soft_act"], 1)
                if i == 14:
                    act.wait_ge(s["soft_act"], q * 5 + 4)
                    act.activation(lg[:], ex[:], ACT.Ln, bias=1.0).then_inc(s["soft_act"], 1)
                if i == 15:
                    act.wait_ge(s["dl_done"], q * 2 + 2)
                    for g in range(WP):
                        last = act.activation(sq[:, g, :], dl[:, g, :], ACT.Square, accum_out=ss[:, g:g + 1])
                    last.then_inc(s["rms_act"], 1)
                    act.wait_ge(s["rms_act"], q * 2 + 1)
                    act.activation(rs2[:], ss[:], ACT.Sqrt, scale=1.0 / D, bias=cols[0:TP, 2:3]).then_inc(s["rms_act"], 1)
                if i == 16:
                    act.wait_ge(s["rms_dve"], q * 2 + 2)
                    act.activation(th[:], w1m[:], ACT.Tanh, scale=1.0 / HALF, bias=cols[0:TP, 3:4]).then_inc(s["gate_act"], 1)
                if i == 17:
                    act.wait_ge(s["gate_act"], q * 3 + 1)
                    act.activation(two_l[:], by_block(th).unsqueeze(2).to_broadcast(twice), ACT.Ln,
                                   scale=HALF, bias=cen[0:TP, :]).then_inc(s["gate_act"], 1)
                    act.activation(sq[:], th[:], ACT.Sqrt, scale=HALF, bias=cen[0:TP, :]).then_inc(s["gate_act"], 1)
                if i == 18:
                    dup_hi(q, 0)
                if i == 19:
                    dup_hi(q, 1)
                if i == 20:
                    dup_hi(q, 2)
                if i == 21:
                    dup_hi(q, 3)

            def behind(q):
                dup_hi(q, 4)
                act.wait_ge(s["rep_act"], q * 2 + 2)
                if not isinstance(q, int):
                    act.wait_ge(s["unit_c"], q * U)
                act.activation(brep[:], next_b[:], ACT.Copy).then_inc(s["set_rep"], 1)
                act.activation(crep[:], next_c[:], ACT.Copy).then_inc(s["set_rep"], 1)
                dup_hi(q, 5)

            def units(q, with_front):
                decay(q, 0)
                for i in range(U):
                    if i + 1 < U:
                        decay(q, i + 1)
                    if i % UC == 1 and i > UC:
                        y_out(act, q, i // UC - 1)
                    if with_front:
                        front(q + 1, i)
                    if i == 1:
                        with act.If(q > 0):
                            gates(before(q))
                    if i == 17:
                        with act.If(q > 0):
                            weights_out(before(q))
                y_out(act, q, DB - 1)
                if with_front:
                    behind(q + 1)

            def gates(q):
                act.wait_ge(s["route"], q * ROUTE + 6)
                act.activation(gp[:], gs[:], ACT.Exp)
                act.activation(ep[:], es[:], ACT.Exp).then_inc(s["route_act"], 1)

            def weights_out(q):
                act.wait_ge(s["comb_t"], q + 1)
                act.activation(combt[:].rearrange("e (b g) r -> e b (g r)", b=2), ps[0:NE, MID:MID + 2, 0:HT], ACT.Copy)\
                    .then_inc(s["comb_c"], 1)

            def decay(q, i):
                act.wait_ge(s["unit_rd"], q * U + i + 1)
                if i >= 2:
                    act.wait_ge(s["unit_s"], q * U + i - 1)
                act.activation(tokens(at[:, i % 2]).rearrange("p (b s) c -> p b s c", b=2),
                               ps[:, 4:6, 0:HT].rearrange("p b (s c) -> p b s c", c=SEQ), ACT.Tanh,
                               scale=-0.5, bias=abias[:, i:i + 1]).then_inc(s["unit_a"], 1)

            def back(q):
                act.wait_ge(s["ln2"], q * 3 + 2)
                act.activation(sd[:], mv[:, :, 1], ACT.Sqrt, bias=cols[0:TP, 1:2]).then_inc(s["ln2_act"], 1)
                act.wait_ge(s["x2_t"], q + 1)
                for kc, p in ((0, 128), (1, 64)):
                    last = act.activation(xnt[0:p, kc, :].rearrange("p (b n) -> p b n", b=2),
                                          ps[0:p, 2 * kc:2 * kc + 2, 0:HT], ACT.Copy)
                last.then_inc(s["x2_c"], 1)
                act.wait_ge(s["x2_c"], q + 1)
                act.sem_inc(s["quarter_done"], 1)

            twice = [TP, WP * DB, 2, 64]
            split(0)
            for i in range(U):
                front(0, i)
                if i == 14:
                    split(1)
            behind(0)
            with act.Fori(0, last_q) as q:
                units(q, True)
                with act.If(q < Q - 2):
                    split(q + 2)
                back(q)
                act.wait_ge(s["quarter_done"], (q + 1) * 4)
            units(last_q, False)
            back(last_q)
            act.wait_ge(s["quarter_done"], Q * 4)
            gates(last_q)
            weights_out(last_q)

        @block.tensor
        def _(pe):
            pe.wait_ge(s["w_loaded"], 16)
            pe.wait_ge(s["made"], 2)
            for j in range(NCH):
                if j >= 4:
                    pe.wait_ge(s["copied"], j - 3)
                for a in range(2):
                    last = pe.transpose(ps[:, j % 4, a * 96:a * 96 + 96], w_in[:, a, j * 128:(j + 1) * 128], ident[0:96, 0:96])
                last.then_inc(s["turned"], 1)
            pe.wait_ge(s["const_in"], 16 * NCONST)
            pe.wait_ge(s["made"], NMADE)
            pe.transpose(ps[:, 7, 0:UC * DB], alog[:], ident[0:UC * DB, 0:UC * DB]).then_inc(s["turned"], 1)
            pe.wait_ge(s["copied"], NCH + 1)
            pe.wait_ge(s["set_dve"], 5)

            def dup(q, i):
                which, k = DUPS[i]
                if i == 0:
                    pe.wait_ge(s["gate_act"], q * 3 + 2)
                    pe.sem_inc(s["passed"], 1)
                if i == 2:
                    pe.wait_ge(s["u_done"], q + 1)
                if not isinstance(q, int):
                    if i > 0:
                        pe.wait_ge(s["dup_lo"], q * 6 + i)
                elif i > 1:
                    pe.wait_ge(s["dup_lo"], i - 1)
                for g in range(WP):
                    last = pe.transpose(ps[:, turn_bank(q, i) + g // 3, (g % 3) * TP:(g % 3 + 1) * TP],
                                        {"l": two_l, "u": two_u}[which][:, g * DB + k].rearrange("p a c -> p (a c)"), ident[0:TP, 0:TP])
                last.then_inc(s["dup_pe"], 1)

            def embed(q, g):
                pe.wait_ge(s["patch_c"], q * WP + g + 1)
                if isinstance(q, int) and g >= 2:
                    pe.wait_ge(s["emb_sum"], g - 1)
                for j in range(NCH):
                    last = pe.matmul(ps[0:TP, emb_bank(q, g), 0:D], xt[:, g % 2, j, :], w_t[:, j, :], start=(j == 0), stop=(j == NCH - 1))
                last.then_inc(s["emb"], 1)

            def front(q, i):
                if i == 0:
                    pe.wait_ge(s["x_split"], (q + 1) * CH)
                if 1 <= i <= WP and not isinstance(q, int):
                    pe.wait_ge(s["emb_sum"], q * WP + i)
                if i < WP:
                    for j in range(NCH):
                        last = pe.transpose(ps[:, turn_bank(q, i) + j // 3, (j % 3) * TP:(j % 3 + 1) * TP],
                                            x_p[:, i, j * 128:(j + 1) * 128], ident[0:TP, 0:TP])
                    last.then_inc(s["patch_t"], 1)
                if i == 8:
                    pe.wait_ge(s["xn_done"], q + 1)
                    pe.matmul(ps[0:TP, MID, 0:D], shift[:], xn[:, WP - 1, :], start=True, stop=True, skip_group_check=True)\
                        .then_inc(s["shifted"], 1)
                if i in (9, 10):
                    kc, p = ((0, 128), (1, 64))[i - 9]
                    if kc == 0:
                        pe.wait_ge(s["xs_done"], q + 1)
                    else:
                        pe.wait_ge(s["xn_c"], q * 2 + 1)
                    pe.sem_inc(s["passed"], 1)
                    for g in range(WP):
                        last = pe.transpose(ps[0:p, MID + g // 3, (g % 3) * TP:(g % 3 + 1) * TP],
                                            xn[:, g, 128 * kc:128 * kc + p], ident[0:TP, 0:TP])
                    last.then_inc(s["xn_t"], 1)
                if i in (15, 16):
                    j = i - 15
                    if j == 1:
                        pe.wait_ge(s["rep_act"], q * 2 + 1)
                    for b in range(2):
                        for kc, p in ((0, 128), (1, 64)):
                            last = pe.matmul(ps[:, MID + b, 0:HT], wrep[0:p, kc, j].rearrange("p a n -> p (a n)"),
                                             xnt[0:p, kc, b * HT:(b + 1) * HT], start=(kc == 0), stop=(kc == 1))
                    last.then_inc(s["rep_pe"], 1)
                if i == 11:
                    pe.wait_ge(s["xn_c"], q * 2 + 2)
                    for b in range(2):
                        for kc, p in ((0, 128), (1, 64)):
                            last = pe.matmul(ps[0:RANK, MID + b, 0:HT], wdt[0:p, kc, :], xnt[0:p, kc, b * HT:(b + 1) * HT],
                                             start=(kc == 0), stop=(kc == 1))
                    last.then_inc(s["z_pe"], 1)
                if i in (12, 13):
                    if i == 12:
                        pe.wait_ge(s["z_act"], q + 1)
                    else:
                        pe.wait_ge(s["soft_act"], q * 5 + 1)
                    for g in (range(0, 4) if i == 12 else range(4, WP)):
                        last = pe.matmul(ps[0:TP, MID + g % 4 // 2, (g % 2) * D:(g % 2 + 1) * D],
                                         zt[:].rearrange("p (r g) -> p g r", g=WP)[:, g, :], wdtp[:], start=True, stop=True)
                    last.then_inc(s["dt_pe"], 1)
                if i == 13:
                    for g in range(WP):
                        for kc, p in ((0, 128), (1, 64)):
                            last = pe.matmul(ps[0:TP, MID + 1, g * 32:g * 32 + 32],
                                             xnt[0:p, kc, :].rearrange("p (r g) -> p g r", g=WP)[:, g, :],
                                             wbc[0:p, kc, :], start=(kc == 0), stop=(kc == 1), skip_group_check=True)
                    last.then_inc(s["bc_pe"], 1)
                if i == 14:
                    pe.wait_ge(s["soft_act"], q * 5 + 2)
                    pe.wait_ge(s["bc_dve"], q * 3 + 1)
                    pe.sem_inc(s["passed"], 1)
                if i == 17:
                    pe.wait_ge(s["rep_act"], q * 2 + 2)
                    pe.sem_inc(s["passed"], 1)
                if i in (18, 19, 20, 21):
                    dup(q, i - 18)
                if i == 22:
                    pe.wait_ge(s["dup_lo"], q * 6 + 4)
                    pe.sem_inc(s["passed"], 1)

            def behind(q):
                dup(q, 4)
                dup(q, 5)

            def units(q, with_front):
                def spread(i):
                    k, c = divmod(i, UC)
                    for src, bank, free, done in ((ru, 6, "unit_w", "unit_ru"), (rd, 4, "unit_a", "unit_rd")):
                        if i >= 1:
                            pe.wait_ge(s[free], q * U + i)
                        for b in range(2):
                            last = pe.matmul(ps[:, bank + b, 0:HT], sel[:, c, :], src[:, k, b * HT:(b + 1) * HT], start=True, stop=True)
                        last.then_inc(s[done], 1)

                def gather_y(i):
                    k, c = divmod(i, UC)
                    pe.wait_ge(s["unit_c"], q * U + i + 1)
                    if c == 0 and k >= 1:
                        pe.wait_ge(s["y_c"], q * DB + k)
                    for b in range(2):
                        last = pe.matmul(ps[0:64, b, 0:HT], red[:, c, :], cs[:, i % 3, b * HT:(b + 1) * HT],
                                         start=(c == 0), stop=(c == UC - 1), skip_group_check=True)
                    last.then_inc(s["unit_y"], 1)

                pe.wait_ge(s["dup_lo"], (q + 1) * 6)
                spread(0)
                for i in range(U):
                    if i + 1 < U:
                        spread(i + 1)
                    if i == 15:
                        with pe.If(q > 0):
                            pe.wait_ge(s["route"], (before(q) + 1) * ROUTE)
                            pe.sem_inc(s["passed"], 1)
                    if i == 18:
                        with pe.If(q > 0):
                            pe.wait_ge(s["comb_c"], before(q) + 1)
                            pe.sem_inc(s["passed"], 1)
                    if with_front:
                        front(q + 1, i)
                    if i >= 2:
                        gather_y(i - 2)
                    if with_front and i < WP:
                        embed(q + 1, i)
                    if i == 14:
                        with pe.If(q > 0):
                            count(before(q))
                    if i in (17, 22, 23):
                        with pe.If(q > 0):
                            bias(before(q), (17, 22, 23).index(i))
                gather_y(U - 2)
                gather_y(U - 1)

            def count(q):
                pe.wait_ge(s["route"], q * ROUTE + ROUTE - 2)
                pe.matmul(ps[:, MID + 1, 0:(WP + 1) * NE], tri[:], mask[:].rearrange("p g e -> p (g e)"), start=True, stop=False,
                          skip_group_check=True)
                for g in range(WP):
                    last = pe.matmul(ps[:, MID + 1, (g + 1) * NE:(WP + 1) * NE], ones[:],
                                     mask[:, g, :].unsqueeze(1).to_broadcast([TP, WP - g, NE]), start=False, stop=(g == WP - 1),
                                     skip_group_check=True)
                last.then_inc(s["cnt_pe"], 1)

            def bias(q, part):
                if part == 0:
                    pe.wait_ge(s["route"], (q + 1) * ROUTE)
                    for g in range(WP):
                        last = pe.transpose(ps[0:NE, MID + g // 3, (g % 3) * TP:(g % 3 + 1) * TP], row[:, g, D:ROWW], ident[0:TP, 0:TP])
                    last.then_inc(s["comb_t"], 1)
                else:
                    if part == 1:
                        pe.wait_ge(s["comb_c"], q + 1)
                    else:
                        pe.wait_ge(s["bias_a"], q + 1)
                    for g in (range(0, 4) if part == 1 else range(4, WP)):
                        bank = MID + g // 2 if part == 1 else MID + 1
                        last = pe.matmul(ps[0:TP, bank, (g % 2) * D:(g % 2 + 1) * D], combt[:, g, :], b2[:], start=True, stop=True)
                    last.then_inc(s[("b2_a", "b2_b")[part - 1]], 1)

            def back(q, with_front):
                pe.wait_ge(s["y_c"], (q + 1) * DB)
                pe.wait_ge(s["unit_w"], (q + 1) * U)
                pe.wait_ge(s["unit_a"], (q + 1) * U)
                pe.sem_inc(s["passed"], 1)
                for g in range(WP):
                    for k in range(DB):
                        last = pe.transpose(ps[0:TP, 4 + g // 2, (g % 2) * D + 64 * k:(g % 2) * D + 64 * k + 64],
                                            yt[:, k, :].rearrange("p (r g) -> p g r", g=WP)[:, g, :], ident[0:64, 0:64])
                last.then_inc(s["y_t"], 1)
                with pe.If(q > 0):
                    pe.wait_ge(s["res"], (before(q) + 1) * 4)
                    pe.sem_inc(s["passed"], 1)
                if with_front:
                    behind(q + 1)
                pe.wait_ge(s["x2_done"], q + 1)
                if with_front:
                    pe.wait_ge(s["dup_lo"], (q + 2) * 6)
                turn_tokens(pe, row, "x2_t")
                pe.wait_ge(s["x2_c"], q + 1)
                for g in range(WP):
                    for kc, p in ((0, 128), (1, 64)):
                        last = pe.matmul(ps[0:TP, 7, g * NR:(g + 1) * NR], xnt[0:p, kc, g * TP:(g + 1) * TP], wrt[0:p, kc, :],
                                         start=(kc == 0), stop=(kc == 1), skip_group_check=True)
                last.then_inc(s["log_pe"], 1)
                pe.wait_ge(s["log_pe"], q + 1)
                pe.sem_inc(s["quarter_done"], 1)
                pe.wait_ge(s["quarter_done"], (q + 1) * 4)

            for i in range(U):
                front(0, i)
                if 1 <= i <= WP:
                    embed(0, i - 1)
            behind(0)
            with pe.Fori(0, last_q) as q:
                units(q, True)
                back(q, True)
            units(last_q, False)
            back(last_q, False)
            count(last_q)
            for part in range(3):
                bias(last_q, part)

        @block.vector
        def _(dve):
            n = [0]

            def setup(ins):
                n[0] += 1
                ins.then_inc(s["set_dve"], 1)

            dve.memset(cols[:, 0:1], 0.5 * LN2)
            dve.memset(cols[:, 1:2], 1e-5)
            dve.memset(cols[:, 2:3], 1e-6)
            dve.memset(cen[:], CEN)
            setup(dve.memset(cols[:, 3:4], -CEN / HALF))
            dve.wait_ge(s["made"], NMADE)
            dve.wait_ge(s["const_in"], 16 * (NCONST))
            setup(dve.tensor_copy(sel[:], sel_f))
            for j in range(2):
                for kc, p in ((0, 128), (1, 64)):
                    last = dve.tensor_copy(wrep[0:p, kc, j], wbc[0:p, kc, j * NST:(j + 1) * NST].unsqueeze(1).to_broadcast([p, 8, NST]))
            setup(last)
            setup(dve.tensor_tensor(pos[:].rearrange("p (g d) -> p g d", d=D), pos[:].rearrange("p (g d) -> p g d", d=D),
                                    b_in[:].unsqueeze(1).to_broadcast([TP, WP, D]), ALU.add))
            dve.wait_ge(s["set_dve"], 4)
            setup(dve.memset(cs[:, :, 0:1], 0.0))

            def moments(q, src, steps):
                for g in range(WP):
                    last = dve.bn_stats(st6[:, g, :], src[:, g, :])
                last.then_inc(s[steps], 1)
                dve.wait_ge(s[steps], q * 3 + 1)
                dve.sem_inc(s["passed"], 1)
                for g in range(WP):
                    last = dve.bn_aggr(mv[:, g, :], st6[:, g, :])
                last.then_inc(s[steps], 1)

            def norm(q, src, dst, steps, roots, done):
                dve.wait_ge(s[roots], q + 1)
                dve.reciprocal(rs[:], sd[:]).then_inc(s[steps], 1)
                dve.wait_ge(s[steps], q * 3 + 3)
                for g in range(WP):
                    last = dve.tensor_scalar(dst[:, g, 0:D], src[:, g, :], mv[:, g, 0:1], rs[:, g:g + 1], ALU.subtract, ALU.mult)
                last.then_inc(s[done], 1)

            def dup_lo(q, i):
                which, k = DUPS[i]
                dve.wait_ge(s["dup_hi"], q * 6 + i + 1)
                b = turn_bank(q, i)
                part = {"l": rd, "u": ru}[which][64:128, k, :].rearrange("p (r b g) -> p b g r", b=2, g=3)
                dve.tensor_tensor(part, ps[64:128, b:b + 2, 0:HT].rearrange("p b (g r) -> p b g r", g=3), part.bitcast(F32),
                                  ALU.subtract).then_inc(s["dup_lo"], 1)

            def front(q, i):
                if i < WP:
                    dve.wait_ge(s["emb"], q * WP + i + 1)
                    dve.tensor_tensor(h[:, i, :], ps[0:TP, emb_bank(q, i), 0:D], pos[:, i * D:(i + 1) * D], ALU.add).then_inc(s["emb_sum"], 1)
                if i == 6:
                    dve.wait_ge(s["emb_sum"], (q + 1) * WP)
                    moments(q, h, "ln")
                if i == 7:
                    norm(q, h, xn, "ln", "ln_act", "xn_done")
                if i == 8:
                    dve.wait_ge(s["xn_done"], q + 1)
                    dve.tensor_tensor(xs[:, 1:, :], xn[:, 1:, :], xn[:, :-1, :], ALU.add)
                    dve.wait_ge(s["shifted"], q + 1)
                    dve.tensor_tensor(xs[:, 0, :], ps[0:TP, MID, 0:D], xn[:, 0, :], ALU.add).then_inc(s["xs_done"], 1)
                if i == 14:
                    dve.wait_ge(s["soft_act"], q * 5 + 4)
                    dve.tensor_scalar(w1m[:], ex[:], 1.0, -1.0, ALU.add, ALU.add).then_inc(s["soft"], 1)
                    dve.wait_ge(s["soft"], q * 2 + 1)
                    dve.tensor_tensor(ab[:], w1m[:], ex[:], ALU.subtract).then_inc(s["soft"], 1)
                if i == 13:
                    dve.wait_ge(s["bc_pe"], q + 1)
                    dve.tensor_copy(bc[:], ps[0:TP, MID + 1, 0:WP * 32].rearrange("p (g n) -> p g n", g=WP)).then_inc(s["bc_dve"], 1)
                    dve.wait_ge(s["bc_dve"], q * 3 + 1)
                    dve.tensor_tensor(bcp[:], bc[:, :, 0:NST], bc[:, :, NST:2 * NST], ALU.mult).then_inc(s["bc_dve"], 1)
                    dve.wait_ge(s["bc_dve"], q * 3 + 2)
                    dve.tensor_reduce(cb[:], bcp[:], AX_X, ALU.add).then_inc(s["bc_dve"], 1)
                if i == 15:
                    dve.wait_ge(s["soft_act"], q * 5 + 5)
                    dve.scalar_tensor_tensor(out=dl[:], in0=dl[:], scalar=0.0, in1=lg[:], op0=ALU.max, op1=ALU.add)\
                        .then_inc(s["dl_done"], 1)
                    dve.wait_ge(s["soft"], q * 2 + 2)
                    dve.wait_ge(s["dl_done"], q * 2 + 1)
                    dve.tensor_tensor(dl[:], dl[:], ab[:], ALU.subtract).then_inc(s["dl_done"], 1)
                if i == 16:
                    dve.wait_ge(s["rms_act"], q * 2 + 2)
                    dve.reciprocal(rs[:], rs2[:]).then_inc(s["rms_dve"], 1)
                    dve.wait_ge(s["rms_dve"], q * 2 + 1)
                    for g in range(WP):
                        last = dve.scalar_tensor_tensor(out=w1m[:, g, :], in0=dl[:, g, :], scalar=rs[:, g:g + 1], in1=rms[:],
                                                        op0=ALU.mult, op1=ALU.mult)
                    last.then_inc(s["rms_dve"], 1)
                if i == 18:
                    dup_lo(q, 0)
                    dve.wait_ge(s["gate_act"], q * 3 + 3)
                    dve.wait_ge(s["xs_done"], q + 1)
                    dve.sem_inc(s["passed"], 1)
                    for d in range(2):
                        last = dve.scalar_tensor_tensor(out=two_u[:, :, d, :], in0=by_block(sq), scalar=0.25, in1=by_block(xs),
                                                        op0=ALU.mult, op1=ALU.mult)
                    last.then_inc(s["u_done"], 1)
                if i == 19:
                    dup_lo(q, 1)
                if i == 20:
                    dup_lo(q, 2)
                if i == 21:
                    dup_lo(q, 3)

            def behind(q):
                dup_lo(q, 4)
                dup_lo(q, 5)

            def units(q, with_front):
                def inputs(i):
                    dve.wait_ge(s["unit_ru"], q * U + i + 1)
                    if i >= 2:
                        dve.wait_ge(s["unit_d"], q * U + i - 1)
                    dve.tensor_tensor(tokens(wt[:, i % 2]).rearrange("p (b s) c -> p b s c", b=2),
                                      ps[:, 6:8, 0:HT].rearrange("p b (s c) -> p b s c", c=SEQ),
                                      brep[:].rearrange("p (b s c) -> p b s c", b=2, c=SEQ), ALU.mult).then_inc(s["unit_w"], 1)

                def outputs(i):
                    dve.wait_ge(s["unit_s"], q * U + i + 1)
                    if i >= 3:
                        dve.wait_ge(s["unit_y"], q * U + i - 2)
                    dve.tensor_tensor(cs[:, i % 3, :].rearrange("p (s c) -> p s c", c=SEQ), tokens(s_t[:, i % 2]),
                                      crep[:].rearrange("p (s c) -> p s c", c=SEQ), ALU.mult).then_inc(s["unit_c"], 1)

                dve.wait_ge(s["set_rep"], (q + 1) * 2)
                inputs(0)
                for i in range(U):
                    if i + 1 < U:
                        inputs(i + 1)
                    if i >= 1:
                        outputs(i - 1)
                    dve.wait_ge(s["unit_d"], q * U + i + 1)
                    dve.wait_ge(s["unit_a"], q * U + i + 1)
                    dve.tensor_tensor_scan(s_t[:, i % 2, :], dt_[:, i % 2, :], at[:, i % 2, :], 0.0, ALU.add, ALU.mult)\
                        .then_inc(s["unit_s"], 1)
                    if with_front:
                        front(q + 1, i)
                    if i in ROUTED:
                        with dve.If(q > 0):
                            routing(before(q), ROUTED.index(i))
                    if i in (22, 23):
                        with dve.If(q > 0):
                            bias(before(q), i - 22)
                outputs(U - 1)

            def bias(q, part):
                dve.wait_ge(s[("b2_a", "b2_b")[part]], q + 1)
                g, b, n_ = ((0, MID, 2), (4, MID + 1, 1))[part]
                mine = h2[:, g:g + 2 * n_, :].rearrange("p (b g) d -> p b (g d)", g=2)
                dve.tensor_tensor(mine, ps[0:TP, b:b + n_, 0:2 * D], mine, ALU.add).then_inc(s[("bias_a", "res")[part]], 1)

            def skip(q):
                dve.wait_ge(s["u_done"], q + 1)
                dve.wait_ge(s["skip_pool"], q * 2 + 2)
                dve.sem_inc(s["passed"], 1)
                for g in range(WP):
                    mine = fs[:, g, :].rearrange("p (k c) -> p k c", k=DB)
                    last = dve.scalar_tensor_tensor(out=mine, in0=two_u[:, g * DB:(g + 1) * DB, 0, :], scalar=cb[:, g:g + 1], in1=mine,
                                                    op0=ALU.mult, op1=ALU.add)
                last.then_inc(s["skip"], 1)

            def back(q, with_front):
                with dve.If(q > 0):
                    dve.wait_ge(s["stored"], (before(q) + 1) * 32)
                    dve.sem_inc(s["passed"], 1)
                dve.wait_ge(s["skip"], q + 1)
                dve.wait_ge(s["y_t"], q + 1)
                dve.sem_inc(s["passed"], 1)
                pair = "p (g d) -> p g d"
                for j in range(3):
                    dve.tensor_tensor(h2[:, 2 * j:2 * j + 2, :], ps[0:TP, 4 + j, 0:2 * D].rearrange(pair, g=2),
                                      fs[:, 2 * j:2 * j + 2, :], ALU.add).then_inc(s["res"], 1)
                if with_front:
                    dup_lo(q + 1, 4)
                dve.wait_ge(s["res"], q * 4 + 3)
                moments(q, h2, "ln2")
                if with_front:
                    dup_lo(q + 1, 5)
                norm(q, h2, row, "ln2", "ln2_act", "x2_done")
                if with_front:
                    skip(q + 1)
                dve.wait_ge(s["log_pe"], q + 1)
                logits = ps[0:TP, 7, 0:WP * NR].rearrange("p (g n) -> p g n", g=WP)
                dve.tensor_tensor(gl[:], logits[:, :, 0:GROUPS], rbias[:, 0:GROUPS].unsqueeze(1).to_broadcast([TP, WP, GROUPS]), ALU.add)\
                    .then_inc(s["route"], 1)
                dve.tensor_tensor(el[:].rearrange("p (w g) e -> p w (g e)", g=GROUPS), logits[:, :, GROUPS:NR],
                                  rbias[:, GROUPS:NR].unsqueeze(1).to_broadcast([TP, WP, NE]), ALU.add).then_inc(s["route"], 1)
                dve.wait_ge(s["route"], q * ROUTE + 2)
                dve.sem_inc(s["quarter_done"], 1)
                dve.wait_ge(s["quarter_done"], (q + 1) * 4)

            WG = WP * GROUPS
            steps = {0: 2, 1: 6, 2: 12, 3: 13, 4: 14, 5: 14, 6: 15, 7: 21, 8: 24}

            def routing(q, i):
                m = [steps[i]]

                def link(ins):
                    m[0] += 1
                    ins.then_inc(s["route"], 1)
                    dve.wait_ge(s["route"], q * ROUTE + m[0])

                def compare(x, cmp, w, n_):
                    big = [TP, w, n_, n_]
                    link(dve.tensor_tensor(cmp, x[:].unsqueeze(2).to_broadcast(big), x[:].unsqueeze(3).to_broadcast(big), ALU.is_gt))

                def ahead(cmp, up, w, n_):
                    link(dve.tensor_tensor(cmp.rearrange("p w i j -> p w (i j)"), cmp.rearrange("p w i j -> p w (i j)"),
                                           up[:].rearrange("p i j -> p (i j)").unsqueeze(1).to_broadcast([TP, w, n_ * n_]), ALU.mult))

                def choose(rk, selx, w, n_):
                    link(dve.tensor_tensor(rk[:, 0], rk[:, 0], rk[:, 1], ALU.subtract))
                    link(dve.tensor_tensor(rk[:, 0], rk[:, 0], rank_i[:, 0:n_].unsqueeze(1).to_broadcast([TP, w, n_]), ALU.add))
                    link(dve.tensor_scalar(selx[:], rk[:, 0], 2.0, None, ALU.is_lt))

                if i == 0:
                    link(dve.tensor_reduce(gmx[:], gl[:], AX_X, ALU.max))
                    link(dve.tensor_reduce(emx[:], el[:], AX_X, ALU.max))
                    link(dve.tensor_tensor(gs[:], gl[:], gmx[:].unsqueeze(2).to_broadcast([TP, WP, GROUPS]), ALU.subtract))
                    link(dve.tensor_tensor(es[:], el[:], emx[:].unsqueeze(2).to_broadcast([TP, WG, PER]), ALU.subtract))
                if i == 1:
                    compare(gl, gcmp[:], WP, GROUPS)
                    ahead(gcmp[:], upper4, WP, GROUPS)
                    dve.tensor_reduce(grk[:, 0], gcmp[:], AX_X, ALU.add)
                    link(dve.tensor_reduce(grk[:, 1], gcmp[:].rearrange("p w i j -> p w j i"), AX_X, ALU.add))
                    choose(grk, gsel, WP, GROUPS)
                if i == 2:
                    compare(el, ecmp, WG, PER)
                if i == 3:
                    ahead(ecmp, upper, WG, PER)
                if i == 4:
                    dve.tensor_reduce(erk[:, 0], ecmp, AX_X, ALU.add)
                if i == 5:
                    link(dve.tensor_reduce(erk[:, 1], ecmp.rearrange("p w i j -> p w j i"), AX_X, ALU.add))
                if i == 6:
                    choose(erk, esel, WG, PER)
                    dve.wait_ge(s["route_act"], q + 1)
                    dve.tensor_tensor(gp[:], gp[:], gsel[:], ALU.mult)
                    link(dve.tensor_tensor(ep[:], ep[:], esel[:], ALU.mult))
                    dve.tensor_reduce(gz[:], gp[:], AX_X, ALU.add)
                    link(dve.tensor_reduce(ez[:], ep[:], AX_X, ALU.add))
                    dve.reciprocal(gz[:], gz[:])
                    link(dve.reciprocal(ez[:], ez[:]))
                if i == 7:
                    link(dve.tensor_tensor(fac[:], gp[:], gz[:].unsqueeze(2).to_broadcast([TP, WP, GROUPS]), ALU.mult))
                    fac24 = fac[:].rearrange("p w g -> p (w g)")
                    link(dve.tensor_tensor(fac24, fac24, ez[:], ALU.mult))
                    chosen = maskf[:, bass.ds(q * WP, WP), :]
                    dve.tensor_tensor(row[:, :, D:ROWW].rearrange("p w (g e) -> p w g e", g=GROUPS), ep[:].rearrange("p (w g) e -> p w g e", g=GROUPS),
                                      fac[:].unsqueeze(3).to_broadcast([TP, WP, GROUPS, PER]), ALU.mult)
                    dve.tensor_tensor(chosen.rearrange("p w (g e) -> p (w g) e", g=GROUPS), esel[:],
                                      gsel[:].rearrange("p w g -> p (w g)").unsqueeze(2).to_broadcast([TP, WG, PER]), ALU.mult)
                    link(dve.tensor_tensor(mask[:, 0:WP, :].rearrange("p w (g e) -> p (w g) e", g=GROUPS), esel[:],
                                           gsel[:].rearrange("p w g -> p (w g)").unsqueeze(2).to_broadcast([TP, WG, PER]), ALU.mult))
                if i == 8:
                    dve.wait_ge(s["cnt_pe"], q + 1)
                    link(dve.tensor_tensor(rank[:, bass.ds(q * WP, WP), :], ps[0:TP, MID + 1, 0:WP * NE].rearrange("p (w e) -> p w e", w=WP),
                                           carry[0:TP].unsqueeze(1).to_broadcast([TP, WP, NE]), ALU.add))
                    link(dve.tensor_tensor(carry[:], carry[:], ps[:, MID + 1, WP * NE:(WP + 1) * NE], ALU.add))
                dve.sem_inc(s["passed"], 1)
                if i + 1 in steps:
                    assert m[0] == steps[i + 1], (i, m)

            for i in range(U):
                front(0, i)
            behind(0)
            skip(0)
            with dve.Fori(0, last_q) as q:
                units(q, True)
                back(q, True)
            units(last_q, False)
            back(last_q, False)
            for i in range(9):
                routing(last_q, i)
            for part in range(2):
                bias(last_q, part)

        early.close()
        def lb(name, shape, dt=F32):
            return ctx.enter_context(nc.sbuf_tensor(name, shape, dt))

        NG = Q * WP
        cnt_i = lb("cnt_i", [128, NE], I32)
        nblk_i = lb("nblk_i", [128, NE], I32)
        nblk = lb("nblk", [128, NE])
        endb = lb("endb", [128, NE])
        first = lb("first", [128, NE])
        key = lb("key", [TP, NG, NE])
        top = lb("top", [TP, NG, 8])
        slot_i = lb("slot_i", [TP, NG, TOPK], I32)
        at_i = lb("at_i", [TP, 2, NG * TOPK], I32)
        at_f = lb("at_f", [TP, 2, NG * TOPK])
        is_row = lb("is_row", [TP, 8, BLK], F32R)
        is_blk = lb("is_blk", [TP, 2, TOPK, NBLK], F32R)
        passed_e = lb("passed_e", [128, NE])
        e_col = lb("e_col", [128, 1])
        e_tab = lb("e_tab", [1, 128], I32)
        ring_tab = lb("ring_tab", [1, 128], I32)
        end_tab = lb("end_tab", [1, NE], I32)
        groups_tab = lb("groups_tab", [1, 1], I32)
        empty = lb("empty", [128, NBLK])
        ix = lb("ix", [128, NBLK + SETR], I32)
        ixg = lb("ixg", [128, SETR], I32)
        ixs = lb("ixs", [128, SETR], I32)
        xg = lb("xg", [128, SETR, ROWW])
        xa = lb("xa", [128, 2, BLK])
        xb = lb("xb", [65, 2, BLK])
        w1a = lb("w1a", [128, WRING, M])
        w1b = lb("w1b", [65, WRING, M])
        w2 = lb("w2", [128, WRING, MC, D])
        ht = lb("ht", [128, 2, M])
        ys = lb("ys", [128, 2, D])
        for n_ in ("tab", "row_set", "blk_set", "oh_used", "e_t", "ready", "gathered0", "gathered1", "gathered2", "gathered3", "col",
                   "added", "x_t", "x_e", "h_pe", "h_act", "y_pe", "y_dve",
                   "w_in0", "w_in1", "w_in2", "w_in3", "w_ready", "out_done", "b1_one"):
            s[n_] = sem("p2_" + n_)
        gathered = [s[f"gathered{j}"] for j in range(SETR)]
        w_in_ = [s[f"w_in{j}"] for j in range(WRING)]
        MH = M // 2
        block2 = ctx.enter_context(nc.Block())

        def used(eng):
            return eng.value_load(groups_tab[0:1, 0:1], min_val=NE // SETR - 1, max_val=NBLK // SETR - 1)

        @block2.sync
        def _(sp):
            def load_expert(e, j):
                one = (lambda ap: ap[e]) if isinstance(e, int) else (lambda ap: ap[bass.ds(e, 1)][0])
                w1, w2_, b1 = one(t["L0_ffn_W1"]), one(t["L0_ffn_W2"]), one(t["L0_ffn_b1"])
                sp.dma_start(w1a[:, j, :], w1[0:128, :]).then_inc(w_in_[j], 16)
                sp.dma_start(w1b[0:64, j, :], w1[128:D, :]).then_inc(w_in_[j], 16)
                sp.dma_start(w1b[64:65, j, :], b1.rearrange("(a m) -> a m", a=1)).then_inc(w_in_[j], 16)
                sp.dma_start(w2[:, j, :, :], w2_.rearrange("(c p) d -> p c d", p=128)).then_inc(w_in_[j], 16)

            for e in range(WRING):
                load_expert(e, e)
                if e >= 1:
                    sp.wait_ge(w_in_[e - 1], 64)
                    sp.sem_inc(s["w_ready"], 1)
            sp.wait_ge(s["ready"], 1)
            with sp.Fori(1, NE // WRING) as r:
                for j in range(WRING):
                    end = sp.value_load(end_tab[0:1, bass.ds((r - 1) * WRING + j, 1)], min_val=1, max_val=NBLK)
                    sp.wait_ge(s["y_pe"], end)
                    load_expert(r * WRING + j, j)
                    sp.wait_ge(w_in_[(j - 1) % WRING], 64 * r if j == 0 else 64 * (r + 1))
                    sp.sem_inc(s["w_ready"], 1)
            sp.wait_ge(w_in_[WRING - 1], 64 * (NE // WRING))
            sp.sem_inc(s["w_ready"], 1)
            sp.wait_ge(s["added"], used(sp) * (SETR * 16) + SETR * 16)
            sp.sem_inc(s["passed"], 1)
            sp.dma_start(out.rearrange("b s d -> (b s) d"), acc_dram[0:TOK, :]).then_inc(s["out_done"], 16)
            sp.wait_ge(s["out_done"], 16)

        @block2.gpsimd
        def _(pool):
            def column(ring, t_, j):
                pool.tensor_copy(ring[:, j:j + 1], ix[:, bass.ds(t_, 1)]).then_inc(s["col"], 1)

            def gather(t_, j, cols):
                column(ixg, t_, j)
                pool.wait_ge(s["col"], cols)
                pool.sem_inc(s["passed"], 1)
                pool.indirect_dma_start(xg[:, j, :], None, rows_dram, bass.IndirectOffsetOnAxis(ixg[:, j:j + 1], 0))\
                    .then_inc(gathered[j], 16)

            pool.wait_ge(s["ready"], 1)
            for j in range(SETR):
                gather(j, j, j + 1)
            groups = used(pool)
            with pool.Fori(0, NBLK // SETR) as r, pool.If(r <= groups):
                for j in range(SETR):
                    if j > 0:
                        pool.wait_ge(s["added"], (r * SETR + j) * 16)
                    column(ixs, r * SETR + j, j)
                    pool.wait_ge(s["col"], (r * SETR + j) * 2 + SETR + 1)
                    pool.wait_ge(s["y_dve"], r * SETR + j + 1)
                    pool.sem_inc(s["passed"], 1)
                    pool.indirect_dma_start(acc_dram, bass.IndirectOffsetOnAxis(ixs[:, j:j + 1], 0), ys[:, j % 2, :], None,
                                            compute_op=ALU.add).then_inc(s["added"], 16)
                    gather(r * SETR + j + SETR, j, (r * SETR + j + 1) * 2 + SETR)
                pool.wait_ge(s["added"], (r + 1) * SETR * 16)
                pool.sem_inc(s["passed"], 1)
            for j in range(SETR):
                pool.wait_ge(gathered[j], groups * 16 + 32)

        def in_steps(eng, step):
            groups = used(eng)
            for i in range(SETR):
                step(i, i)
            with eng.Fori(0, NBLK // SETR - 1) as r:
                with eng.If(r < groups):
                    for j in range(SETR):
                        step(r * SETR + j + SETR, j)
            step(groups * SETR + SETR, 0, True)

        @block2.scalar
        def _(act):
            act.wait_ge(s["b1_one"], 1)
            act.wait_ge(s["ready"], 1)

            def x_out(t_, j):
                act.wait_ge(s["x_t"], t_ + 1)
                if not (isinstance(t_, int) and t_ < 2):
                    act.wait_ge(s["h_pe"], t_ - 1)
                act.activation(xa[:, j, :], ps[:, 5 * j, 0:BLK], ACT.Copy)
                act.activation(xb[0:64, j, :], ps[0:64, 5 * j, BLK:2 * BLK], ACT.Copy).then_inc(s["x_e"], 1)

            def step(t_, j, last=False):
                fixed = isinstance(t_, int)
                if fixed and t_ == 0:
                    x_out(0, 0)
                if not last:
                    act.wait_ge(s["h_pe"], t_ + 1)
                    if not fixed or t_ >= 2:
                        act.wait_ge(s["y_pe"], t_ - 1)
                    b = 1 + 2 * (j % 2)
                    act.activation(ht[:, j % 2, :].rearrange("p (b m) -> p b m", b=2), ps[:, b:b + 2, 0:MH], ACT.Gelu)\
                        .then_inc(s["h_act"], 1)
                    x_out(t_ + 1, (j + 1) % 2)

            in_steps(act, step)

        @block2.tensor
        def _(pe):
            pe.wait_ge(s["e_t"], 1)
            pe.transpose(ps[0:1, 1, 0:128], e_col[:], ident[:]).then_inc(s["e_t"], 1)
            for g in range(NG):
                for k in range(TOPK):
                    i = g * TOPK + k
                    if k == 0:
                        pe.wait_ge(s["blk_set"], g + 1)
                    pe.wait_ge(s["row_set"], i + 1)
                    pe.matmul(ps[:, 0, 0:NBLK], is_row[:, i % 8, :], is_blk[:, g % 2, k, :], start=(i == 0), stop=(i == NG * TOPK - 1))\
                        .then_inc(s["oh_used"], 1)
            pe.wait_ge(s["ready"], 1)

            def turn_x(t_, j):
                if isinstance(t_, int):
                    pe.wait_ge(gathered[j], (t_ // SETR + 1) * 16)
                else:
                    pe.wait_ge(gathered[j], (t_ - j) * (16 // SETR) + 16)
                if not isinstance(t_, int) or t_ >= 2:
                    pe.wait_ge(s["x_e"], t_ - 1)
                pe.sem_inc(s["passed"], 1)
                pe.transpose(ps[:, 5 * (j % 2), 0:BLK], xg[:, j, 0:128], ident[:])
                pe.transpose(ps[0:64, 5 * (j % 2), BLK:2 * BLK], xg[:, j, 128:D], ident[:]).then_inc(s["x_t"], 1)

            def hidden(b, x, k):
                for c in range(MC):
                    dst = ps[:, b + c // 3, (c % 3) * BLK:(c % 3 + 1) * BLK]
                    pe.matmul(dst, w1a[:, k, c * 128:(c + 1) * 128], xa[:, x, :], start=True, stop=False)
                    last = pe.matmul(dst, w1b[:, k, c * 128:(c + 1) * 128], xb[:, x, :], start=False, stop=True)
                last.then_inc(s["h_pe"], 1)

            def output(b, x, k):
                for c in range(MC):
                    last = pe.matmul(ps[:, b, 0:D], ht[:, x, c * BLK:(c + 1) * BLK], w2[:, k, c, :],
                                     start=(c == 0), stop=(c == MC - 1))
                last.then_inc(s["y_pe"], 1)

            def at_place(place, layer, b, x):
                with pe.If(place < 2):
                    with pe.If(place < 1):
                        layer(b, x, 0)
                    with pe.Else():
                        layer(b, x, 1)
                with pe.Else():
                    with pe.If(place < 3):
                        layer(b, x, 2)
                    with pe.Else():
                        layer(b, x, 3)

            held = [None]

            def step(t_, j, last=False):
                fixed = isinstance(t_, int)
                if fixed and t_ == 0:
                    turn_x(0, 0)
                if not last:
                    e = pe.value_load(e_tab[0:1, bass.ds(t_, 1)], min_val=0, max_val=NE - 1)
                    place = e & (WRING - 1)
                    before, held[0] = held[0], (place, j)
                    pe.wait_ge(s["w_ready"], e + 1)
                    pe.wait_ge(s["x_e"], t_ + 1)
                    if not fixed or t_ >= 2:
                        pe.wait_ge(s["h_act"], t_ - 1)
                    pe.sem_inc(s["passed"], 1)
                    at_place(place, hidden, 1 + 2 * (j % 2), j % 2)
                    turn_x(t_ + 1, (j + 1) % SETR)
                if not fixed or t_ >= 1:
                    if fixed or last or j == 0:
                        place = pe.value_load(ring_tab[0:1, bass.ds(t_ - 1, 1)], min_val=0, max_val=WRING - 1)
                    else:
                        place = before[0]
                    pe.wait_ge(s["h_act"], t_)
                    if not fixed or t_ >= 3:
                        pe.wait_ge(s["y_dve"], t_ - 2)
                    pe.sem_inc(s["passed"], 1)
                    at_place(place, output, 6 + (j - 1) % 2, (j - 1) % 2)

            in_steps(pe, step)

        @block2.vector
        def _(dve):
            n = [0]

            def link(ins):
                n[0] += 1
                ins.then_inc(s["tab"], 1)
                dve.wait_ge(s["tab"], n[0])

            dve.memset(xb[64:65, :, :], 1.0).then_inc(s["b1_one"], 1)
            link(dve.tensor_scalar(cnt_i[:], carry[:], float(BLK - 1), None, ALU.add))
            link(dve.tensor_scalar(nblk_i[:], cnt_i[:], 7, None, ALU.arith_shift_right))
            link(dve.tensor_copy(nblk[:], nblk_i[:]))
            link(dve.tensor_scalar(nblk[:], nblk[:], 1.0, None, ALU.max))
            link(dve.tensor_tensor_scan(endb[:], nblk[:], zero[:, 0:NE], 0.0, ALU.add, ALU.add))
            link(dve.tensor_tensor(first[:], endb[:], nblk[:], ALU.subtract))
            link(dve.tensor_scalar(first[:], first[:], float(BLK), 1.0, ALU.mult, ALU.add))
            link(dve.tensor_scalar(passed_e[:], endb[:], iota_p[:, 0:1], None, ALU.is_le))
            link(dve.tensor_reduce(e_col[:], passed_e[:], AX_X, ALU.add))
            dve.tensor_scalar(e_col[:], e_col[:], float(NE - 1), None, ALU.min).then_inc(s["e_t"], 1)
            dve.tensor_copy(end_tab[:], endb[0:1, :])
            link(dve.tensor_scalar(groups_tab[:], endb[0:1, NE - 1:NE], -1.0, None, ALU.add))
            link(dve.tensor_scalar(groups_tab[:], groups_tab[:], 2, None, ALU.arith_shift_right))
            link(dve.tensor_tensor(key[:], rank[:], first[0:TP].unsqueeze(1).to_broadcast([TP, NG, NE]), ALU.add))
            link(dve.tensor_tensor(key[:], key[:], maskf[:], ALU.mult))
            for g in range(NG):
                last = dve.max(top[:, g, :], key[:, g, :])
            link(last)
            link(dve.tensor_scalar(slot_i[:], top[:, :, 0:TOPK], -1.0, None, ALU.add))
            flat = slot_i[:].rearrange("p g k -> p (g k)")
            dve.tensor_scalar(at_i[:, 0, :], flat, BLK - 1, None, ALU.bitwise_and)
            link(dve.tensor_scalar(at_i[:, 1, :], flat, 7, None, ALU.arith_shift_right))
            link(dve.tensor_copy(at_f[:], at_i[:]))
            dve.wait_ge(s["e_t"], 2)
            link(dve.tensor_copy(e_tab[:], ps[0:1, 1, 0:128]))
            dve.tensor_scalar(ring_tab[:], e_tab[:], WRING - 1, None, ALU.bitwise_and)
            for g in range(NG):
                if g >= 2:
                    dve.wait_ge(s["oh_used"], (g - 1) * TOPK)
                one = [TP, TOPK, NBLK]
                dve.tensor_tensor(is_blk[:, g % 2], iota[0:TP, 0:NBLK].unsqueeze(1).to_broadcast(one),
                                  at_f[:, 1, g * TOPK:(g + 1) * TOPK].unsqueeze(2).to_broadcast(one), ALU.is_equal).then_inc(s["blk_set"], 1)
                for k in range(TOPK):
                    i = g * TOPK + k
                    if i >= 8:
                        dve.wait_ge(s["oh_used"], i - 7)
                    dve.tensor_scalar(is_row[:, i % 8, :], iota[0:TP, :], at_f[:, 0, i:i + 1], tok_id[:, g:g + 1],
                                      ALU.is_equal, ALU.mult).then_inc(s["row_set"], 1)
            dve.wait_ge(s["oh_used"], NG * TOPK)
            link(dve.tensor_scalar(empty[:], ps[:, 0, 0:NBLK], 0.0, pad_id[:, 0:1], ALU.is_equal, ALU.mult))
            dve.tensor_scalar(ix[:, NBLK:], zero[:, 0:SETR], 0.0, pad_id[:, 0:1], ALU.mult, ALU.add)
            link(dve.scalar_tensor_tensor(out=empty[:], in0=ps[:, 0, 0:NBLK], scalar=-1.0, in1=empty[:], op0=ALU.add, op1=ALU.add))
            link(dve.tensor_scalar(ix[:, NBLK:], zero[:, 0:SETR], pad_id[:, 0:1], -1.0, ALU.add, ALU.add))
            dve.tensor_copy(ix[:, 0:NBLK], empty[:]).then_inc(s["ready"], 1)

            def step(t_, j, last=False):
                fixed = isinstance(t_, int)
                if not fixed or t_ >= 1:
                    e = dve.value_load(e_tab[0:1, bass.ds(t_ - 1, 1)], min_val=0, max_val=NE - 1)
                    dve.wait_ge(s["y_pe"], t_)
                    if not fixed or t_ >= 3:
                        dve.wait_ge(s["added"], 16 * (t_ - 2))
                    dve.tensor_scalar(ys[:, (j - 1) % 2, :], ps[:, 6 + (j - 1) % 2, 0:D], xg[:, (j - 1) % SETR, bass.ds(e + D, 1)], None, ALU.mult)\
                        .then_inc(s["y_dve"], 1)

            dve.wait_ge(s["ready"], 1)
            in_steps(dve, step)


_INS = ["x", "L0_tok_W", "L0_tok_b", "L0_tok_pos_emb", "L0_attn_A_log", "L0_attn_D_param", "L0_attn_W_bc",
        "L0_attn_W_dt", "L0_attn_W_dtp", "L0_attn_b_dt", "L0_attn_rms_scale", "L0_ffn_Wg", "L0_ffn_bg",
        "L0_ffn_Wge", "L0_ffn_bge", "L0_ffn_W1", "L0_ffn_b1", "L0_ffn_W2", "L0_ffn_b2"]


def kernel(**inputs):
    import numpy as _np
    import concourse.bacc as _bacc
    from concourse import mybir as _mybir
    from concourse.bass_utils import run_bass_kernel_spmd as _run

    nc = _bacc.Bacc("TRN2", target_bir_lowering=False, num_devices=1)
    arrays, t = {}, {}
    for name in _INS:
        a = _np.ascontiguousarray(inputs[name])
        arrays[f"in_{name}"] = a
        t[name] = nc.dram_tensor(f"in_{name}", a.shape, _mybir.dt.from_np(a.dtype), kind="ExternalInput").ap()
    out = nc.dram_tensor("out_0", (BATCH, SEQ, D), F32, kind="ExternalOutput").ap()
    tower(nc, t, out)
    r = _run(nc, [arrays], core_ids=[0])
    return r.results[0]["out_0"]
```
